# Optimizing a Trainium2 kernel written in Bass

```python
import numpy as np
import jax
import jax.numpy as jnp

def _softmax(x, axis=-1):
    return jax.nn.softmax(x, axis=axis)

def _gelu(x):
    return jax.nn.gelu(x, approximate=True)

def _silu(x):
    return jax.nn.silu(x)

def _sigmoid(x):
    return jax.nn.sigmoid(x)

def _layernorm(x, axis=-1, eps=1e-05):
    m = jnp.mean(x, axis=axis, keepdims=True)
    v = jnp.var(x, axis=axis, keepdims=True)
    return (x - m) / jnp.sqrt(v + eps)

def _scatter_add(tgt, idx, src, axis=0):
    return tgt.at[idx].add(src)

def _segment_sum(src, seg, n):
    return jax.ops.segment_sum(src, seg, n)
kernel_name = 'mk_hybrid_d1_jaxref_r8_1bcb6a'

def setup_inputs(seed: int=0):
    np.random.seed(seed)
    _w = jnp.asarray

    def _L0_attn_a_setup():
        import jax, jax.numpy as jnp
        import numpy as np
        import math
        B, T, D = (4, 512, 256)
        H = 16
        HD = D // H
        L = 64
        K_TOP = 4
        key = jax.random.key(seed)
        ks = jax.random.split(key, 10)
        lim = 1.0 / math.sqrt(D)
        u = lambda k, shape: jax.random.uniform(k, shape, jnp.float32, -lim, lim)
        return {'hidden_states': jax.random.normal(ks[0], (B, T, D), jnp.float32), 'Wq': u(ks[1], (D, D)), 'bq': u(ks[2], (D,)), 'Wk': u(ks[3], (D, D)), 'bk': u(ks[4], (D,)), 'Wv': u(ks[5], (D, D)), 'bv': u(ks[6], (D,)), 'Wo': u(ks[7], (D, D)), 'bo': u(ks[8], (D,)), 'latent_keys': jax.random.normal(ks[9], (L, D), jnp.float32) * 0.1}
    _L0_attn_a_in = _L0_attn_a_setup()

    def _L0_attn_b_setup():
        import jax, jax.numpy as jnp
        import numpy as np
        HIDDEN = 256
        N_HEADS = 32
        HEAD_DIM = HIDDEN // N_HEADS
        SEQ = 256
        BATCH = 1
        CHUNK = 32
        TOPK = 4
        THETA = 10000.0
        EPS = 1e-06
        NEG = jnp.float32(-1e+30)

        def _rope(t):
            D = t.shape[-1]
            pos = jnp.arange(t.shape[1], dtype=jnp.float32)
            inv_freq = 1.0 / THETA ** (jnp.arange(0, D, 2, dtype=jnp.float32) / D)
            freqs = pos[:, None] * inv_freq[None, :]
            cos = jnp.cos(freqs)[None, :, None, :]
            sin = jnp.sin(freqs)[None, :, None, :]
            t1, t2 = (t[..., :D // 2], t[..., D // 2:])
            return jnp.concatenate([t1 * cos - t2 * sin, t1 * sin + t2 * cos], axis=-1)
        key = jax.random.key(seed)
        ks = jax.random.split(key, 8)
        s = 0.02
        return {'hidden_states': jax.random.normal(ks[0], (BATCH, SEQ, HIDDEN), jnp.float32), 'Wq': jax.random.normal(ks[1], (HIDDEN, HIDDEN), jnp.float32) * s, 'Wk': jax.random.normal(ks[2], (HIDDEN, HIDDEN), jnp.float32) * s, 'Wv': jax.random.normal(ks[3], (HIDDEN, HIDDEN), jnp.float32) * s, 'Wo': jax.random.normal(ks[4], (HIDDEN, HIDDEN), jnp.float32) * s, 'Wg1': jax.random.normal(ks[5], (HEAD_DIM, HIDDEN), jnp.float32) * s, 'Wg2': jax.random.normal(ks[6], (HIDDEN, HEAD_DIM), jnp.float32) * s, 'o_norm_weight': jnp.ones((HEAD_DIM,), jnp.float32)}
    _L0_attn_b_in = _L0_attn_b_setup()

    def _L0_ffn_setup():
        import jax, jax.numpy as jnp
        import numpy as np
        K_TOP = 2
        key = jax.random.key(seed)
        ks = jax.random.split(key, 6)
        s = 0.02
        B, S, H, D = (4, 128, 256, 128)
        E_SH, E_RT = (2, 16)
        return {'x': jax.random.normal(ks[0], (B, S, H), dtype=jnp.float32), 'Wsh_up': jax.random.normal(ks[1], (E_SH, H, D), dtype=jnp.float32) * s, 'Wsh_down': jax.random.normal(ks[2], (E_SH, D, H), dtype=jnp.float32) * s, 'Wrt_up': jax.random.normal(ks[3], (E_RT, H, D), dtype=jnp.float32) * s, 'Wrt_down': jax.random.normal(ks[4], (E_RT, D, H), dtype=jnp.float32) * s, 'W_router': jax.random.normal(ks[5], (H, E_RT), dtype=jnp.float32) * s}
    _L0_ffn_in = _L0_ffn_setup()
    _d = {'L0_attn_a_hidden_states': _L0_attn_a_in['hidden_states'], 'L0_attn_a_Wq': _L0_attn_a_in['Wq'], 'L0_attn_a_bq': _L0_attn_a_in['bq'], 'L0_attn_a_Wk': _L0_attn_a_in['Wk'], 'L0_attn_a_bk': _L0_attn_a_in['bk'], 'L0_attn_a_Wv': _L0_attn_a_in['Wv'], 'L0_attn_a_bv': _L0_attn_a_in['bv'], 'L0_attn_a_Wo': _L0_attn_a_in['Wo'], 'L0_attn_a_bo': _L0_attn_a_in['bo'], 'L0_attn_a_latent_keys': _L0_attn_a_in['latent_keys'], 'L0_attn_b_Wq': _L0_attn_b_in['Wq'], 'L0_attn_b_Wk': _L0_attn_b_in['Wk'], 'L0_attn_b_Wv': _L0_attn_b_in['Wv'], 'L0_attn_b_Wo': _L0_attn_b_in['Wo'], 'L0_attn_b_Wg1': _L0_attn_b_in['Wg1'], 'L0_attn_b_Wg2': _L0_attn_b_in['Wg2'], 'L0_attn_b_o_norm_weight': _L0_attn_b_in['o_norm_weight'], 'L0_ffn_Wsh_up': _L0_ffn_in['Wsh_up'], 'L0_ffn_Wsh_down': _L0_ffn_in['Wsh_down'], 'L0_ffn_Wrt_up': _L0_ffn_in['Wrt_up'], 'L0_ffn_Wrt_down': _L0_ffn_in['Wrt_down'], 'L0_ffn_W_router': _L0_ffn_in['W_router']}
    _x0 = _d['L0_attn_a_hidden_states']
    _d['L0_attn_a_hidden_states'] = jax.random.normal(jax.random.fold_in(jax.random.key(seed), 1), (4, 512, 256), dtype=_x0.dtype)
    del _x0
    return _d

def reference(L0_attn_a_hidden_states, L0_attn_a_Wq, L0_attn_a_bq, L0_attn_a_Wk, L0_attn_a_bk, L0_attn_a_Wv, L0_attn_a_bv, L0_attn_a_Wo, L0_attn_a_bo, L0_attn_a_latent_keys, L0_attn_b_Wq, L0_attn_b_Wk, L0_attn_b_Wv, L0_attn_b_Wo, L0_attn_b_Wg1, L0_attn_b_Wg2, L0_attn_b_o_norm_weight, L0_ffn_Wsh_up, L0_ffn_Wsh_down, L0_ffn_Wrt_up, L0_ffn_Wrt_down, L0_ffn_W_router):

    def _L0_attn_a_ref(hidden_states, Wq, bq, Wk, bk, Wv, bv, Wo, bo, latent_keys):
        import jax, jax.numpy as jnp
        import numpy as np
        import math
        B, T, D = (4, 512, 256)
        H = 16
        HD = D // H
        L = 64
        K_TOP = 4
        b, t, d = hidden_states.shape
        Q = (hidden_states @ Wq.T + bq).reshape(b, t, H, HD).transpose(0, 2, 1, 3)
        K = (hidden_states @ Wk.T + bk).reshape(b, t, H, HD).transpose(0, 2, 1, 3)
        V = (hidden_states @ Wv.T + bv).reshape(b, t, H, HD).transpose(0, 2, 1, 3)
        latent = latent_keys.reshape(L, H, HD)
        attn_logits = jnp.einsum('bhtd,lhd->bhtl', Q, latent) / math.sqrt(HD)
        topk_logits, topk_idx = jax.lax.top_k(attn_logits, K_TOP)
        attn_weights = jax.nn.softmax(topk_logits, axis=-1)
        latent_h = latent.transpose(1, 0, 2)
        selected = latent_h[jnp.arange(H)[None, :, None, None], topk_idx]
        weighted = jnp.einsum('bhtk,bhtkd->bhtd', attn_weights, selected)
        attn_output = (weighted + V).transpose(0, 2, 1, 3).reshape(b, t, d)
        return attn_output @ Wo.T + bo

    def _L0_attn_b_ref(hidden_states, Wq, Wk, Wv, Wo, Wg1, Wg2, o_norm_weight):
        import jax, jax.numpy as jnp
        import numpy as np
        HIDDEN = 256
        N_HEADS = 32
        HEAD_DIM = HIDDEN // N_HEADS
        SEQ = 256
        BATCH = 1
        CHUNK = 32
        TOPK = 4
        THETA = 10000.0
        EPS = 1e-06
        NEG = jnp.float32(-1e+30)

        def _rope(t):
            D = t.shape[-1]
            pos = jnp.arange(t.shape[1], dtype=jnp.float32)
            inv_freq = 1.0 / THETA ** (jnp.arange(0, D, 2, dtype=jnp.float32) / D)
            freqs = pos[:, None] * inv_freq[None, :]
            cos = jnp.cos(freqs)[None, :, None, :]
            sin = jnp.sin(freqs)[None, :, None, :]
            t1, t2 = (t[..., :D // 2], t[..., D // 2:])
            return jnp.concatenate([t1 * cos - t2 * sin, t1 * sin + t2 * cos], axis=-1)
        B, S, _ = hidden_states.shape
        H, D, C = (N_HEADS, HEAD_DIM, CHUNK)
        NC = S // C
        q = (hidden_states @ Wq.T).reshape(B, S, H, D)
        k = (hidden_states @ Wk.T).reshape(B, S, H, D)
        v = (hidden_states @ Wv.T).reshape(B, S, H, D)
        q, k = (_rope(q), _rope(k))
        kmean = k.reshape(B, NC, C, H, D).mean(axis=2)
        gate = jnp.einsum('bshd,bnhd->bhsn', q, kmean)
        pos = jnp.arange(S)
        q_chunk = pos // C
        chunk_ids = jnp.arange(NC)
        future = chunk_ids[None, :] > q_chunk[:, None]
        self_blk = chunk_ids[None, :] == q_chunk[:, None]
        gate = jnp.where(future[None, None], NEG, gate)
        gate = jnp.where(self_blk[None, None], -NEG, gate)
        _, topk_idx = jax.lax.top_k(gate, TOPK)
        sel = jax.nn.one_hot(topk_idx, NC, dtype=jnp.bool_).any(axis=-2)
        allowed = jnp.take(sel, q_chunk, axis=-1)
        causal = pos[None, :] <= pos[:, None]
        allowed = allowed & causal[None, None]
        scale = 1.0 / np.sqrt(D)
        scores = jnp.einsum('bshd,bthd->bhst', q, k) * scale
        scores = jnp.where(allowed, scores, NEG)
        p = jax.nn.softmax(scores, axis=-1)
        o = jnp.einsum('bhst,bthd->bshd', p, v)
        g = (hidden_states @ Wg1.T @ Wg2.T).reshape(B, S, H, D)
        rms = jax.lax.rsqrt(jnp.mean(o * o, axis=-1, keepdims=True) + EPS)
        o = o * rms * o_norm_weight * jax.nn.sigmoid(g)
        return o.reshape(B, S, H * D) @ Wo.T

    def _L0_ffn_ref(x, Wsh_up, Wsh_down, Wrt_up, Wrt_down, W_router):
        import jax, jax.numpy as jnp
        import numpy as np
        K_TOP = 2
        B, S, H = x.shape
        E_rt = Wrt_up.shape[0]
        xt = x.reshape(B * S, H)
        sh_mid = jax.nn.gelu(jnp.einsum('th,ehd->ted', xt, Wsh_up), approximate=False)
        shared_out = jnp.einsum('ted,edh->th', sh_mid, Wsh_down)
        probs = jax.nn.softmax(xt @ W_router, axis=-1)
        top_v, top_i = jax.lax.top_k(probs, K_TOP)
        gate = jnp.sum(jax.nn.one_hot(top_i, E_rt, dtype=xt.dtype) * top_v[..., None], axis=1)
        rt_mid = jax.nn.gelu(jnp.einsum('th,ehd->ted', xt, Wrt_up), approximate=False)
        routed_out = jnp.einsum('ted,edh->th', rt_mid * gate[:, :, None], Wrt_down)
        return (shared_out + routed_out).reshape(B, S, H)
    x = L0_attn_a_hidden_states
    x = x + _L0_attn_a_ref(_layernorm(x, axis=-1), L0_attn_a_Wq, L0_attn_a_bq, L0_attn_a_Wk, L0_attn_a_bk, L0_attn_a_Wv, L0_attn_a_bv, L0_attn_a_Wo, L0_attn_a_bo, L0_attn_a_latent_keys)
    x = x + _L0_ffn_ref(_layernorm(x, axis=-1), L0_ffn_Wsh_up, L0_ffn_Wsh_down, L0_ffn_Wrt_up, L0_ffn_Wrt_down, L0_ffn_W_router)
    x = x + _L0_attn_b_ref(_layernorm(x, axis=-1), L0_attn_b_Wq, L0_attn_b_Wk, L0_attn_b_Wv, L0_attn_b_Wo, L0_attn_b_Wg1, L0_attn_b_Wg2, L0_attn_b_o_norm_weight)
    x = x + _L0_ffn_ref(_layernorm(x, axis=-1), L0_ffn_Wsh_up, L0_ffn_Wsh_down, L0_ffn_Wrt_up, L0_ffn_Wrt_down, L0_ffn_W_router)
    return x

_drawn_inputs = setup_inputs


def setup_inputs(seed=0):
    import zlib

    import numpy as np

    out = dict(_drawn_inputs(seed))
    spreads = {'L0_attn_b_o_norm_weight': (1.0, 0.6)}
    factors = {'L0_attn_a_bq': 4.036,
     'L0_attn_b_Wg1': 8.0,
     'L0_attn_b_Wg2': 8.0,
     'L0_ffn_Wrt_up': 4.423,
     'L0_ffn_Wrt_down': 4.272,
     'L0_ffn_W_router': 4.495}
    for name, (base, spread) in spreads.items():
        noise = np.random.default_rng([zlib.crc32(name.encode()), seed]).standard_normal(out[name].shape)
        drawn = base * np.exp(spread * noise) if base else spread * noise
        out[name] = jnp.asarray(drawn.astype(out[name].dtype))
    for name, factor in factors.items():
        out[name] = (out[name] * factor).astype(out[name].dtype)
    return out
```

```python
from contextlib import ExitStack

import numpy as np

import concourse.bass as bass
from concourse import mybir

ALU = mybir.AluOpType
ACT = mybir.ActivationFunctionType
AX_X = mybir.AxisListType.X
F32 = mybir.dt.float32
F32R = mybir.dt.float32r
BF16 = mybir.dt.bfloat16

P = 128
B, T, D = 4, 512, 256
NT = T // P
DC = D // P
LN_EPS = 1e-5

HA, HDA = 16, 16
L = 64
TOP_A = 4
HPC = P // HDA
NPAIR_A = HA // 2
SCALE_A = 1.0 / float(np.sqrt(HDA))

HB, HDB = 32, 8
CH = 32
NCH = T // CH
CPT = P // CH
PAST = 3
THETA = 10000.0
RMS_EPS = 1e-6
SCALE_B = 1.0 / float(np.sqrt(HDB))
NEG = -1e30

E_SH, E_RT = 2, 16
E_ALL = E_SH + E_RT
DF = 128

MARK = 3.0e38
NONE = 3.3e38


class Links:

    def __init__(self, eng, sem):
        self.eng, self.sem, self.n = eng, sem, 0

    def __call__(self, ins):
        self.n += 1
        ins.then_inc(self.sem, 1)
        self.eng.wait_ge(self.sem, self.n)


def program(nc, x_in, Wq_a, bq_a, Wk_a, bk_a, Wv_a, bv_a, Wo_a, bo_a, latent,
            Wq_b, Wk_b, Wv_b, Wo_b, Wg1, Wg2, o_norm, Wsh_up, Wsh_down, Wrt_up, Wrt_down, W_router,
            rope, out):
    with ExitStack() as whole:
        def sb(ctx, name, shape, dt=F32):
            return ctx.enter_context(nc.sbuf_tensor(name, shape, dt))

        def psum(ctx, name, shape, dt=F32):
            return ctx.enter_context(nc.psum_tensor(name, shape, dt))

        def sem(ctx, name):
            return ctx.enter_context(nc.semaphore(name))

        def clear(sems):
            nums = sorted(s.num for s in sems)
            assert nums == list(range(nums[0], nums[0] + len(nums)))
            nc.gpsimd.sem_clear(range(nums[0], nums[-1] + 1))
            nc.all_engine_barrier()

        x = sb(whole, "x", [P, B * NT * D])
        ident = sb(whole, "ident", [P, P])
        ones_row = sb(whole, "ones_row", [1, P])
        minus_half = sb(whole, "minus_half", [P, 1])
        ln_stats = sb(whole, "ln_stats", [P, NT, 6])
        ln_mv = sb(whole, "ln_mv", [P, NT, 2])
        ln_var = sb(whole, "ln_var", [P, NT])
        ln_rstd = sb(whole, "ln_rstd", [P, NT])
        h = sb(whole, "h", [P, NT, D])
        hT = sb(whole, "hT", [P, DC, T])

        s_setup = sem(whole, "s_setup")
        s_setup_dma = sem(whole, "s_setup_dma")

        with nc.Block() as block:
            @block.sync
            def _(sp):
                for b in range(B):
                    sp.dma_start(x[:, b * NT * D:(b + 1) * NT * D].rearrange("p (i d) -> p i d", i=NT),
                                 x_in[b].rearrange("(i p) d -> p i d", p=P)).then_inc(s_setup_dma, 16)
                sp.wait_ge(s_setup_dma, 16 * B)

            @block.gpsimd
            def _(pool):
                pool.memset(ident[:, :], 0.0).then_inc(s_setup, 1)
                pool.memset(ones_row[:, :], 1.0)
                pool.memset(minus_half[:, :], -0.5)
                pool.wait_ge(s_setup, 1)
                pool.affine_select(out=ident[:, :], in_=ident[:, :], compare_op=ALU.not_equal, fill=1.0,
                                   base=0, pattern=[[-1, P]], channel_multiplier=1)

        def x_tile(b, i):
            return x[:, bass.ds(b * (NT * D) + i * D, D)]

        def ln_vector(dve, link, b, s_var, s_rstd, s_h):
            for i in range(NT):
                st = dve.bn_stats(ln_stats[:, i, :], x_tile(b, i))
            link(st)
            for i in range(NT):
                st = dve.bn_aggr(ln_mv[:, i, :], ln_stats[:, i, :])
            link(st)
            dve.tensor_scalar(ln_var[:, :], ln_mv[:, :, 1], LN_EPS, None, ALU.add).then_inc(s_var, 1)
            dve.wait_ge(s_rstd, 1)
            for i in range(NT):
                dve.tensor_scalar(h[:, i, :], x_tile(b, i), ln_mv[:, i, 0:1], ln_rstd[:, i:i + 1],
                                  ALU.subtract, ALU.mult).then_inc(s_h, 1)

        def ln_gpsimd(pool, s_var, s_rstd):
            pool.wait_ge(s_var, 1)
            pool.tensor_tensor(ln_rstd[:, :], ln_var[:, :], minus_half[:, 0:1].broadcast_to([P, NT]), ALU.pow).then_inc(s_rstd, 1)

        def ln_turn(pe, banks, s_h, s_hT):
            for i in range(NT):
                pe.wait_ge(s_h, i + 1)
                for m in range(DC):
                    t = pe.transpose(banks[m][:, i * P:(i + 1) * P], h[:, i, m * P:(m + 1) * P], ident[:, :])
            t.then_inc(s_hT, 1)

        def ln_keep(act, banks, s_hT, s_hTs):
            act.wait_ge(s_hT, 1)
            for m in range(DC):
                act.activation(hT[:, m, :], banks[m][:, :], ACT.Copy).then_inc(s_hTs, 1)

        def latent_attention():
          with ExitStack() as ctx:
            WqT = sb(ctx, "a_WqT", [P, DC, D])
            WvT = sb(ctx, "a_WvT", [P, DC, D])
            WoT = sb(ctx, "a_WoT", [P, DC, D])
            bq = sb(ctx, "a_bq", [P, DC])
            bv = sb(ctx, "a_bv", [P, DC])
            bo = sb(ctx, "a_bo", [1, D])
            latT = sb(ctx, "a_latT", [P, DC, HPC, L])
            latP = sb(ctx, "a_latP", [P, NPAIR_A, 2 * HDA])
            lat2 = sb(ctx, "a_lat2", [P, D])
            QT = sb(ctx, "a_QT", [P, DC, T])
            logits = sb(ctx, "a_logits", [P, NT, HA, L])
            marked = sb(ctx, "a_marked", [P, 2, HA, L])
            shifted = sb(ctx, "a_shifted", [P, 2, HA, L])
            probs = sb(ctx, "a_probs", [P, 2, HA, L])
            probsT = sb(ctx, "a_probsT", [P, NPAIR_A, T])
            top8 = sb(ctx, "a_top8", [P, NT, HA, 8])
            find = sb(ctx, "a_find", [P, 2, HA, 8])
            topd = sb(ctx, "a_topd", [P, NT, HA, TOP_A])
            tope = sb(ctx, "a_tope", [P, NT, HA, TOP_A])
            total = sb(ctx, "a_total", [P, NT, HA])
            inv = sb(ctx, "a_inv", [P, NT, HA])
            AOT = sb(ctx, "a_AOT", [P, DC, T])
            raw = sb(ctx, "a_raw", [P, 3, DC, D])
            bk = [psum(ctx, f"a_bank{i}", [P, 512]) for i in range(8)]
            pT, pQ, pL, pP = bk[0:2], bk[2:4], bk[4:6], bk[6:8]
            d_w = sem(ctx, "a_d_w")
            s_zero, s_wT, s_ws, s_lT, s_ls, s_sel = (sem(ctx, "a_" + n) for n in
                                                     ("zero", "wT", "ws", "lT", "ls", "sel"))

            with nc.Block() as block:
                @block.sync
                def _(sp):
                    for n, w in enumerate((Wq_a, Wv_a, Wo_a)):
                        sp.dma_start(raw[:, n, :, :], w.rearrange("(m p) d -> p m d", p=P)).then_inc(d_w, 16)
                    sp.dma_start(lat2[0:L, :], latent).then_inc(d_w, 16)
                    sp.dma_start(lat2[L:2 * L, :], latent).then_inc(d_w, 16)
                    sp.dma_start(bq[:, :], bq_a.rearrange("(m p) -> p m", p=P), allow_slow_non_contiguous=True).then_inc(d_w, 16)
                    sp.dma_start(bv[:, :], bv_a.rearrange("(m p) -> p m", p=P), allow_slow_non_contiguous=True).then_inc(d_w, 16)
                    sp.dma_start(bo[:, :], bo_a.rearrange("(o d) -> o d", o=1)).then_inc(d_w, 16)
                    sp.wait_ge(d_w, 16 * 8)

                @block.tensor
                def _(pe):
                    pe.wait_ge(d_w, 16 * 8)
                    for n in range(3):
                        for m in range(DC):
                            for c in range(DC):
                                t = pe.transpose(bk[n][:, c * D + m * P:c * D + m * P + P],
                                                 raw[:, n, m, c * P:(c + 1) * P], ident[:, :])
                        t.then_inc(s_wT, 1)
                    for m in range(DC):
                        t = pe.transpose(bk[3][:, m * L:(m + 1) * L], lat2[0:L, m * P:(m + 1) * P],
                                         ident[0:L, 0:L])
                    t.then_inc(s_lT, 1)

                @block.scalar
                def _(act):
                    for n, w in enumerate((WqT, WvT, WoT)):
                        act.wait_ge(s_wT, n + 1)
                        act.activation(w[:, :, :], bk[n][:, :].rearrange("p (c o) -> p c o", c=DC), ACT.Copy)

                @block.vector
                def _(dve):
                    dve.memset(find[:, :, :, :], NONE)
                    dve.memset(latP[:, :, :], 0.0).then_inc(s_zero, 1)
                    dve.wait_ge(s_zero, 1)
                    dve.wait_ge(d_w, 16 * 8)
                    pairs = lat2[:, :].rearrange("p (c a e) -> p c a e", a=2, e=HDA)
                    for a in range(2):
                        dve.tensor_copy(latP[a * L:(a + 1) * L, :, a * HDA:(a + 1) * HDA],
                                        pairs[a * L:(a + 1) * L, :, a, :])
                    dve.wait_ge(s_lT, 1)
                    for m in range(DC):
                        for e in range(HPC):
                            t = dve.tensor_copy(latT[:, m, e, :], bk[3][:, m * L:(m + 1) * L])
                    t.then_inc(s_ls, 1)

                @block.gpsimd
                def _(pool):
                    pool.wait_ge(s_ls, 1)
                    v = latT[:, :, :, :]
                    pool.affine_select(out=v, in_=v, compare_op=ALU.is_ge, fill=0.0, base=0,
                                       pattern=[[0, DC], [-HDA, HPC], [0, L]], channel_multiplier=1).then_inc(s_sel, 1)
                    pool.wait_ge(s_sel, 1)
                    pool.affine_select(out=v, in_=v, compare_op=ALU.is_ge, fill=0.0, base=HDA - 1,
                                       pattern=[[0, DC], [HDA, HPC], [0, L]], channel_multiplier=-1).then_inc(s_sel, 1)

            sems = [sem(ctx, "a_" + n) for n in
                    ("var", "rstd", "h", "hT", "hTs", "q", "qs", "l", "lsb", "mx", "d4", "sh", "ex", "ex4",
                     "w", "inv", "pr", "pT", "pTs", "ao", "aos", "o", "xo", "dve")]
            (s_var, s_rstd, s_h, s_hT, s_hTs, s_q, s_qs, s_l, s_lsb, s_mx, s_d4, s_sh, s_ex, s_ex4,
             s_w, s_inv, s_pr, s_pT, s_pTs, s_ao, s_aos, s_o, s_xo, s_dve) = sems

            with nc.Fori(0, B) as b:
                with nc.Block() as block:
                    @block.tensor
                    def _(pe):
                        ln_turn(pe, pT, s_h, s_hT)
                        pe.wait_ge(s_hTs, DC)
                        for m in range(DC):
                            for c in range(DC):
                                mm = pe.matmul(pQ[m][:, :], WqT[:, c, m * P:(m + 1) * P], hT[:, c, :],
                                               start=(c == 0), stop=(c == DC - 1))
                            mm.then_inc(s_q, 1)
                        pe.wait_ge(s_qs, DC)
                        for i in range(NT):
                            if i:
                                pe.wait_ge(s_lsb, i)
                            for m in range(DC):
                                mm = pe.matmul(pL[m][:, :], QT[:, m, i * P:(i + 1) * P],
                                               latT[:, m, :, :].rearrange("p e l -> p (e l)"), start=True, stop=True)
                            mm.then_inc(s_l, 1)
                        for m in range(DC):
                            for c in range(DC):
                                pe.matmul(pQ[m][:, :], WvT[:, c, m * P:(m + 1) * P], hT[:, c, :],
                                          start=(c == 0), stop=False, skip_group_check=True)
                        for i in range(NT):
                            pe.wait_ge(s_pr, i + 1)
                            if i:
                                pe.wait_ge(s_pTs, i)
                            for c in range(NPAIR_A):
                                t = pe.transpose(pP[c // 4][:, (c % 4) * P:(c % 4 + 1) * P],
                                                 probs[:, i % 2, 2 * c:2 * c + 2, :].rearrange("p e l -> p (e l)"),
                                                 ident[:, :])
                            t.then_inc(s_pT, 1)
                        pe.wait_ge(s_pTs, NT)
                        for m in range(DC):
                            for q in range(4):
                                mm = pe.matmul(pQ[m][32 * q:32 * q + 32, :], latP[:, 4 * m + q, :],
                                               probsT[:, 4 * m + q, :], start=False, stop=True,
                                               skip_group_check=True)
                            mm.then_inc(s_ao, 1)
                        pe.wait_ge(s_aos, DC)
                        for i in range(NT):
                            if i >= 2:
                                pe.wait_ge(s_xo, i - 1)
                            o = pT[i % 2][:, 0:D]
                            pe.matmul(o, ones_row[:, :], bo[:, :], start=True, stop=False)
                            for c in range(DC):
                                mm = pe.matmul(o, AOT[:, c, i * P:(i + 1) * P], WoT[:, c, :],
                                               start=False, stop=(c == DC - 1))
                            mm.then_inc(s_o, 1)

                    @block.scalar
                    def _(act):
                        ln_keep(act, pT, s_hT, s_hTs)
                        for m in range(DC):
                            act.wait_ge(s_q, m + 1)
                            act.activation(QT[:, m, :], pQ[m][:, :], ACT.Identity, bias=bq[:, m:m + 1]).then_inc(s_qs, 1)
                        for i in range(NT):
                            act.wait_ge(s_l, i + 1)
                            for m in range(DC):
                                cp = act.activation(logits[:, i, HPC * m:HPC * (m + 1), :].rearrange("p e l -> p (e l)"),
                                                    pL[m][:, :], ACT.Copy, scale=SCALE_A)
                            cp.then_inc(s_lsb, 1)

                        def turned(i):
                            act.wait_ge(s_pT, i + 1)
                            for c in range(2):
                                cp = act.activation(probsT[:, 4 * c:4 * c + 4, i * P:(i + 1) * P],
                                                    pP[c][:, :].rearrange("p (c t) -> p c t", c=4), ACT.Copy)
                            cp.then_inc(s_pTs, 1)

                        for i in range(NT):
                            act.wait_ge(s_sh, i + 1)
                            act.activation(shifted[:, i % 2], shifted[:, i % 2], ACT.Exp).then_inc(s_ex, 1)
                            act.wait_ge(s_d4, i + 1)
                            act.activation(tope[:, i], topd[:, i], ACT.Exp).then_inc(s_ex4, 1)
                            if i:
                                turned(i - 1)
                        turned(NT - 1)
                        for m in range(DC):
                            act.wait_ge(s_ao, m + 1)
                            act.activation(AOT[:, m, :], pQ[m][:, :], ACT.Identity, bias=bv[:, m:m + 1]).then_inc(s_aos, 1)

                    @block.vector
                    def _(dve):
                        link = Links(dve, s_dve)
                        ln_vector(dve, link, b, s_var, s_rstd, s_h)

                        def weights(i):
                            dve.wait_ge(s_ex, i + 1)
                            if i >= 2:
                                dve.wait_ge(s_pT, i - 1)
                            dve.scalar_tensor_tensor(out=probs[:, i % 2], in0=marked[:, i % 2], scalar=MARK,
                                                     in1=shifted[:, i % 2], op0=ALU.is_equal, op1=ALU.mult).then_inc(s_w, 1)
                            dve.wait_ge(s_ex4, i + 1)
                            link(dve.tensor_reduce(total[:, i], tope[:, i], AX_X, ALU.add))
                            dve.reciprocal(inv[:, i], total[:, i]).then_inc(s_inv, 1)

                        for i in range(NT):
                            dve.wait_ge(s_lsb, i + 1)
                            for e in range(HA):
                                mx = dve.max(top8[:, i, e, :], logits[:, i, e, :])
                            link(mx)
                            dve.tensor_tensor(topd[:, i], top8[:, i, :, 0:TOP_A],
                                              top8[:, i, :, 0:1].broadcast_to([P, HA, TOP_A]), ALU.subtract).then_inc(s_d4, 1)
                            link(dve.tensor_copy(find[:, i % 2, :, 0:TOP_A], top8[:, i, :, 0:TOP_A]))
                            for e in range(HA):
                                mr = dve.match_replace(marked[:, i % 2, e, :], find[:, i % 2, e, :],
                                                       logits[:, i, e, :], MARK)
                            link(mr)
                            if i:
                                weights(i - 1)
                        weights(NT - 1)
                        for i in range(NT):
                            dve.wait_ge(s_o, i + 1)
                            dve.tensor_tensor(x_tile(b, i), pT[i % 2][:, 0:D], x_tile(b, i), ALU.add).then_inc(s_xo, 1)

                    @block.gpsimd
                    def _(pool):
                        ln_gpsimd(pool, s_var, s_rstd)

                        def scaled(i):
                            pool.wait_ge(s_w, i + 1)
                            pool.wait_ge(s_inv, i + 1)
                            pool.tensor_tensor(probs[:, i % 2], probs[:, i % 2],
                                               inv[:, i, :, None].broadcast_to([P, HA, L]), ALU.mult).then_inc(s_pr, 1)

                        for i in range(NT):
                            if i >= 2:
                                pool.wait_ge(s_w, i - 1)
                            pool.wait_ge(s_d4, i + 1)
                            pool.tensor_tensor(shifted[:, i % 2], logits[:, i],
                                               top8[:, i, :, 0:1].broadcast_to([P, HA, L]), ALU.subtract).then_inc(s_sh, 1)
                            if i:
                                scaled(i - 1)
                        scaled(NT - 1)
                clear(sems)

        def experts(n):
          with ExitStack() as ctx:
            w_up = sb(ctx, f"f{n}_w_up", [P, E_ALL, DC, DF])
            w_down = sb(ctx, f"f{n}_w_down", [P, E_ALL, D])
            w_r = sb(ctx, f"f{n}_w_r", [P, DC, E_RT])
            mid = sb(ctx, f"f{n}_mid", [P, 2, T])
            lg = sb(ctx, f"f{n}_lg", [P, NT, E_RT])
            ex = sb(ctx, f"f{n}_ex", [P, NT, E_RT])
            pr = sb(ctx, f"f{n}_pr", [P, NT, E_RT])
            mk = sb(ctx, f"f{n}_mk", [P, NT, E_RT])
            gate = sb(ctx, f"f{n}_gate", [P, NT, E_RT])
            great = sb(ctx, f"f{n}_great", [P, NT])
            total = sb(ctx, f"f{n}_total", [P, NT])
            inv = sb(ctx, f"f{n}_inv", [P, NT])
            top8 = sb(ctx, f"f{n}_top8", [P, NT, 8])
            find = sb(ctx, f"f{n}_find", [P, NT, 8])
            bk = [psum(ctx, f"f{n}_bank{i}", [P, 512]) for i in range(8)]
            pT, pU, pD = bk[0:2], bk[2:4], bk[4:8]
            d_w = sem(ctx, f"f{n}_d_w")
            with nc.Block() as block:
                @block.sync
                def _(sp):
                    sp.dma_start(w_r[:, :, :], W_router.rearrange("(m p) e -> p m e", p=P)).then_inc(d_w, 16)
                    k = 1
                    for lo, count, up, down in ((0, E_SH, Wsh_up, Wsh_down), (E_SH, E_RT, Wrt_up, Wrt_down)):
                        for e in range(count):
                            sp.dma_start(w_up[:, lo + e], up[e].rearrange("(m p) f -> p m f", p=P)).then_inc(d_w, 16)
                            sp.dma_start(w_down[:, lo + e, :], down[e]).then_inc(d_w, 16)
                            k += 2
                    sp.wait_ge(d_w, 16 * k)

                @block.vector
                def _(dve):
                    dve.memset(find[:, :, :], NONE)

            sems = [sem(ctx, f"f{n}_" + s) for s in
                    ("var", "rstd", "h", "hT", "hTs", "r", "sub", "ex", "up", "mid", "dn", "xo", "dve")]
            (s_var, s_rstd, s_h, s_hT, s_hTs, s_r, s_sub, s_ex, s_up, s_mid, s_dn, s_xo, s_dve) = sems

            groups = [list(range(E_SH))] + [[e] for e in range(E_SH, E_ALL)]

            with nc.Fori(0, B) as b:
                with nc.Block() as block:
                    @block.tensor
                    def _(pe):
                        ln_turn(pe, pT, s_h, s_hT)
                        pe.wait_ge(s_hTs, DC)
                        for i in range(NT):
                            for c in range(DC):
                                mm = pe.matmul(pT[0][:, i * E_RT:(i + 1) * E_RT], hT[:, c, i * P:(i + 1) * P],
                                               w_r[:, c, :], start=(c == 0), stop=(c == DC - 1))
                        mm.then_inc(s_r, 1)

                        def up(e):
                            if e >= 2:
                                pe.wait_ge(s_mid, e - 1)
                            for c in range(DC):
                                mm = pe.matmul(pU[e % 2][:, :], w_up[:, e, c, :], hT[:, c, :],
                                               start=(c == 0), stop=(c == DC - 1))
                            mm.then_inc(s_up, 1)

                        up(0)
                        for g, members in enumerate(groups):
                            for e in members:
                                if e + 1 < E_ALL:
                                    up(e + 1)
                            pe.wait_ge(s_mid, members[-1] + 1)
                            if g >= 2:
                                pe.wait_ge(s_xo, NT * (g - 1))
                            for i in range(NT):
                                o = pD[2 * (g % 2) + i // 2][:, (i % 2) * D:(i % 2 + 1) * D]
                                for e in members:
                                    mm = pe.matmul(o, mid[:, e % 2, i * P:(i + 1) * P], w_down[:, e, :],
                                                   start=(e == members[0]), stop=(e == members[-1]))
                            mm.then_inc(s_dn, 1)

                    @block.scalar
                    def _(act):
                        ln_keep(act, pT, s_hT, s_hTs)
                        act.wait_ge(s_sub, 1)
                        act.activation(ex[:, :, :], lg[:, :, :], ACT.Exp).then_inc(s_ex, 1)
                        group_of = [g for g, members in enumerate(groups) for _ in members]
                        for e in range(E_ALL):
                            act.wait_ge(s_up, e + 1)
                            if e >= 2:
                                act.wait_ge(s_dn, group_of[e - 2] + 1)
                            act.activation(mid[:, e % 2, :], pU[e % 2][:, :], ACT.Gelu).then_inc(s_mid, 1)

                    @block.vector
                    def _(dve):
                        link = Links(dve, s_dve)
                        ln_vector(dve, link, b, s_var, s_rstd, s_h)
                        dve.wait_ge(s_r, 1)
                        r = pT[0][:, 0:NT * E_RT].rearrange("p (i e) -> p i e", i=NT)
                        link(dve.tensor_reduce(great[:, :], r, AX_X, ALU.max))
                        dve.tensor_tensor(lg[:, :, :], r, great[:, :, None].broadcast_to([P, NT, E_RT]),
                                          ALU.subtract).then_inc(s_sub, 1)
                        dve.wait_ge(s_ex, 1)
                        link(dve.tensor_reduce(total[:, :], ex[:, :, :], AX_X, ALU.add))
                        link(dve.reciprocal(inv[:, :], total[:, :]))
                        link(dve.tensor_tensor(pr[:, :, :], ex[:, :, :],
                                               inv[:, :, None].broadcast_to([P, NT, E_RT]), ALU.mult))
                        for i in range(NT):
                            mx = dve.max(top8[:, i, :], pr[:, i, :])
                        link(mx)
                        link(dve.tensor_copy(find[:, :, 0:2], top8[:, :, 0:2]))
                        for i in range(NT):
                            mr = dve.match_replace(mk[:, i, :], find[:, i, :], pr[:, i, :], MARK)
                        link(mr)
                        link(dve.scalar_tensor_tensor(out=gate[:, :, :], in0=mk[:, :, :], scalar=MARK,
                                                      in1=pr[:, :, :], op0=ALU.is_equal, op1=ALU.mult))
                        prev = 0
                        for g, members in enumerate(groups):
                            dve.wait_ge(s_dn, g + 1)
                            for i in range(NT):
                                if g:
                                    dve.wait_ge(s_xo, NT * (g - 1) + i + 1)
                                o = pD[2 * (g % 2) + i // 2][:, (i % 2) * D:(i % 2 + 1) * D]
                                if g == 0:
                                    st = dve.tensor_tensor(x_tile(b, i), o, x_tile(b, i), ALU.add)
                                else:
                                    st = dve.scalar_tensor_tensor(out=x_tile(b, i), in0=o,
                                                                  scalar=gate[:, i, g - 1:g],
                                                                  in1=x_tile(b, i), op0=ALU.mult, op1=ALU.add)
                                st.then_inc(s_xo, 1)

                    @block.gpsimd
                    def _(pool):
                        ln_gpsimd(pool, s_var, s_rstd)
                clear(sems)
        def block_attention():
          NPR = HB // 2
          HR = P // 2
          MROW = 48
          NV = HDB + 1
          PTW = T + (T - P) + (T - 2 * P) + (T - 3 * P)
          RING = 6
          NG = HB // 4
          AT = [0, T, 2 * T, T + (T - P)]
          with ExitStack() as ctx:
            WT = sb(ctx, "b_WT", [P, DC, 3 * D])
            WoT = sb(ctx, "b_WoT", [P, DC, D])
            Wg1T = sb(ctx, "b_Wg1T", [P, DC, HDB])
            Wg2T = sb(ctx, "b_Wg2T", [HDB, D])
            table = sb(ctx, "b_table", [P, NT, 2 * HDB])
            tri = sb(ctx, "b_tri", [P, P], BF16)
            identb = sb(ctx, "b_identb", [P, P], BF16)
            avg = sb(ctx, "b_avg", [P, CPT])
            own = sb(ctx, "b_own", [P, P // HDB])
            onehot = sb(ctx, "b_onehot", [P, NT, NCH])
            past = sb(ctx, "b_past", [P, NT, NCH])
            notself = sb(ctx, "b_notself", [P, NT, NCH])
            bank = psum(ctx, "b_bank", [P, 8, 512])
            d_w = sem(ctx, "b_d_w")
            s_g0, s_g1, s_g2, s_g3, s_wT, s_z = (sem(ctx, "b_" + n) for n in ("c0", "c1", "c2", "c3", "wT", "z"))
            with ExitStack() as first:
                raw = sb(first, "b_raw", [P, 4, DC, D])
                rawg1 = sb(first, "b_rawg1", [HDB, D])
                rawg2 = sb(first, "b_rawg2", [P, DC, HDB])
                wcol = sb(first, "b_wcol", [P, 1])
                with nc.Block() as block:
                    @block.sync
                    def _(sp):
                        for n, w in enumerate((Wq_b, Wk_b, Wv_b, Wo_b)):
                            sp.dma_start(raw[:, n, :, :], w.rearrange("(m p) d -> p m d", p=P)).then_inc(d_w, 16)
                        sp.dma_start(rawg1[:, :], Wg1).then_inc(d_w, 16)
                        sp.dma_start(rawg2[:, :, :], Wg2.rearrange("(m p) d -> p m d", p=P)).then_inc(d_w, 16)
                        sp.dma_start(table[:, :, :], rope.rearrange("(i p) e -> p i e", p=P)).then_inc(d_w, 16)
                        for r in range(P // HDB):
                            sp.dma_start(wcol[r * HDB:(r + 1) * HDB, :],
                                         o_norm.rearrange("(d o) -> d o", o=1)).then_inc(d_w, 16)
                        sp.wait_ge(d_w, 16 * (7 + P // HDB))

                    @block.tensor
                    def _(pe):
                        pe.wait_ge(d_w, 16 * (7 + P // HDB))
                        for n in range(4):
                            for m in range(DC):
                                for c in range(DC):
                                    pe.transpose(bank[:, n, c * D + m * P:c * D + m * P + P],
                                                 raw[:, n, m, c * P:(c + 1) * P], ident[:, :])
                        for m in range(DC):
                            pe.transpose(bank[:, 4, m * HDB:(m + 1) * HDB], rawg1[:, m * P:(m + 1) * P],
                                         ident[0:HDB, 0:HDB])
                        for m in range(DC):
                            t = pe.transpose(bank[0:HDB, 5, m * P:(m + 1) * P], rawg2[:, m, :], ident[:, :])
                        t.then_inc(s_wT, 1)

                    @block.scalar
                    def _(act):
                        act.wait_ge(s_wT, 1)
                        for n in range(3):
                            act.activation(WT[:, :, n * D:(n + 1) * D],
                                           bank[:, n, :].rearrange("p (c o) -> p c o", c=DC), ACT.Copy)
                        act.activation(WoT[:, :, :], bank[:, 3, :].rearrange("p (c o) -> p c o", c=DC),
                                       ACT.Copy, scale=wcol[:, 0:1])
                        act.activation(Wg1T[:, :, :], bank[:, 4, 0:DC * HDB].rearrange("p (c o) -> p c o", c=DC), ACT.Copy)
                        act.activation(Wg2T[:, :], bank[0:HDB, 5, 0:D], ACT.Copy)

                    @block.gpsimd
                    def _(pool):
                        pool.memset(tri[:, :], 0.0)
                        pool.memset(avg[:, :], 1.0 / CH)
                        pool.memset(own[:, :], 1.0)
                        pool.memset(onehot[:, :, :], 1.0)
                        pool.memset(past[:, :, :], 0.0)
                        pool.tensor_copy(identb[:, :], ident[:, :]).then_inc(s_g0, 1)
                        pool.wait_ge(s_g0, 1)

                        def keep(t, base, pattern, mult, fill):
                            return pool.affine_select(out=t, in_=t, compare_op=ALU.is_ge, fill=fill, base=base,
                                                      pattern=pattern, channel_multiplier=mult)

                        keep(tri[:, :], 0, [[1, P]], -1, NEG)
                        keep(avg[:, :], 0, [[-CH, CPT]], 1, 0.0)
                        keep(own[:, :], 0, [[-HDB, P // HDB]], 1, 0.0)
                        keep(onehot[:, :, :], 0, [[P, NT], [-CH, NCH]], 1, 0.0)
                        keep(past[:, :, :], -CH, [[P, NT], [-CH, NCH]], 1, NEG).then_inc(s_g1, 1)
                        pool.wait_ge(s_g1, 1)
                        keep(avg[:, :], CH - 1, [[CH, CPT]], -1, 0.0)
                        keep(own[:, :], HDB - 1, [[HDB, P // HDB]], -1, 0.0)
                        keep(onehot[:, :, :], CH - 1, [[-P, NT], [CH, NCH]], -1, 0.0).then_inc(s_g2, 1)

                    @block.vector
                    def _(dve):
                        dve.wait_ge(s_g2, 1)
                        dve.tensor_scalar(notself[:, :, :], onehot[:, :, :], -NEG, NEG, ALU.mult, ALU.add)

            QT = sb(ctx, "b_QT", [P, NPR, T], F32R)
            KT = sb(ctx, "b_KT", [P, HB, T], F32R)
            VA = sb(ctx, "b_VA", [P, NT, HB * NV + 32])
            rows = sb(ctx, "b_rows", [P, 2 * HB, HR])
            rot = sb(ctx, "b_rot", [P, 2 * HB, HDB])
            rotA = sb(ctx, "b_rotA", [P, 2 * HB, HDB])
            rotB = sb(ctx, "b_rotB", [P, 2 * HB, HDB])
            qT = sb(ctx, "b_qT", [P, DC, P])
            kmean = sb(ctx, "b_kmean", [P, DC, P // HDB, NCH])
            gm = sb(ctx, "b_gm", [P, HB, NCH])
            mk = sb(ctx, "b_mk", [P, HB, NCH])
            top8 = sb(ctx, "b_top8", [P, HB, 8])
            find = sb(ctx, "b_find", [P, HB, 8])
            negmax = sb(ctx, "b_negmax", [P, NT, HB])
            mrow = sb(ctx, "b_mrow", [P, NT, 2, 2, NPR])
            mT = rotA[0:4 * NPR, :, :].rearrange("p h e -> p (h e)").bitcast(F32R)
            PT = sb(ctx, "b_PT", [P, RING, PTW])
            OT = sb(ctx, "b_OT", [P, T])
            rden = sb(ctx, "b_rden", [P, NT, 4])
            O = h[:, :, :].rearrange("p i (h e) -> p i h e", e=HDB)
            g1 = OT[0:HDB, :]
            sig = sb(ctx, "b_sig", [P, NT, D])
            ms = sb(ctx, "b_ms", [P, NT * HB])
            rms = sb(ctx, "b_rms", [P, NT * HB])
            sq = rot
            OGT = hT

            with nc.Block() as block:
                @block.gpsimd
                def _(pool):
                    pool.memset(KT[HR:P, 0:HB:2, :].bitcast(F32), 0.0).then_inc(s_g3, 1)
                    pool.wait_ge(s_g3, 1)
                    pool.memset(rows[:, :, MROW:HR], 0.0).then_inc(s_g3, 1)
                    pool.wait_ge(s_g3, 2)
                    pool.memset(rows[:, HB:2 * HB, MROW:MROW + 2], 1.0)

                @block.vector
                def _(dve):
                    dve.memset(KT[0:HR, 1:HB:2, :].bitcast(F32), 0.0)
                    dve.memset(find[:, :, :], NONE)
                    dve.memset(kmean[:, :, :, :], 0.0)
                    dve.memset(VA[:, :, :], 0.0).then_inc(s_z, 1)
                    dve.wait_ge(s_z, 1)
                    dve.memset(VA[:, :, 0:HB * NV].rearrange("p i (h e) -> p i h e", e=NV)[:, :, :, HDB:NV], 1.0)

            sems = [sem(ctx, "b_" + n) for n in
                    ("var", "rstd", "h", "hT", "hTs", "g1", "g1s", "g", "eg", "eg1", "sig",
                     "qkv", "v", "rp", "rot", "qt", "qts", "km", "gm", "gt", "hi", "lo", "sel", "cp", "oh", "tq", "tqs",
                     "tks0", "tks1", "s1", "mx", "mr", "mt", "mts", "mdma", "s2", "e2", "pv", "ot", "ott", "on",
                     "sq", "ms", "mse", "rms", "orm", "og", "gT", "gTs", "o", "xo", "dve")]
            (s_var, s_rstd, s_h, s_hT, s_hTs, s_g1, s_g1s, s_g, s_eg, s_eg1, s_sig,
             s_qkv, s_v, s_rp, s_rot, s_qt, s_qts, s_km, s_gm, s_gt, s_hi, s_lo, s_sel, s_cp, s_oh, s_tq, s_tqs,
             s_tks0, s_tks1, s_s1, s_mx, s_mr, s_mt, s_mts, s_mdma, s_s2, s_e2, s_pv, s_ot, s_ott, s_on,
             s_sq, s_ms, s_mse, s_rms, s_orm, s_og, s_gT, s_gTs, s_o, s_xo, s_dve) = sems

            NF = 8
            UNITS = [(p, i) for p in range(NPR) for i in range(NT)]

            with nc.Fori(0, B) as b:
                with nc.Block() as block:
                    @block.sync
                    def _(sp):
                        sp.wait_ge(s_mts, 1)
                        sp.wait_ge(s_mx, len(UNITS))
                        for a in range(2):
                            for j in range(2):
                                r = HR * a + MROW + j
                                sp.dma_start(QT[r:r + 1, :, :].bitcast(F32),
                                             mT[(2 * a + j) * NPR:(2 * a + j + 1) * NPR, :].bitcast(F32)).then_inc(s_mdma, 16)
                        sp.wait_ge(s_mdma, 64)

                    @block.tensor
                    def _(pe):
                        ln_turn(pe, [bank[:, 0, :], bank[:, 1, :]], s_h, s_hT)
                        pe.wait_ge(s_hTs, DC)
                        for c in range(DC):
                            mm = pe.matmul(bank[0:HDB, 4, :], Wg1T[:, c, :], hT[:, c, :],
                                           start=(c == 0), stop=(c == DC - 1))
                        mm.then_inc(s_g1, 1)
                        pe.wait_ge(s_g1s, 1)
                        for i in range(NT):
                            mm = pe.matmul(bank[:, 5 + i // 2, (i % 2) * D:(i % 2 + 1) * D], g1[:, i * P:(i + 1) * P],
                                           Wg2T[:, :], start=True, stop=True)
                        mm.then_inc(s_g, 1)

                        def project(i):
                            if i:
                                pe.wait_ge(s_rp, i)
                                pe.wait_ge(s_v, i)
                            for lo, hi, k in ((0, 2 * D, 0), (2 * D, 3 * D, 1)):
                                for c in range(DC):
                                    mm = pe.matmul(bank[:, k, 0:hi - lo], hT[:, c, i * P:(i + 1) * P],
                                                   WT[:, c, lo:hi], start=(c == 0), stop=(c == DC - 1))
                            mm.then_inc(s_qkv, 1)

                        project(0)
                        for i in range(NT):
                            pe.wait_ge(s_rot, i + 1)
                            if i:
                                pe.wait_ge(s_qts, i)
                                pe.wait_ge(s_km, i)
                            if i >= 2:
                                pe.wait_ge(s_gm, i - 1)
                            flat = rot[:, :, :].rearrange("p h e -> p (h e)")
                            for m in range(DC):
                                pe.transpose(bank[:, 2, m * P:(m + 1) * P], flat[:, m * P:(m + 1) * P], ident[:, :])
                            for m in range(DC):
                                mm = pe.matmul(bank[:, 3, m * CPT:(m + 1) * CPT],
                                               flat[:, D + m * P:D + (m + 1) * P], avg[:, :], start=True, stop=True)
                            mm.then_inc(s_qt, 1)
                            if i:
                                pe.wait_ge(s_qts, i + 1)
                                pe.wait_ge(s_km, i + 1)
                                for m in range(DC):
                                    mm = pe.matmul(bank[:, 3, m * D:(m + 1) * D], qT[:, m, :],
                                                   kmean[:, m, :, :].rearrange("p h n -> p (h n)"),
                                                   start=True, stop=True)
                                mm.then_inc(s_gt, 1)
                            if i + 1 < NT:
                                project(i + 1)
                            pe.wait_ge(s_cp, i + 1)
                            pe.wait_ge(s_sel, i + 1)
                            if i == 0:
                                pe.wait_ge(s_eg, 2)
                            for f in range(NF):
                                n = NF * i + f
                                if n >= 4:
                                    last = n - 4
                                    q, r = divmod(last, NF)
                                    if r < 4:
                                        pe.wait_ge(s_tqs, 4 * q + r + 1)
                                    else:
                                        pe.wait_ge(s_tks0, 4 * q + r - 3)
                                        pe.wait_ge(s_tks1, 4 * q + r - 3)
                                for k in range(4):
                                    hd = (8 * f if f < 4 else HB + 8 * (f - 4)) + 2 * k
                                    t = pe.transpose(bank[:, 4 + f % 4, k * P:(k + 1) * P],
                                                     rows[:, hd:hd + 2, :].rearrange("p h r -> p (h r)"), ident[:, :])
                                t.then_inc(s_tq, 1)

                        pe.wait_ge(s_tqs, 4 * NT)
                        pe.wait_ge(s_tks0, 4 * NT)
                        pe.wait_ge(s_tks1, 4 * NT)
                        for u, (p, i) in enumerate(UNITS):
                            if u >= 4:
                                pe.wait_ge(s_mx, u - 3)
                            for a in range(2):
                                k = 2 * (u % 4) + a
                                pe.matmul(bank[:, k, 0:P * (i + 1)], QT[:, p, i * P:(i + 1) * P],
                                          KT[:, 2 * p + a, 0:P * (i + 1)], start=True, stop=True)
                                mm = pe.matmul(bank[:, k, P * i:P * (i + 1)], tri[:, :], identb[:, :],
                                               start=False, stop=True, skip_group_check=True)
                            mm.then_inc(s_s1, 1)
                        pe.wait_ge(s_mr, 1)
                        for i in range(NT):
                            t = pe.transpose(bank[0:4 * NPR, 7, i * P:(i + 1) * P],
                                             mrow[:, i, :, :, :].rearrange("p a j c -> p (a j c)"), ident[:, :])
                        t.then_inc(s_mt, 1)
                        pe.wait_ge(s_mdma, 64)

                        def scores(hd):
                            if hd >= 2:
                                pe.wait_ge(s_e2, hd - 1)
                            k0 = 3 * (hd % 2)
                            for j in (0, 1, 3, 2):
                                w = T - P * j
                                o = bank[:, k0 + AT[j] // T, AT[j] % T:AT[j] % T + w]
                                pe.matmul(o, KT[:, hd, j * P:(j + 1) * P], QT[:, hd // 2, j * P:T],
                                          start=True, stop=True, skip_group_check=True)
                                mm = pe.matmul(o[:, 0:P], identb[:, :], tri[:, :], start=False, stop=True,
                                               skip_group_check=True)
                            mm.then_inc(s_s2, 1)

                        def values(g):
                            pe.wait_ge(s_e2, 4 * g + 4)
                            if g == 1:
                                pe.wait_ge(s_mts, 1)
                            if g >= 2:
                                pe.wait_ge(s_on, g - 1)
                            for j in range(NT):
                                for s in range(4):
                                    hd = 4 * g + s
                                    mm = pe.matmul(bank[32 * s:32 * s + 32, 6 + g % 2, j * P:T],
                                                   VA[:, j, hd * NV:hd * NV + 32],
                                                   PT[:, hd % RING, AT[j]:AT[j] + T - P * j],
                                                   start=(j == 0), stop=True, skip_group_check=True)
                            mm.then_inc(s_pv, 1)

                        def turn(g):
                            pe.wait_ge(s_ot, g + 1)
                            for i in range(NT):
                                t = pe.transpose(bank[:, 6 + g % 2, i * P:(i + 1) * P], OT[:, i * P:(i + 1) * P],
                                                 ident[:, :])
                            t.then_inc(s_ott, 1)

                        for hd in range(4):
                            scores(hd)
                        for g in range(NG):
                            if g + 1 < NG:
                                scores(4 * g + 4)
                                scores(4 * g + 5)
                            values(g)
                            if g + 1 < NG:
                                scores(4 * g + 6)
                                scores(4 * g + 7)
                            turn(g)
                        for m in range(DC):
                            for i in range(NT):
                                pe.wait_ge(s_og, i + 1)
                                t = pe.transpose(bank[:, m, i * P:(i + 1) * P],
                                                 O[:, i, :, :].rearrange("p h e -> p (h e)")[:, m * P:(m + 1) * P],
                                                 ident[:, :])
                        t.then_inc(s_gT, 1)
                        pe.wait_ge(s_gTs, DC)
                        for i in range(NT):
                            for c in range(DC):
                                mm = pe.matmul(bank[:, 2 + i, 0:D], OGT[:, c, i * P:(i + 1) * P], WoT[:, c, :],
                                               start=(c == 0), stop=(c == DC - 1))
                            mm.then_inc(s_o, 1)

                    @block.scalar
                    def _(act):
                        ln_keep(act, [bank[:, 0, :], bank[:, 1, :]], s_hT, s_hTs)
                        act.wait_ge(s_g1, 1)
                        act.activation(g1[:, :], bank[0:HDB, 4, :], ACT.Copy).then_inc(s_g1s, 1)
                        act.wait_ge(s_g, 1)
                        for k in range(2):
                            act.activation(sig[:, 2 * k:2 * k + 2, :].rearrange("p i d -> p (i d)"), bank[:, 5 + k, :],
                                           ACT.Exp, scale=-1.0).then_inc(s_eg, 1)
                        for i in range(NT):
                            act.wait_ge(s_qkv, i + 1)
                            act.activation(VA[:, i, 0:HB * NV].rearrange("p (h e) -> p h e", e=NV)[:, :, 0:HDB],
                                           bank[:, 1, 0:D].rearrange("p (h e) -> p h e", e=HDB), ACT.Copy).then_inc(s_v, 1)
                            act.wait_ge(s_qt, i + 1)
                            if i >= 2:
                                act.wait_ge(s_gt, i - 1)
                            act.activation(qT[:, :, :], bank[:, 2, 0:DC * P].rearrange("p (m t) -> p m t", m=DC),
                                           ACT.Copy).then_inc(s_qts, 1)
                            for f in range(NF):
                                act.wait_ge(s_tq, NF * i + f + 1)
                                if f < 4:
                                    act.activation(QT[:, 4 * f:4 * f + 4, i * P:(i + 1) * P],
                                                   bank[:, 4 + f, :].rearrange("p (k t) -> p k t", k=4),
                                                   ACT.Copy).then_inc(s_tqs, 1)
                                else:
                                    h0 = 8 * (f - 4) + 1
                                    act.activation(KT[HR:P, h0:h0 + 7:2, i * P:(i + 1) * P],
                                                   bank[HR:P, f, :].rearrange("p (k t) -> p k t", k=4),
                                                   ACT.Copy).then_inc(s_tks1, 1)
                        act.wait_ge(s_mt, 1)
                        act.activation(mT[:, :], bank[0:4 * NPR, 7, :], ACT.Copy).then_inc(s_mts, 1)
                        for hd in range(HB):
                            act.wait_ge(s_s2, hd + 1)
                            if hd >= RING:
                                act.wait_ge(s_pv, (hd - RING) // 4 + 1)
                            k0 = 3 * (hd % 2)
                            act.activation(PT[:, hd % RING, :],
                                           bank[:, k0:k0 + 3, :].rearrange("p k t -> p (k t)")[:, 0:PTW],
                                           ACT.Exp, scale=SCALE_B).then_inc(s_e2, 1)
                        act.wait_ge(s_gT, 1)
                        for m in range(DC):
                            act.activation(OGT[:, m, :], bank[:, m, :], ACT.Copy).then_inc(s_gTs, 1)

                    @block.vector
                    def _(dve):
                        link = Links(dve, s_dve)
                        ln_vector(dve, link, b, s_var, s_rstd, s_h)
                        dve.wait_ge(s_eg1, 1)
                        dve.reciprocal(sig[:, :, :], sig[:, :, :]).then_inc(s_sig, 1)
                        for i in range(NT):
                            dve.wait_ge(s_qkv, i + 1)
                            if i:
                                dve.wait_ge(s_rot, i)
                            qk = bank[:, 0, :].rearrange("p (h e) -> p h e", e=HDB)
                            half = HDB // 2

                            def tab(lo, hi):
                                return table[:, i, None, lo:hi].broadcast_to([P, 2 * HB, hi - lo])

                            dve.tensor_tensor(rotA[:, :, :], qk, tab(0, HDB), ALU.mult)
                            dve.tensor_tensor(rotB[:, :, 0:half], qk[:, :, half:HDB], tab(HDB, HDB + half), ALU.mult)
                            dve.tensor_tensor(rotB[:, :, half:HDB], qk[:, :, 0:half], tab(HDB + half, 2 * HDB),
                                              ALU.mult).then_inc(s_rp, 1)
                            dve.wait_ge(s_rot, i + 1)
                            if i:
                                dve.wait_ge(s_tq, NF * i)
                            link(dve.tensor_copy(rows[:, :, 0:HDB].bitcast(F32R), rot[:, :, :]))
                            dve.tensor_tensor(rows[:, :, 3 * HDB:4 * HDB].bitcast(F32R), rot[:, :, :],
                                              rows[:, :, 0:HDB], ALU.subtract).then_inc(s_lo, 1)
                            dve.wait_ge(s_qt, i + 1)
                            for m in range(DC):
                                c0 = m * CPT
                                km = dve.tensor_tensor(
                                    kmean[:, m, :, i * CPT:(i + 1) * CPT],
                                    bank[:, 3, None, c0:c0 + CPT].broadcast_to([P, P // HDB, CPT]),
                                    own[:, :, None].broadcast_to([P, P // HDB, CPT]), ALU.mult)
                            km.then_inc(s_km, 1)
                            if i == 0:
                                dve.memset(rows[:, 0:HB, 4 * HDB:4 * HDB + NCH], 0.0).then_inc(s_sel, 1)
                            else:
                                dve.wait_ge(s_gt, i)
                                dve.tensor_tensor(gm[:, :, :], bank[:, 3, :].rearrange("p (h n) -> p h n", n=NCH),
                                                  past[:, i, None, :].broadcast_to([P, HB, NCH]), ALU.add).then_inc(s_gm, 1)
                                dve.wait_ge(s_gm, i)
                                for e in range(HB):
                                    mx = dve.max(top8[:, e, :], gm[:, e, :])
                                link(mx)
                                link(dve.tensor_copy(find[:, :, 0:PAST], top8[:, :, 0:PAST]))
                                for e in range(HB):
                                    mr = dve.match_replace(mk[:, e, :], find[:, e, :], gm[:, e, :], MARK)
                                link(mr)
                                dve.scalar_tensor_tensor(out=rows[:, 0:HB, 4 * HDB:4 * HDB + NCH], in0=mk[:, :, :],
                                                         scalar=MARK,
                                                         in1=notself[:, i, None, :].broadcast_to([P, HB, NCH]),
                                                         op0=ALU.not_equal, op1=ALU.mult).then_inc(s_sel, 1)
                            for f in range(4, NF):
                                dve.wait_ge(s_tq, NF * i + f + 1)
                                h0 = 8 * (f - 4)
                                dve.tensor_copy(KT[0:HR, h0:h0 + 7:2, i * P:(i + 1) * P],
                                                bank[0:HR, f, :].rearrange("p (k t) -> p k t", k=4)).then_inc(s_tks0, 1)
                        for u, (p, i) in enumerate(UNITS):
                            dve.wait_ge(s_s1, u + 1)
                            k = 2 * (u % 4)
                            dve.tensor_reduce(negmax[:, i, 2 * p:2 * p + 2], bank[:, k:k + 2, 0:P * (i + 1)], AX_X,
                                              ALU.max, negate=True).then_inc(s_mx, 1)
                        dve.wait_ge(s_mx, len(UNITS))
                        nm = negmax[:, :, :].rearrange("p i (c a) -> p i a c", a=2)
                        link(dve.tensor_copy(mrow[:, :, :, 0, :].bitcast(F32R), nm))
                        dve.tensor_tensor(mrow[:, :, :, 1, :].bitcast(F32R), nm, mrow[:, :, :, 0, :],
                                          ALU.subtract).then_inc(s_mr, 1)

                        def normal(g):
                            dve.wait_ge(s_ott, g + 1)
                            o = bank[:, 6 + g % 2, :].rearrange("p (i s e) -> p i s e", i=NT, s=4)
                            link(dve.reciprocal(rden[:, :, :], o[:, :, :, HDB]))
                            dve.tensor_tensor(O[:, :, 4 * g:4 * g + 4, :], o[:, :, :, 0:HDB],
                                              rden[:, :, :, None].broadcast_to([P, NT, 4, HDB]), ALU.mult).then_inc(s_on, 1)

                        for g in range(NG):
                            dve.wait_ge(s_pv, g + 1)
                            if g:
                                dve.wait_ge(s_ott, g)
                            dve.tensor_copy(OT[:, :], bank[:, 6 + g % 2, :]).then_inc(s_ot, 1)
                            normal(g)
                        dve.wait_ge(s_on, NG)
                        for i in range(NT):
                            dve.wait_ge(s_sq, i + 1)
                            dve.tensor_reduce(ms[:, i * HB:(i + 1) * HB], sq[:, 0:HB, :] if i % 2 == 0 else sq[:, HB:2 * HB, :],
                                              AX_X, ALU.add).then_inc(s_ms, 1)
                        dve.wait_ge(s_ms, NT)
                        dve.tensor_scalar(ms[:, :], ms[:, :], 1.0 / HDB, RMS_EPS, ALU.mult, ALU.add).then_inc(s_mse, 1)
                        dve.wait_ge(s_rms, 1)
                        for i in range(NT):
                            link(dve.tensor_tensor(O[:, i], O[:, i],
                                                   rms[:, i * HB:(i + 1) * HB, None].broadcast_to([P, HB, HDB]), ALU.mult))
                            dve.tensor_tensor(O[:, i].rearrange("p h e -> p (h e)"), O[:, i].rearrange("p h e -> p (h e)"),
                                              sig[:, i, :], ALU.mult).then_inc(s_og, 1)
                        for i in range(NT):
                            dve.wait_ge(s_o, i + 1)
                            dve.tensor_tensor(x_tile(b, i), bank[:, 2 + i, 0:D], x_tile(b, i), ALU.add).then_inc(s_xo, 1)

                    @block.gpsimd
                    def _(pool):
                        ln_gpsimd(pool, s_var, s_rstd)
                        pool.wait_ge(s_eg, 2)
                        pool.tensor_scalar(sig[:, :, :], sig[:, :, :], 1.0, None, ALU.add).then_inc(s_eg1, 1)
                        for i in range(NT):
                            pool.wait_ge(s_rp, i + 1)
                            if i:
                                pool.wait_ge(s_lo, i)
                                pool.wait_ge(s_qt, i)
                            pool.tensor_tensor(rot[:, :, :], rotA[:, :, :], rotB[:, :, :], ALU.add).then_inc(s_rot, 1)
                            if i:
                                pool.wait_ge(s_tq, NF * i)
                            pool.tensor_copy(rows[:, HB:2 * HB, 4 * HDB:4 * HDB + NCH],
                                             onehot[:, i, None, :].broadcast_to([P, HB, NCH]))
                            pool.wait_ge(s_lo, i + 1)
                            lo, hi = slice(3 * HDB, 4 * HDB), slice(0, HDB)
                            pool.tensor_copy(rows[:, 0:HB, HDB:2 * HDB], rows[:, 0:HB, hi])
                            pool.tensor_copy(rows[:, 0:HB, 2 * HDB:3 * HDB], rows[:, 0:HB, lo])
                            pool.tensor_copy(rows[:, HB:2 * HB, HDB:2 * HDB], rows[:, HB:2 * HB, lo])
                            pool.tensor_copy(rows[:, HB:2 * HB, 2 * HDB:3 * HDB], rows[:, HB:2 * HB, hi]).then_inc(s_cp, 1)
                        pool.wait_ge(s_on, NG)
                        for i in range(NT):
                            if i >= 2:
                                pool.wait_ge(s_ms, i - 1)
                            pool.tensor_tensor(sq[:, 0:HB, :] if i % 2 == 0 else sq[:, HB:2 * HB, :],
                                               O[:, i], O[:, i], ALU.mult).then_inc(s_sq, 1)
                        pool.wait_ge(s_mse, 1)
                        pool.tensor_tensor(rms[:, :], ms[:, :], minus_half[:, 0:1].broadcast_to([P, NT * HB]), ALU.pow).then_inc(s_rms, 1)
                clear(sems)

        latent_attention()
        experts(0)
        block_attention()
        experts(1)

        s_out = sem(whole, "s_out")
        with nc.Block() as block:
            @block.sync
            def _(sp):
                for b in range(B):
                    sp.dma_start(out[b].rearrange("(i p) d -> p i d", p=P),
                                 x[:, b * NT * D:(b + 1) * NT * D].rearrange("p (i d) -> p i d", i=NT)).then_inc(s_out, 16)
                sp.wait_ge(s_out, 16 * B)


_INS = ["L0_attn_a_hidden_states", "L0_attn_a_Wq", "L0_attn_a_bq", "L0_attn_a_Wk", "L0_attn_a_bk", "L0_attn_a_Wv",
        "L0_attn_a_bv", "L0_attn_a_Wo", "L0_attn_a_bo", "L0_attn_a_latent_keys", "L0_attn_b_Wq", "L0_attn_b_Wk",
        "L0_attn_b_Wv", "L0_attn_b_Wo", "L0_attn_b_Wg1", "L0_attn_b_Wg2", "L0_attn_b_o_norm_weight",
        "L0_ffn_Wsh_up", "L0_ffn_Wsh_down", "L0_ffn_Wrt_up", "L0_ffn_Wrt_down", "L0_ffn_W_router"]


def rope_table():
    pos = np.arange(T, dtype=np.float32)
    inv_freq = (1.0 / np.float32(THETA) ** (np.arange(0, HDB, 2, dtype=np.float32) / np.float32(HDB))).astype(np.float32)
    ang = (pos[:, None] * inv_freq[None, :]).astype(np.float32)
    c, s = np.cos(ang), np.sin(ang)
    return np.concatenate([c, c, -s, s], axis=1).astype(np.float32)


def kernel(**inputs):
    import numpy as _np
    import concourse.bacc as _bacc
    from concourse import mybir as _mybir
    from concourse.bass_utils import run_bass_kernel_spmd as _run

    nc = _bacc.Bacc("TRN2", target_bir_lowering=False, num_devices=1)
    arrays, args = {}, []
    for name in _INS:
        a = _np.ascontiguousarray(inputs[name])
        arrays[f"in_{name}_dram"] = a
        args.append(nc.dram_tensor(f"in_{name}_dram", a.shape, _mybir.dt.from_np(a.dtype), kind="ExternalInput").ap())
    table = rope_table()
    arrays["rope_dram"] = table
    args.append(nc.dram_tensor("rope_dram", table.shape, _mybir.dt.float32, kind="ExternalInput").ap())
    args.append(nc.dram_tensor("out_0_dram", (B, T, D), _mybir.dt.float32, kind="ExternalOutput").ap())
    program(nc, *args)
    r = _run(nc, [arrays], core_ids=[0])
    return r.results[0]["out_0_dram"]
```

```python
from contextlib import ExitStack

import numpy as np

import concourse.bass as bass
from concourse import mybir

ALU = mybir.AluOpType
ACT = mybir.ActivationFunctionType
AX_X = mybir.AxisListType.X
F32 = mybir.dt.float32
F32R = mybir.dt.float32r
BF16 = mybir.dt.bfloat16

P = 128
B, T, D = 4, 512, 256
NT = T // P
DC = D // P
LN_EPS = 1e-5

HA, HDA = 16, 16
L = 64
TOP_A = 4
HPC = P // HDA
NPAIR_A = HA // 2
SCALE_A = 1.0 / float(np.sqrt(HDA))

HB, HDB = 32, 8
CH = 32
NCH = T // CH
CPT = P // CH
PAST = 3
THETA = 10000.0
RMS_EPS = 1e-6
SCALE_B = 1.0 / float(np.sqrt(HDB))
NEG = -1e30

E_SH, E_RT = 2, 16
E_ALL = E_SH + E_RT
DF = 128

MARK = 3.0e38
NONE = 3.3e38


class Links:

    def __init__(self, eng, sem):
        self.eng, self.sem, self.n = eng, sem, 0

    def __call__(self, ins):
        self.n += 1
        ins.then_inc(self.sem, 1)
        self.eng.wait_ge(self.sem, self.n)


def program(nc, x_in, Wq_a, bq_a, Wk_a, bk_a, Wv_a, bv_a, Wo_a, bo_a, latent,
            Wq_b, Wk_b, Wv_b, Wo_b, Wg1, Wg2, o_norm, Wsh_up, Wsh_down, Wrt_up, Wrt_down, W_router,
            rope, out):
    with ExitStack() as whole:
        def sb(ctx, name, shape, dt=F32):
            return ctx.enter_context(nc.sbuf_tensor(name, shape, dt))

        def psum(ctx, name, shape, dt=F32):
            return ctx.enter_context(nc.psum_tensor(name, shape, dt))

        def sem(ctx, name):
            return ctx.enter_context(nc.semaphore(name))

        def clear(sems):
            nums = sorted(s.num for s in sems)
            assert nums == list(range(nums[0], nums[0] + len(nums)))
            nc.gpsimd.sem_clear(range(nums[0], nums[-1] + 1))
            nc.all_engine_barrier()

        x = sb(whole, "x", [P, B * NT * D])
        ident = sb(whole, "ident", [P, P])
        ones_row = sb(whole, "ones_row", [1, P])
        minus_half = sb(whole, "minus_half", [P, 1])
        ln_stats = sb(whole, "ln_stats", [P, NT, 6])
        ln_mv = sb(whole, "ln_mv", [P, NT, 2])
        ln_var = sb(whole, "ln_var", [P, NT])
        ln_rstd = sb(whole, "ln_rstd", [P, NT])
        h = sb(whole, "h", [P, NT, D])
        hT = sb(whole, "hT", [P, DC, T])

        s_setup = sem(whole, "s_setup")
        s_setup_dma = sem(whole, "s_setup_dma")

        with nc.Block() as block:
            @block.sync
            def _(sp):
                for b in range(B):
                    sp.dma_start(x[:, b * NT * D:(b + 1) * NT * D].rearrange("p (i d) -> p i d", i=NT),
                                 x_in[b].rearrange("(i p) d -> p i d", p=P)).then_inc(s_setup_dma, 16)
                sp.wait_ge(s_setup_dma, 16 * B)

            @block.gpsimd
            def _(pool):
                pool.memset(ident[:, :], 0.0).then_inc(s_setup, 1)
                pool.memset(ones_row[:, :], 1.0)
                pool.memset(minus_half[:, :], -0.5)
                pool.wait_ge(s_setup, 1)
                pool.affine_select(out=ident[:, :], in_=ident[:, :], compare_op=ALU.not_equal, fill=1.0,
                                   base=0, pattern=[[-1, P]], channel_multiplier=1)

        def x_tile(b, i):
            return x[:, bass.ds(b * (NT * D) + i * D, D)]

        def ln_vector(dve, link, b, s_var, s_rstd, s_h):
            for i in range(NT):
                st = dve.bn_stats(ln_stats[:, i, :], x_tile(b, i))
            link(st)
            for i in range(NT):
                st = dve.bn_aggr(ln_mv[:, i, :], ln_stats[:, i, :])
            link(st)
            dve.tensor_scalar(ln_var[:, :], ln_mv[:, :, 1], LN_EPS, None, ALU.add).then_inc(s_var, 1)
            dve.wait_ge(s_rstd, 1)
            for i in range(NT):
                dve.tensor_scalar(h[:, i, :], x_tile(b, i), ln_mv[:, i, 0:1], ln_rstd[:, i:i + 1],
                                  ALU.subtract, ALU.mult).then_inc(s_h, 1)

        def ln_gpsimd(pool, s_var, s_rstd):
            pool.wait_ge(s_var, 1)
            pool.tensor_tensor(ln_rstd[:, :], ln_var[:, :], minus_half[:, 0:1].broadcast_to([P, NT]), ALU.pow).then_inc(s_rstd, 1)

        def ln_turn(pe, banks, s_h, s_hT):
            for i in range(NT):
                pe.wait_ge(s_h, i + 1)
                for m in range(DC):
                    t = pe.transpose(banks[m][:, i * P:(i + 1) * P], h[:, i, m * P:(m + 1) * P], ident[:, :])
            t.then_inc(s_hT, 1)

        def ln_keep(act, banks, s_hT, s_hTs):
            act.wait_ge(s_hT, 1)
            for m in range(DC):
                act.activation(hT[:, m, :], banks[m][:, :], ACT.Copy).then_inc(s_hTs, 1)

        def latent_attention():
          with ExitStack() as ctx:
            WqT = sb(ctx, "a_WqT", [P, DC, D])
            WvT = sb(ctx, "a_WvT", [P, DC, D])
            WoT = sb(ctx, "a_WoT", [P, DC, D])
            bq = sb(ctx, "a_bq", [P, DC])
            bv = sb(ctx, "a_bv", [P, DC])
            bo = sb(ctx, "a_bo", [1, D])
            latT = sb(ctx, "a_latT", [P, DC, HPC, L])
            latP = sb(ctx, "a_latP", [P, NPAIR_A, 2 * HDA])
            lat2 = sb(ctx, "a_lat2", [P, D])
            QT = sb(ctx, "a_QT", [P, DC, T])
            logits = sb(ctx, "a_logits", [P, NT, HA, L])
            marked = sb(ctx, "a_marked", [P, 2, HA, L])
            shifted = sb(ctx, "a_shifted", [P, 2, HA, L])
            probs = sb(ctx, "a_probs", [P, 2, HA, L])
            probsT = sb(ctx, "a_probsT", [P, NPAIR_A, T])
            top8 = sb(ctx, "a_top8", [P, NT, HA, 8])
            find = sb(ctx, "a_find", [P, 2, HA, 8])
            topd = sb(ctx, "a_topd", [P, NT, HA, TOP_A])
            tope = sb(ctx, "a_tope", [P, NT, HA, TOP_A])
            total = sb(ctx, "a_total", [P, NT, HA])
            inv = sb(ctx, "a_inv", [P, NT, HA])
            AOT = sb(ctx, "a_AOT", [P, DC, T])
            raw = sb(ctx, "a_raw", [P, 3, DC, D])
            bk = [psum(ctx, f"a_bank{i}", [P, 512]) for i in range(8)]
            pT, pQ, pL, pP = bk[0:2], bk[2:4], bk[4:6], bk[6:8]
            d_w = sem(ctx, "a_d_w")
            s_zero, s_wT, s_ws, s_lT, s_ls, s_sel = (sem(ctx, "a_" + n) for n in
                                                     ("zero", "wT", "ws", "lT", "ls", "sel"))

            with nc.Block() as block:
                @block.sync
                def _(sp):
                    for n, w in enumerate((Wq_a, Wv_a, Wo_a)):
                        sp.dma_start(raw[:, n, :, :], w.rearrange("(m p) d -> p m d", p=P)).then_inc(d_w, 16)
                    sp.dma_start(lat2[0:L, :], latent).then_inc(d_w, 16)
                    sp.dma_start(lat2[L:2 * L, :], latent).then_inc(d_w, 16)
                    sp.dma_start(bq[:, :], bq_a.rearrange("(m p) -> p m", p=P), allow_slow_non_contiguous=True).then_inc(d_w, 16)
                    sp.dma_start(bv[:, :], bv_a.rearrange("(m p) -> p m", p=P), allow_slow_non_contiguous=True).then_inc(d_w, 16)
                    sp.dma_start(bo[:, :], bo_a.rearrange("(o d) -> o d", o=1)).then_inc(d_w, 16)
                    sp.wait_ge(d_w, 16 * 8)

                @block.tensor
                def _(pe):
                    pe.wait_ge(d_w, 16 * 8)
                    for n in range(3):
                        for m in range(DC):
                            for c in range(DC):
                                t = pe.transpose(bk[n][:, c * D + m * P:c * D + m * P + P],
                                                 raw[:, n, m, c * P:(c + 1) * P], ident[:, :])
                        t.then_inc(s_wT, 1)
                    for m in range(DC):
                        t = pe.transpose(bk[3][:, m * L:(m + 1) * L], lat2[0:L, m * P:(m + 1) * P],
                                         ident[0:L, 0:L])
                    t.then_inc(s_lT, 1)

                @block.scalar
                def _(act):
                    for n, w in enumerate((WqT, WvT, WoT)):
                        act.wait_ge(s_wT, n + 1)
                        act.activation(w[:, :, :], bk[n][:, :].rearrange("p (c o) -> p c o", c=DC), ACT.Copy)

                @block.vector
                def _(dve):
                    dve.memset(find[:, :, :, :], NONE)
                    dve.memset(latP[:, :, :], 0.0).then_inc(s_zero, 1)
                    dve.wait_ge(s_zero, 1)
                    dve.wait_ge(d_w, 16 * 8)
                    pairs = lat2[:, :].rearrange("p (c a e) -> p c a e", a=2, e=HDA)
                    for a in range(2):
                        dve.tensor_copy(latP[a * L:(a + 1) * L, :, a * HDA:(a + 1) * HDA],
                                        pairs[a * L:(a + 1) * L, :, a, :])
                    dve.wait_ge(s_lT, 1)
                    for m in range(DC):
                        for e in range(HPC):
                            t = dve.tensor_copy(latT[:, m, e, :], bk[3][:, m * L:(m + 1) * L])
                    t.then_inc(s_ls, 1)

                @block.gpsimd
                def _(pool):
                    pool.wait_ge(s_ls, 1)
                    v = latT[:, :, :, :]
                    pool.affine_select(out=v, in_=v, compare_op=ALU.is_ge, fill=0.0, base=0,
                                       pattern=[[0, DC], [-HDA, HPC], [0, L]], channel_multiplier=1).then_inc(s_sel, 1)
                    pool.wait_ge(s_sel, 1)
                    pool.affine_select(out=v, in_=v, compare_op=ALU.is_ge, fill=0.0, base=HDA - 1,
                                       pattern=[[0, DC], [HDA, HPC], [0, L]], channel_multiplier=-1).then_inc(s_sel, 1)

            sems = [sem(ctx, "a_" + n) for n in
                    ("var", "rstd", "h", "hT", "hTs", "q", "qs", "l", "lsb", "mx", "d4", "sh", "ex", "ex4",
                     "w", "inv", "pr", "pT", "pTs", "ao", "aos", "o", "xo", "dve")]
            (s_var, s_rstd, s_h, s_hT, s_hTs, s_q, s_qs, s_l, s_lsb, s_mx, s_d4, s_sh, s_ex, s_ex4,
             s_w, s_inv, s_pr, s_pT, s_pTs, s_ao, s_aos, s_o, s_xo, s_dve) = sems

            with nc.Fori(0, B) as b:
                with nc.Block() as block:
                    @block.tensor
                    def _(pe):
                        ln_turn(pe, pT, s_h, s_hT)
                        pe.wait_ge(s_hTs, DC)
                        for m in range(DC):
                            for c in range(DC):
                                mm = pe.matmul(pQ[m][:, :], WqT[:, c, m * P:(m + 1) * P], hT[:, c, :],
                                               start=(c == 0), stop=(c == DC - 1))
                            mm.then_inc(s_q, 1)
                        pe.wait_ge(s_qs, DC)
                        for i in range(NT):
                            if i:
                                pe.wait_ge(s_lsb, i)
                            for m in range(DC):
                                mm = pe.matmul(pL[m][:, :], QT[:, m, i * P:(i + 1) * P],
                                               latT[:, m, :, :].rearrange("p e l -> p (e l)"), start=True, stop=True)
                            mm.then_inc(s_l, 1)
                        for m in range(DC):
                            for c in range(DC):
                                pe.matmul(pQ[m][:, :], WvT[:, c, m * P:(m + 1) * P], hT[:, c, :],
                                          start=(c == 0), stop=False, skip_group_check=True)
                        for i in range(NT):
                            pe.wait_ge(s_pr, i + 1)
                            if i:
                                pe.wait_ge(s_pTs, i)
                            for c in range(NPAIR_A):
                                t = pe.transpose(pP[c // 4][:, (c % 4) * P:(c % 4 + 1) * P],
                                                 probs[:, i % 2, 2 * c:2 * c + 2, :].rearrange("p e l -> p (e l)"),
                                                 ident[:, :])
                            t.then_inc(s_pT, 1)
                        pe.wait_ge(s_pTs, NT)
                        for m in range(DC):
                            for q in range(4):
                                mm = pe.matmul(pQ[m][32 * q:32 * q + 32, :], latP[:, 4 * m + q, :],
                                               probsT[:, 4 * m + q, :], start=False, stop=True,
                                               skip_group_check=True)
                            mm.then_inc(s_ao, 1)
                        pe.wait_ge(s_aos, DC)
                        for i in range(NT):
                            if i >= 2:
                                pe.wait_ge(s_xo, i - 1)
                            o = pT[i % 2][:, 0:D]
                            pe.matmul(o, ones_row[:, :], bo[:, :], start=True, stop=False)
                            for c in range(DC):
                                mm = pe.matmul(o, AOT[:, c, i * P:(i + 1) * P], WoT[:, c, :],
                                               start=False, stop=(c == DC - 1))
                            mm.then_inc(s_o, 1)

                    @block.scalar
                    def _(act):
                        ln_keep(act, pT, s_hT, s_hTs)
                        for m in range(DC):
                            act.wait_ge(s_q, m + 1)
                            act.activation(QT[:, m, :], pQ[m][:, :], ACT.Identity, bias=bq[:, m:m + 1]).then_inc(s_qs, 1)
                        for i in range(NT):
                            act.wait_ge(s_l, i + 1)
                            for m in range(DC):
                                cp = act.activation(logits[:, i, HPC * m:HPC * (m + 1), :].rearrange("p e l -> p (e l)"),
                                                    pL[m][:, :], ACT.Copy, scale=SCALE_A)
                            cp.then_inc(s_lsb, 1)

                        def turned(i):
                            act.wait_ge(s_pT, i + 1)
                            for c in range(2):
                                cp = act.activation(probsT[:, 4 * c:4 * c + 4, i * P:(i + 1) * P],
                                                    pP[c][:, :].rearrange("p (c t) -> p c t", c=4), ACT.Copy)
                            cp.then_inc(s_pTs, 1)

                        for i in range(NT):
                            act.wait_ge(s_sh, i + 1)
                            act.activation(shifted[:, i % 2], shifted[:, i % 2], ACT.Exp).then_inc(s_ex, 1)
                            act.wait_ge(s_d4, i + 1)
                            act.activation(tope[:, i], topd[:, i], ACT.Exp).then_inc(s_ex4, 1)
                            if i:
                                turned(i - 1)
                        turned(NT - 1)
                        for m in range(DC):
                            act.wait_ge(s_ao, m + 1)
                            act.activation(AOT[:, m, :], pQ[m][:, :], ACT.Identity, bias=bv[:, m:m + 1]).then_inc(s_aos, 1)

                    @block.vector
                    def _(dve):
                        link = Links(dve, s_dve)
                        ln_vector(dve, link, b, s_var, s_rstd, s_h)

                        def weights(i):
                            dve.wait_ge(s_ex, i + 1)
                            if i >= 2:
                                dve.wait_ge(s_pT, i - 1)
                            dve.scalar_tensor_tensor(out=probs[:, i % 2], in0=marked[:, i % 2], scalar=MARK,
                                                     in1=shifted[:, i % 2], op0=ALU.is_equal, op1=ALU.mult).then_inc(s_w, 1)
                            dve.wait_ge(s_ex4, i + 1)
                            link(dve.tensor_reduce(total[:, i], tope[:, i], AX_X, ALU.add))
                            dve.reciprocal(inv[:, i], total[:, i]).then_inc(s_inv, 1)

                        for i in range(NT):
                            dve.wait_ge(s_lsb, i + 1)
                            for e in range(HA):
                                mx = dve.max(top8[:, i, e, :], logits[:, i, e, :])
                            link(mx)
                            dve.tensor_tensor(topd[:, i], top8[:, i, :, 0:TOP_A],
                                              top8[:, i, :, 0:1].broadcast_to([P, HA, TOP_A]), ALU.subtract).then_inc(s_d4, 1)
                            link(dve.tensor_copy(find[:, i % 2, :, 0:TOP_A], top8[:, i, :, 0:TOP_A]))
                            for e in range(HA):
                                mr = dve.match_replace(marked[:, i % 2, e, :], find[:, i % 2, e, :],
                                                       logits[:, i, e, :], MARK)
                            link(mr)
                            if i:
                                weights(i - 1)
                        weights(NT - 1)
                        for i in range(NT):
                            dve.wait_ge(s_o, i + 1)
                            dve.tensor_tensor(x_tile(b, i), pT[i % 2][:, 0:D], x_tile(b, i), ALU.add).then_inc(s_xo, 1)

                    @block.gpsimd
                    def _(pool):
                        ln_gpsimd(pool, s_var, s_rstd)

                        def scaled(i):
                            pool.wait_ge(s_w, i + 1)
                            pool.wait_ge(s_inv, i + 1)
                            pool.tensor_tensor(probs[:, i % 2], probs[:, i % 2],
                                               inv[:, i, :, None].broadcast_to([P, HA, L]), ALU.mult).then_inc(s_pr, 1)

                        for i in range(NT):
                            if i >= 2:
                                pool.wait_ge(s_w, i - 1)
                            pool.wait_ge(s_d4, i + 1)
                            pool.tensor_tensor(shifted[:, i % 2], logits[:, i],
                                               top8[:, i, :, 0:1].broadcast_to([P, HA, L]), ALU.subtract).then_inc(s_sh, 1)
                            if i:
                                scaled(i - 1)
                        scaled(NT - 1)
                clear(sems)

        def experts(n):
          with ExitStack() as ctx:
            w_up = sb(ctx, f"f{n}_w_up", [P, E_ALL, DC, DF])
            w_down = sb(ctx, f"f{n}_w_down", [P, E_ALL, D])
            w_r = sb(ctx, f"f{n}_w_r", [P, DC, E_RT])
            mid = sb(ctx, f"f{n}_mid", [P, 2, T])
            lg = sb(ctx, f"f{n}_lg", [P, NT, E_RT])
            ex = sb(ctx, f"f{n}_ex", [P, NT, E_RT])
            pr = sb(ctx, f"f{n}_pr", [P, NT, E_RT])
            mk = sb(ctx, f"f{n}_mk", [P, NT, E_RT])
            gate = sb(ctx, f"f{n}_gate", [P, NT, E_RT])
            great = sb(ctx, f"f{n}_great", [P, NT])
            total = sb(ctx, f"f{n}_total", [P, NT])
            inv = sb(ctx, f"f{n}_inv", [P, NT])
            top8 = sb(ctx, f"f{n}_top8", [P, NT, 8])
            find = sb(ctx, f"f{n}_find", [P, NT, 8])
            bk = [psum(ctx, f"f{n}_bank{i}", [P, 512]) for i in range(8)]
            pT, pU, pD = bk[0:2], bk[2:4], bk[4:8]
            d_w = sem(ctx, f"f{n}_d_w")
            with nc.Block() as block:
                @block.sync
                def _(sp):
                    sp.dma_start(w_r[:, :, :], W_router.rearrange("(m p) e -> p m e", p=P)).then_inc(d_w, 16)
                    k = 1
                    for lo, count, up, down in ((0, E_SH, Wsh_up, Wsh_down), (E_SH, E_RT, Wrt_up, Wrt_down)):
                        for e in range(count):
                            sp.dma_start(w_up[:, lo + e], up[e].rearrange("(m p) f -> p m f", p=P)).then_inc(d_w, 16)
                            sp.dma_start(w_down[:, lo + e, :], down[e]).then_inc(d_w, 16)
                            k += 2
                    sp.wait_ge(d_w, 16 * k)

                @block.vector
                def _(dve):
                    dve.memset(find[:, :, :], NONE)

            sems = [sem(ctx, f"f{n}_" + s) for s in
                    ("var", "rstd", "h", "hT", "hTs", "r", "sub", "ex", "up", "mid", "dn", "xo", "dve")]
            (s_var, s_rstd, s_h, s_hT, s_hTs, s_r, s_sub, s_ex, s_up, s_mid, s_dn, s_xo, s_dve) = sems

            groups = [list(range(E_SH))] + [[e] for e in range(E_SH, E_ALL)]

            with nc.Fori(0, B) as b:
                with nc.Block() as block:
                    @block.tensor
                    def _(pe):
                        ln_turn(pe, pT, s_h, s_hT)
                        pe.wait_ge(s_hTs, DC)
                        for i in range(NT):
                            for c in range(DC):
                                mm = pe.matmul(pT[0][:, i * E_RT:(i + 1) * E_RT], hT[:, c, i * P:(i + 1) * P],
                                               w_r[:, c, :], start=(c == 0), stop=(c == DC - 1))
                        mm.then_inc(s_r, 1)

                        def up(e):
                            if e >= 2:
                                pe.wait_ge(s_mid, e - 1)
                            for c in range(DC):
                                mm = pe.matmul(pU[e % 2][:, :], w_up[:, e, c, :], hT[:, c, :],
                                               start=(c == 0), stop=(c == DC - 1))
                            mm.then_inc(s_up, 1)

                        up(0)
                        for g, members in enumerate(groups):
                            for e in members:
                                if e + 1 < E_ALL:
                                    up(e + 1)
                            pe.wait_ge(s_mid, members[-1] + 1)
                            if g >= 2:
                                pe.wait_ge(s_xo, NT * (g - 1))
                            for i in range(NT):
                                o = pD[2 * (g % 2) + i // 2][:, (i % 2) * D:(i % 2 + 1) * D]
                                for e in members:
                                    mm = pe.matmul(o, mid[:, e % 2, i * P:(i + 1) * P], w_down[:, e, :],
                                                   start=(e == members[0]), stop=(e == members[-1]))
                            mm.then_inc(s_dn, 1)

                    @block.scalar
                    def _(act):
                        ln_keep(act, pT, s_hT, s_hTs)
                        act.wait_ge(s_sub, 1)
                        act.activation(ex[:, :, :], lg[:, :, :], ACT.Exp).then_inc(s_ex, 1)
                        group_of = [g for g, members in enumerate(groups) for _ in members]
                        for e in range(E_ALL):
                            act.wait_ge(s_up, e + 1)
                            if e >= 2:
                                act.wait_ge(s_dn, group_of[e - 2] + 1)
                            act.activation(mid[:, e % 2, :], pU[e % 2][:, :], ACT.Gelu).then_inc(s_mid, 1)

                    @block.vector
                    def _(dve):
                        link = Links(dve, s_dve)
                        ln_vector(dve, link, b, s_var, s_rstd, s_h)
                        dve.wait_ge(s_r, 1)
                        r = pT[0][:, 0:NT * E_RT].rearrange("p (i e) -> p i e", i=NT)
                        link(dve.tensor_reduce(great[:, :], r, AX_X, ALU.max))
                        dve.tensor_tensor(lg[:, :, :], r, great[:, :, None].broadcast_to([P, NT, E_RT]),
                                          ALU.subtract).then_inc(s_sub, 1)
                        dve.wait_ge(s_ex, 1)
                        link(dve.tensor_reduce(total[:, :], ex[:, :, :], AX_X, ALU.add))
                        link(dve.reciprocal(inv[:, :], total[:, :]))
                        link(dve.tensor_tensor(pr[:, :, :], ex[:, :, :],
                                               inv[:, :, None].broadcast_to([P, NT, E_RT]), ALU.mult))
                        for i in range(NT):
                            mx = dve.max(top8[:, i, :], pr[:, i, :])
                        link(mx)
                        link(dve.tensor_copy(find[:, :, 0:2], top8[:, :, 0:2]))
                        for i in range(NT):
                            mr = dve.match_replace(mk[:, i, :], find[:, i, :], pr[:, i, :], MARK)
                        link(mr)
                        link(dve.scalar_tensor_tensor(out=gate[:, :, :], in0=mk[:, :, :], scalar=MARK,
                                                      in1=pr[:, :, :], op0=ALU.is_equal, op1=ALU.mult))
                        prev = 0
                        for g, members in enumerate(groups):
                            dve.wait_ge(s_dn, g + 1)
                            for i in range(NT):
                                if g:
                                    dve.wait_ge(s_xo, NT * (g - 1) + i + 1)
                                o = pD[2 * (g % 2) + i // 2][:, (i % 2) * D:(i % 2 + 1) * D]
                                if g == 0:
                                    st = dve.tensor_tensor(x_tile(b, i), o, x_tile(b, i), ALU.add)
                                else:
                                    st = dve.scalar_tensor_tensor(out=x_tile(b, i), in0=o,
                                                                  scalar=gate[:, i, g - 1:g],
                                                                  in1=x_tile(b, i), op0=ALU.mult, op1=ALU.add)
                                st.then_inc(s_xo, 1)

                    @block.gpsimd
                    def _(pool):
                        ln_gpsimd(pool, s_var, s_rstd)
                clear(sems)
        def block_attention():
          HH = HB // 2
          NPR = HH // 2
          HR = P // 2
          MROW = 4 * HDB
          SROW = MROW + 2
          NV = HDB + 1
          PTW = T + (T - P) + (T - 2 * P) + (T - 3 * P)
          RING = 6
          NG = HH // 4
          AT = [0, T, 2 * T, T + (T - P)]
          with ExitStack() as ctx:
            WT = sb(ctx, "b_WT", [P, DC, 2, 4, P])
            WoT = sb(ctx, "b_WoT", [P, DC, D])
            table = sb(ctx, "b_table", [P, NT, 2 * HDB])
            tri = sb(ctx, "b_tri", [P, P], BF16)
            identb = sb(ctx, "b_identb", [P, P], BF16)
            avg = sb(ctx, "b_avg", [P, CPT])
            own = sb(ctx, "b_own", [P, P // HDB])
            onehot = sb(ctx, "b_onehot", [P, NT, NCH])
            past = sb(ctx, "b_past", [P, NT, NCH])
            notself = sb(ctx, "b_notself", [P, NT, NCH])
            bank = psum(ctx, "b_bank", [P, 8, 512])
            d_w = sem(ctx, "b_d_w")
            s_g0, s_g1, s_g2, s_g3, s_wT, s_z, s_c0 = (sem(ctx, "b_" + n) for n in ("g0", "g1", "g2", "g3", "wT", "z", "c0"))
            with ExitStack() as first:
                raw = sb(first, "b_raw", [P, 4, DC, D])
                rawg1 = sb(first, "b_rawg1", [HDB, D])
                rawg2 = sb(first, "b_rawg2", [P, DC, HDB])
                wcol = sb(first, "b_wcol", [P, 1])
                Wg2T = sb(first, "b_Wg2T", [HDB, D])
                with nc.Block() as block:
                    @block.sync
                    def _(sp):
                        for n, w in enumerate((Wq_b, Wk_b, Wv_b, Wo_b)):
                            sp.dma_start(raw[:, n, :, :], w.rearrange("(m p) d -> p m d", p=P)).then_inc(d_w, 16)
                        sp.dma_start(rawg1[:, :], Wg1).then_inc(d_w, 16)
                        sp.dma_start(rawg2[:, :, :], Wg2.rearrange("(m p) d -> p m d", p=P)).then_inc(d_w, 16)
                        sp.dma_start(table[:, :, :], rope.rearrange("(i p) e -> p i e", p=P)).then_inc(d_w, 16)
                        for r in range(P // HDB):
                            sp.dma_start(wcol[r * HDB:(r + 1) * HDB, :],
                                         o_norm.rearrange("(d o) -> d o", o=1)).then_inc(d_w, 16)
                        sp.wait_ge(d_w, 16 * (7 + P // HDB))

                    @block.tensor
                    def _(pe):
                        pe.wait_ge(d_w, 16 * (7 + P // HDB))
                        for n in range(4):
                            for m in range(DC):
                                for c in range(DC):
                                    pe.transpose(bank[:, n, c * D + m * P:c * D + m * P + P],
                                                 raw[:, n, m, c * P:(c + 1) * P], ident[:, :])
                        for m in range(DC):
                            t = pe.transpose(bank[0:HDB, 5, m * P:(m + 1) * P], rawg2[:, m, :], ident[:, :])
                        t.then_inc(s_wT, 1)
                        pe.wait_ge(s_c0, 1)
                        for c in range(DC):
                            mm = pe.matmul(bank[:, 6, c * D:(c + 1) * D], rawg1[:, c * P:(c + 1) * P], Wg2T[:, :],
                                           start=True, stop=True)
                        mm.then_inc(s_wT, 1)

                    @block.scalar
                    def _(act):
                        act.wait_ge(s_wT, 1)
                        act.activation(Wg2T[:, :], bank[0:HDB, 5, 0:D], ACT.Copy).then_inc(s_c0, 1)
                        for n in range(3):
                            act.activation(WT[:, :, :, n, :],
                                           bank[:, n, :].rearrange("p (c f o) -> p c f o", c=DC, f=2), ACT.Copy)
                        act.activation(WoT[:, :, :], bank[:, 3, :].rearrange("p (c o) -> p c o", c=DC),
                                       ACT.Copy, scale=wcol[:, 0:1])
                        act.wait_ge(s_wT, 2)
                        act.activation(WT[:, :, :, 3, :], bank[:, 6, :].rearrange("p (c f o) -> p c f o", c=DC, f=2),
                                       ACT.Copy)

                    @block.gpsimd
                    def _(pool):
                        pool.memset(tri[:, :], 0.0)
                        pool.memset(avg[:, :], 1.0 / CH)
                        pool.memset(own[:, :], 1.0)
                        pool.memset(onehot[:, :, :], 1.0)
                        pool.memset(past[:, :, :], 0.0)
                        pool.tensor_copy(identb[:, :], ident[:, :]).then_inc(s_g0, 1)
                        pool.wait_ge(s_g0, 1)

                        def keep(t, base, pattern, mult, fill):
                            return pool.affine_select(out=t, in_=t, compare_op=ALU.is_ge, fill=fill, base=base,
                                                      pattern=pattern, channel_multiplier=mult)

                        keep(tri[:, :], 0, [[1, P]], -1, NEG)
                        keep(avg[:, :], 0, [[-CH, CPT]], 1, 0.0)
                        keep(own[:, :], 0, [[-HDB, P // HDB]], 1, 0.0)
                        keep(onehot[:, :, :], 0, [[P, NT], [-CH, NCH]], 1, 0.0)
                        keep(past[:, :, :], -CH, [[P, NT], [-CH, NCH]], 1, NEG).then_inc(s_g1, 1)
                        pool.wait_ge(s_g1, 1)
                        keep(avg[:, :], CH - 1, [[CH, CPT]], -1, 0.0)
                        keep(own[:, :], HDB - 1, [[HDB, P // HDB]], -1, 0.0)
                        keep(onehot[:, :, :], CH - 1, [[-P, NT], [CH, NCH]], -1, 0.0).then_inc(s_g2, 1)

                    @block.vector
                    def _(dve):
                        dve.wait_ge(s_g2, 1)
                        dve.tensor_scalar(notself[:, :, :], onehot[:, :, :], -NEG, NEG, ALU.mult, ALU.add)

            QTs = sb(ctx, "b_QT", [P, 2, NPR, T], F32R)
            KTs = sb(ctx, "b_KT", [P, 2, HH, T], F32R)
            VAs = sb(ctx, "b_VA", [P, 2, NT, HH * NV + 32])
            rows = sb(ctx, "b_rows", [P, 2 * HH, HR], F32R)
            rot = sb(ctx, "b_rot", [P, 2 * HH, HDB])
            rotA = sb(ctx, "b_rotA", [P, 2 * HH, HDB])
            rotB = sb(ctx, "b_rotB", [P, 2 * HH, HDB])
            qT = sb(ctx, "b_qT", [P, P])
            kmean = sb(ctx, "b_kmean", [P, HH, NCH])
            gm = sb(ctx, "b_gm", [P, HH, NCH])
            mk = sb(ctx, "b_mk", [P, HH, NCH])
            top8 = sb(ctx, "b_top8", [P, HH, 8])
            find = sb(ctx, "b_find", [P, HH, 8])
            identr = sb(ctx, "b_identr", [P, P], F32R)
            negmax = sb(ctx, "b_negmax", [P, 2, NT, 2])
            mrow = sb(ctx, "b_mrow", [P, NT, 2, HR], F32R)
            PT = sb(ctx, "b_PT", [P, RING, PTW])
            OT = sb(ctx, "b_OT", [P, T])
            OgT = sb(ctx, "b_OgT", [P, T])
            rden = sb(ctx, "b_rden", [P, NT, 4])
            Os = sb(ctx, "b_O", [P, 2, NT, HH, HDB])
            sigs = sb(ctx, "b_sig", [P, 2, NT, P])
            gate = sb(ctx, "b_gate", [P, NT, P])
            sq = sb(ctx, "b_sq", [P, NT * HH, HDB])
            ms = sb(ctx, "b_ms", [P, NT * HH])
            rms = sb(ctx, "b_rms", [P, NT * HH])

            with nc.Block() as block:
                @block.gpsimd
                def _(pool):
                    pool.memset(KTs[HR:P, :, 0:HH:2, :].bitcast(F32), 0.0).then_inc(s_g3, 1)
                    pool.wait_ge(s_g3, 1)
                    pool.memset(rows[:, :, MROW:HR].bitcast(F32), 0.0).then_inc(s_g3, 1)
                    pool.memset(mrow[:, :, :, :].bitcast(F32), 0.0)
                    pool.wait_ge(s_g3, 2)
                    pool.memset(rows[:, 0:HH, MROW:MROW + 2].bitcast(F32), 1.0)

                @block.vector
                def _(dve):
                    dve.memset(KTs[0:HR, :, 1:HH:2, :].bitcast(F32), 0.0)
                    dve.memset(find[:, :, :], NONE)
                    dve.memset(kmean[:, :, :], 0.0)
                    dve.tensor_copy(identr[:, :], ident[:, :])
                    dve.memset(VAs[:, :, :, :], 0.0).then_inc(s_z, 1)
                    dve.wait_ge(s_z, 1)
                    for f in range(2):
                        dve.memset(VAs[:, f, :, 0:HH * NV].rearrange("p i (h e) -> p i h e", e=NV)[:, :, :, HDB:NV], 1.0)

            sems = [sem(ctx, "b_" + n) for n in
                    ("var", "rstd", "h", "hT", "hTs",
                     "qkv", "rp", "ga", "one", "rot", "lo", "cp", "qt", "km", "gt", "gm", "top", "sel", "tq", "tqs", "tk",
                     "s1", "mx", "mr", "mt", "mts", "s2", "e2", "pv", "ot", "ott", "on",
                     "sq", "mse", "rms", "og", "gT", "gTs", "fo", "xo", "gate", "dve")]
            (s_var, s_rstd, s_h, s_hT, s_hTs,
             s_qkv, s_rp, s_ga, s_one, s_rot, s_lo, s_cp, s_qt, s_km, s_gt, s_gm, s_top, s_sel, s_tq, s_tqs, s_tk,
             s_s1, s_mx, s_mr, s_mt, s_mts, s_s2, s_e2, s_pv, s_ot, s_ott, s_on,
             s_sq, s_mse, s_rms, s_og, s_gT, s_gTs, s_fo, s_xo, s_gate, s_dve) = sems

            T0, T1, T2, V0 = (bank[:, k, :] for k in (0, 1, 2, 7))
            rbank, sbank = (3, 4), (5, 6)
            FILL1 = [(0, (0, 1)), (1, (0, 1)), (2, (0,)), (2, (1,)), (3, (0,)), (3, (1,))]
            FILL2 = [(0, (0,), ((0, 0),)), (T, (0,), ((1, 0), (3, T - P))),
                     (0, (1,), ((0, 0),)), (T, (1,), ((1, 0), (3, T - P))),
                     (2 * T, (0, 1), ((2, 0),))]
            N1, N2 = len(FILL1), len(FILL2)
            USES1 = N1 + 1
            STEPS = 2 * NPR + 2
            """
            Steps of a phase. Score: step s makes three fills of the first pass of pair s // 2, and two or three
            of the second pass of the pair before. Make: tile i is projected at step 4 i, rotated at 4 i + 1,
            split at 4 i + 2, its chunks chosen at 4 i + 3, and its rows are turned at 4 i + 3 to 4 i + 5.
            Values of heads 4 g to 4 g + 3: from step 4 g + 6; the last four's in the phase after.
            Finish, of the unit before: squares, mean and root at steps 3 to 12, gate 13, transposes 14,
            projection and sum 17.
            """

            def made(s):
                return (s // 4, s % 4) if s < 4 * NT else (None, None)

            def turned(s):
                return s // 4 - 1 if s >= 4 and s % 4 < 2 else None

            class Part:

                def __init__(self, half, score, make, b_done, b_norm, qs, qm, qf, qn):
                    self.half, self.score, self.make, self.finish = half, score, make, b_done is not None
                    self.b_done, self.b_norm, self.norm = b_done, b_norm, b_norm is not None
                    self.qs, self.qm, self.qf, self.qn = qs, qm, qf, qn

                def group(self, g):
                    return self.qf + (NG - 1) * self.qs + (g + 1 if self.finish else g)

            def chain(*phases):
                parts, qs, qm, qf, qn = [], 0, 0, 0, 0
                for half, score, make, b_done, b_norm in phases:
                    parts.append(Part(half, score, make, b_done, b_norm, qs, qm, qf, qn))
                    qs, qm, qf, qn = qs + score, qm + make, qf + (b_done is not None), qn + (b_norm is not None)
                return parts

            def tensor_part(pe, w):
                half, other = w.half, 1 - w.half
                QT, KT = QTs[:, half], KTs[:, half]
                first_pair = w.qs * NPR
                Od = Os[:, other]

                def project(i):
                    t = w.qm * NT + i
                    if i > 1:
                        pe.wait_ge(s_gm, w.qm * (NT - 1) + i - 1)
                    elif i:
                        pe.wait_ge(s_km, t)
                    elif w.qm:
                        pe.wait_ge(s_gm, w.qm * (NT - 1))
                    if i == 0 and w.qf:
                        pe.wait_ge(s_gTs, w.qf)
                    if i == 0 and w.qn:
                        pe.wait_ge(s_hTs, DC)
                    for c in range(DC):
                        mm = pe.matmul(T0, hT[:, c, i * P:(i + 1) * P],
                                       WT[:, c, other, :, :].rearrange("p n o -> p (n o)"),
                                       start=(c == 0), stop=(c == DC - 1))
                    mm.then_inc(s_qkv, 1)

                def means(i):
                    t = w.qm * NT + i
                    pe.wait_ge(s_rot, t + 1)
                    pe.wait_ge(s_ga, t + 1)
                    flat = rot[:, :, :].rearrange("p h e -> p (h e)")
                    pe.transpose(T0[:, 0:P], flat[:, 0:P], ident[:, :])
                    pe.matmul(T0[:, P:P + CPT], flat[:, P:2 * P], avg[:, :], start=True, stop=True).then_inc(s_qt, 1)

                def gates(i):
                    pe.wait_ge(s_km, w.qm * NT + i + 1)
                    pe.matmul(T0[:, 0:HH * NCH], qT[:, :], kmean[:, :, :].rearrange("p h n -> p (h n)"),
                              start=True, stop=True).then_inc(s_gt, 1)

                def turn_rows(i, f):
                    t = w.qm * NT + i
                    if f == 0:
                        pe.wait_ge(s_cp, t + 1)
                        if t:
                            pe.wait_ge(s_tqs, 2 * t - 1)
                    elif f == 1:
                        if t:
                            pe.wait_ge(s_tqs, 2 * t)
                    else:
                        pe.wait_ge(s_sel, t + 1)
                        pe.wait_ge(s_tk, 2 * t + f - 1)
                    for k in range(4):
                        hd = 8 * f + 2 * k
                        mm = pe.matmul((T1 if f % 2 else T2)[:, k * P:(k + 1) * P],
                                       rows[:, hd:hd + 2, :].rearrange("p h r -> p (h r)"), identr[:, :],
                                       start=True, stop=True)
                    mm.then_inc(s_tq, 1)

                def first_pass(p, n):
                    pair = first_pair + p
                    i, heads = FILL1[n]
                    if n == 2:
                        if pair:
                            pe.wait_ge(s_mts, pair)
                    elif n or pair:
                        back = {0: -1, 1: 1, 3: 2, 4: 3, 5: 4}[n]
                        pe.wait_ge(s_mx, N1 * pair + back)
                    if n == 0 and p == 0 and w.qf:
                        pe.wait_ge(s_xo, NT * w.qf)
                    if n == 0 and p == 0 and w.qm:
                        pe.wait_ge(s_tqs, 2 * NT * w.qm)
                        pe.wait_ge(s_tk, 2 * NT * w.qm)
                    use = USES1 * pair + (n + 1 if n else 0)
                    for k, a in enumerate(heads):
                        wd = P * (i + 1)
                        o = bank[:, rbank[use % 2], k * wd:(k + 1) * wd]
                        pe.matmul(o, QT[:, p, i * P:wd], KT[:, 2 * p + a, 0:wd], start=True, stop=True,
                                  skip_group_check=True)
                        mm = pe.matmul(o[:, P * i:wd], tri[:, :], identb[:, :], start=False, stop=True,
                                       skip_group_check=True)
                    mm.then_inc(s_s1, 1)

                def turn_maximum(p):
                    pair = first_pair + p
                    pe.wait_ge(s_mr, pair + 1)
                    o = bank[:, rbank[(USES1 * (pair + 1) + 1) % 2], :]
                    for i in range(NT):
                        mm = pe.matmul(o[:, i * P:(i + 1) * P], mrow[:, i, :, :].rearrange("p a r -> p (a r)"),
                                       identr[:, :], start=True, stop=True)
                    mm.then_inc(s_mt, 1)

                def second_pass(p, n):
                    pair = first_pair + p
                    u = N2 * pair + n
                    _, heads, blocks = FILL2[n]
                    if n == 0:
                        pe.wait_ge(s_mts, pair + 1)
                    if u >= 2:
                        pe.wait_ge(s_e2, u - 1)
                    for k, a in enumerate(heads):
                        for j, c0 in blocks:
                            c0 += k * (T - 2 * P)
                            o = bank[:, sbank[u % 2], c0:c0 + T - P * j]
                            pe.matmul(o, KT[:, 2 * p + a, j * P:(j + 1) * P], QT[:, p, j * P:T],
                                      start=True, stop=True, skip_group_check=True)
                            mm = pe.matmul(o[:, 0:P], identb[:, :], tri[:, :], start=False, stop=True,
                                           skip_group_check=True)
                    mm.then_inc(s_s2, 1)

                def values(g):
                    n = w.group(g)
                    if g < 0:
                        if w.qs:
                            pe.wait_ge(s_e2, N2 * NPR * w.qs)
                    else:
                        pe.wait_ge(s_e2, N2 * (first_pair + 2 * (g + 1)))
                    if g == 0 and w.qm:
                        pe.wait_ge(s_ga, NT * w.qm)
                    if n:
                        pe.wait_ge(s_on, n)
                    hd0 = 4 * (NG - 1 if g < 0 else g)
                    VA = VAs[:, other if g < 0 else half]
                    for j in range(NT):
                        for s in range(4):
                            hd = hd0 + s
                            mm = pe.matmul(V0[32 * s:32 * s + 32, j * P:T], VA[:, j, hd * NV:hd * NV + 32],
                                           PT[:, hd % RING, AT[j]:AT[j] + T - P * j],
                                           start=(j == 0), stop=True, skip_group_check=True)
                    mm.then_inc(s_pv, 1)

                def turn(g):
                    pe.wait_ge(s_ot, w.group(g) + 1)
                    for i in range(NT):
                        t = pe.transpose(V0[:, i * P:(i + 1) * P], OT[:, i * P:(i + 1) * P], ident[:, :])
                    t.then_inc(s_ott, 1)

                def finish_turn():
                    if w.make:
                        pe.wait_ge(s_gm, (NT - 1) * (w.qm + 1))
                    pe.wait_ge(s_og, w.qf + 1)
                    for i in range(NT):
                        t = pe.transpose(T0[:, i * P:(i + 1) * P], Od[:, i].rearrange("p h e -> p (h e)"), ident[:, :])
                    t.then_inc(s_gT, 1)

                def finish_project():
                    pe.wait_ge(s_gTs, w.qf + 1)
                    if w.score:
                        pe.wait_ge(s_mx, N1 * (first_pair + NPR))
                        pe.wait_ge(s_mts, first_pair + NPR)
                    for i in range(NT):
                        pe.matmul(bank[:, rbank[i // 2], (i % 2) * D:(i % 2 + 1) * D], OgT[:, i * P:(i + 1) * P],
                                  WoT[:, other, :], start=True, stop=True).then_inc(s_fo, 1)

                def turn_h(m):
                    if m == 0:
                        pe.wait_ge(s_h, NT)
                        if w.finish:
                            pe.wait_ge(s_gTs, w.qf + 1)
                    else:
                        pe.wait_ge(s_hTs, m)
                    for i in range(NT):
                        t = pe.transpose(T0[:, i * P:(i + 1) * P], h[:, i, m * P:(m + 1) * P], ident[:, :])
                    t.then_inc(s_hT, 1)

                for s in range(STEPS):
                    p, b2 = s // 2, 3 * (s % 2)
                    i, part = made(s) if w.make else (None, None)
                    ti = turned(s) if w.make else None
                    if w.score and p < NPR:
                        first_pass(p, b2)
                    if w.finish and s == 0:
                        values(-1)
                    if w.finish and s == 1:
                        turn(-1)
                    if ti is not None:
                        turn_rows(ti, 1 if s % 4 == 0 else 2)
                    if part == 2:
                        means(i)
                    if part == 3 and i:
                        gates(i)
                    if w.score and s % 2 == 0 and s:
                        turn_maximum(p - 1)
                    if w.score and p < NPR:
                        first_pass(p, b2 + 1)
                    if w.score and p and s % 2:
                        second_pass(p - 1, 2)
                    if part == 0:
                        project(i)
                    if w.score and p < NPR:
                        first_pass(p, b2 + 2)
                    if part == 3:
                        turn_rows(i, 0)
                    if w.score and p:
                        second_pass(p - 1, 3 if s % 2 else 0)
                        second_pass(p - 1, 4 if s % 2 else 1)
                    if ti is not None and s % 4 == 1:
                        turn_rows(ti, 3)
                    if w.score and s >= 6:
                        if s % 4 == 2 and s // 4 <= NG - 1:
                            values(s // 4 - 1)
                        if s % 4 == 3 and s // 4 <= NG - 1:
                            turn(s // 4 - 1)
                    if w.finish and s == 16:
                        finish_turn()
                    if w.norm and s == 17:
                        turn_h(0)
                    if w.finish and s == 17:
                        finish_project()
                    if w.norm and s == 17:
                        turn_h(1)

            def scalar_part(act, w):
                half, other = w.half, 1 - w.half
                QT, QTn, KTn, VAn, sign = QTs[:, half], QTs[:, other], KTs[:, other], VAs[:, other], sigs[:, other]
                first_pair = w.qs * NPR

                def keep_values(i):
                    t = w.qm * NT + i
                    act.wait_ge(s_rp, t + 1)
                    if i == 0 and w.finish:
                        act.wait_ge(s_pv, w.group(-1) + 1)
                    if i == 0 and w.qs:
                        act.wait_ge(s_gate, NT * w.qs)
                    act.activation(VAn[:, i, 0:HH * NV].rearrange("p (h e) -> p h e", e=NV)[:, :, 0:HDB],
                                   T0[:, 2 * P:3 * P].rearrange("p (h e) -> p h e", e=HDB), ACT.Copy)
                    act.activation(sign[:, i, :], T0[:, 3 * P:4 * P], ACT.Exp, scale=-1.0).then_inc(s_ga, 1)

                def keep_keys(i, f):
                    act.wait_ge(s_tq, 4 * (w.qm * NT + i) + f + 1)
                    for a in range(2):
                        r = slice(HR * a, HR * (a + 1))
                        cp = act.activation(KTn[r, 8 * f + a:8 * f + 7 + a:2, i * P:(i + 1) * P],
                                            (T1 if f else T2)[r, :].rearrange("p (k t) -> p k t", k=4), ACT.Copy)
                    cp.then_inc(s_tk, 1)

                def keep_queries(i, f):
                    act.wait_ge(s_tq, 4 * (w.qm * NT + i) + f + 3)
                    act.activation(QTn[:, 4 * f:4 * f + 4, i * P:(i + 1) * P],
                                   (T1 if f else T2).rearrange("p (k t) -> p k t", k=4), ACT.Copy).then_inc(s_tqs, 1)

                def take(g):
                    n = w.group(g)
                    act.wait_ge(s_pv, n + 1)
                    if n:
                        act.wait_ge(s_ott, n)
                    act.activation(OT[:, :], V0, ACT.Copy).then_inc(s_ot, 1)

                def keep_maximum(p):
                    pair = first_pair + p
                    act.wait_ge(s_mt, pair + 1)
                    o = bank[:, rbank[(USES1 * (pair + 1) + 1) % 2], :]
                    for a in range(2):
                        r = slice(HR * a + MROW, HR * a + MROW + 2)
                        cp = act.activation(QT[r, p, :], o[r, :], ACT.Copy)
                    cp.then_inc(s_mts, 1)

                def exponentials(p, n):
                    pair = first_pair + p
                    u = N2 * pair + n
                    c0, heads, blocks = FILL2[n]
                    act.wait_ge(s_s2, u + 1)
                    if n == 0 and p >= RING // 2:
                        act.wait_ge(s_pv, w.group((p - RING // 2) // 2) + 1)
                    if n == 0 and p == 0 and w.finish:
                        act.wait_ge(s_pv, w.group(-1) + 1)
                    wd = sum(T - P * j for j, _ in blocks)
                    r0 = (2 * p) % RING + heads[0]
                    act.activation(PT[:, r0:r0 + len(heads), c0:c0 + wd],
                                   bank[:, sbank[u % 2], 0:wd * len(heads)].rearrange("p (h w) -> p h w", w=wd),
                                   ACT.Exp, scale=SCALE_B).then_inc(s_e2, 1)

                for s in range(STEPS):
                    p = s // 2 - 1
                    i, part = made(s) if w.make else (None, None)
                    ti = turned(s) if w.make else None
                    if ti is not None:
                        if s % 4 == 0:
                            keep_keys(ti, 0)
                        else:
                            keep_queries(ti, 0)
                    if part == 1:
                        keep_values(i)
                    if w.score and p >= 0:
                        if s % 2 == 0:
                            keep_maximum(p)
                        if s % 2:
                            exponentials(p, 2)
                    if ti is not None:
                        if s % 4 == 0:
                            keep_keys(ti, 1)
                        else:
                            keep_queries(ti, 1)
                    if w.score and p >= 0:
                        exponentials(p, 3 if s % 2 else 0)
                        exponentials(p, 4 if s % 2 else 1)
                    if w.finish and s == 0:
                        take(-1)
                    if w.score and s >= 6 and s % 4 == 2 and s // 4 <= NG - 1:
                        take(s // 4 - 1)
                    if w.finish and s == 16:
                        act.wait_ge(s_gT, w.qf + 1)
                        if w.qf:
                            act.wait_ge(s_fo, NT * w.qf)
                        act.activation(OgT[:, :], T0, ACT.Copy).then_inc(s_gTs, 1)
                    if w.norm and s == 17:
                        for m in range(DC):
                            act.wait_ge(s_hT, m + 1)
                            act.activation(hT[:, m, :], T0, ACT.Copy).then_inc(s_hTs, 1)

            def vector_part(dve, link, w):
                half, other = w.half, 1 - w.half
                KTn = KTs[:, other]
                first_pair = w.qs * NPR
                Od = Os[:, other]

                def rotate(i):
                    t = w.qm * NT + i
                    dve.wait_ge(s_qkv, t + 1)
                    if t:
                        dve.wait_ge(s_rot, t)
                    qk = T0[:, 0:2 * P].rearrange("p (h e) -> p h e", e=HDB)
                    mid = HDB // 2

                    def tab(lo, hi):
                        return table[:, i, None, lo:hi].broadcast_to([P, 2 * HH, hi - lo])

                    dve.tensor_tensor(rotA[:, :, :], qk, tab(0, HDB), ALU.mult)
                    dve.tensor_tensor(rotB[:, :, 0:mid], qk[:, :, mid:HDB], tab(HDB, HDB + mid), ALU.mult)
                    dve.tensor_tensor(rotB[:, :, mid:HDB], qk[:, :, 0:mid], tab(HDB + mid, 2 * HDB),
                                      ALU.mult).then_inc(s_rp, 1)

                def split(i):
                    t = w.qm * NT + i
                    dve.wait_ge(s_rot, t + 1)
                    if t:
                        dve.wait_ge(s_tq, 4 * t)
                    for lo, hi in ((0, HH), (HH, 2 * HH)):
                        sp = dve.tensor_copy(rows[:, HH - lo:2 * HH - lo, 0:HDB], rot[:, lo:hi, :])
                    link(sp)
                    for lo, hi in ((0, HH), (HH, 2 * HH)):
                        sp = dve.tensor_tensor(rows[:, HH - lo:2 * HH - lo, 3 * HDB:4 * HDB], rot[:, lo:hi, :],
                                               rows[:, HH - lo:2 * HH - lo, 0:HDB], ALU.subtract)
                    sp.then_inc(s_lo, 1)

                def keep_means(i):
                    t = w.qm * NT + i
                    dve.wait_ge(s_qt, t + 1)
                    if i > 1:
                        dve.wait_ge(s_gt, w.qm * (NT - 1) + i - 1)
                    elif i == 0 and w.qm:
                        dve.wait_ge(s_gt, w.qm * (NT - 1))
                    dve.tensor_copy(qT[:, :], T0[:, 0:P])
                    dve.tensor_tensor(kmean[:, :, i * CPT:(i + 1) * CPT],
                                      T0[:, None, P:P + CPT].broadcast_to([P, HH, CPT]),
                                      own[:, :, None].broadcast_to([P, HH, CPT]), ALU.mult).then_inc(s_km, 1)

                def greatest(i):
                    n = w.qm * (NT - 1) + i
                    dve.wait_ge(s_gt, n)
                    dve.tensor_tensor(gm[:, :, :], T0[:, 0:HH * NCH].rearrange("p (h n) -> p h n", n=NCH),
                                      past[:, i, None, :].broadcast_to([P, HH, NCH]), ALU.add).then_inc(s_gm, 1)
                    dve.wait_ge(s_gm, n)
                    for e in range(HH):
                        mx = dve.max(top8[:, e, :], gm[:, e, :])
                    mx.then_inc(s_top, 1)

                def choose(i):
                    if i == 0:
                        dve.memset(rows[:, HH:2 * HH, SROW:SROW + NCH].bitcast(F32), 0.0).then_inc(s_sel, 1)
                        return
                    dve.wait_ge(s_top, w.qm * (NT - 1) + i)
                    link(dve.tensor_copy(find[:, :, 0:PAST], top8[:, :, 0:PAST]))
                    for e in range(HH):
                        mr = dve.match_replace(mk[:, e, :], find[:, e, :], gm[:, e, :], MARK)
                    link(mr)
                    dve.scalar_tensor_tensor(out=rows[:, HH:2 * HH, SROW:SROW + NCH], in0=mk[:, :, :],
                                             scalar=MARK,
                                             in1=notself[:, i, None, :].broadcast_to([P, HH, NCH]),
                                             op0=ALU.not_equal, op1=ALU.mult).then_inc(s_sel, 1)

                def maximum(p, n):
                    i, heads = FILL1[n]
                    u = N1 * (first_pair + p) + n
                    wd = P * (i + 1)
                    use = USES1 * (first_pair + p) + (n + 1 if n else 0)
                    dve.wait_ge(s_s1, u + 1)
                    if n == 0 and first_pair + p >= 2:
                        dve.wait_ge(s_mr, first_pair + p - 1)
                    dve.tensor_reduce(negmax[:, p % 2, i, heads[0]:heads[0] + len(heads)],
                                      bank[:, rbank[use % 2], 0:wd * len(heads)].rearrange("p (h w) -> p h w", w=wd),
                                      AX_X, ALU.max, negate=True).then_inc(s_mx, 1)

                def split_maximum(p):
                    pair = first_pair + p
                    dve.wait_ge(s_mx, N1 * (pair + 1))
                    if pair:
                        dve.wait_ge(s_mt, pair)
                    nm = negmax[:, p % 2]
                    link(dve.tensor_copy(mrow[:, :, :, MROW], nm))
                    dve.tensor_tensor(mrow[:, :, :, MROW + 1], nm, mrow[:, :, :, MROW],
                                      ALU.subtract).then_inc(s_mr, 1)

                def normal(g):
                    O = Od if g < 0 else Os[:, half]
                    h0 = 4 * (NG - 1 if g < 0 else g)
                    dve.wait_ge(s_ott, w.group(g) + 1)
                    if g == 0 and w.qf:
                        dve.wait_ge(s_gT, w.qf)
                    o = V0.rearrange("p (i s e) -> p i s e", i=NT, s=4)
                    link(dve.reciprocal(rden[:, :, :], o[:, :, :, HDB]))
                    dve.tensor_tensor(O[:, :, h0:h0 + 4, :], o[:, :, :, 0:HDB],
                                      rden[:, :, :, None].broadcast_to([P, NT, 4, HDB]), ALU.mult).then_inc(s_on, 1)

                for s in range(STEPS):
                    p, b2 = s // 2, 3 * (s % 2)
                    i, part = made(s) if w.make else (None, None)
                    ti = turned(s) if w.make else None
                    if w.score and p < NPR:
                        maximum(p, b2)
                    if ti is not None and s % 4 == 0:
                        choose(ti)
                    if part == 1:
                        rotate(i)
                    if part == 2:
                        split(i)
                    if part == 3 and i:
                        greatest(i)
                    if w.score and p < NPR:
                        maximum(p, b2 + 1)
                    if part == 2:
                        keep_means(i)
                    if w.finish and s == 2:
                        normal(-1)
                    if w.finish and s == 4:
                        dve.wait_ge(s_sq, w.qf + 1)
                        link(dve.tensor_reduce(ms[:, :], sq[:, :, :], AX_X, ALU.add))
                        dve.tensor_scalar(ms[:, :], ms[:, :], 1.0 / HDB, RMS_EPS, ALU.mult, ALU.add).then_inc(s_mse, 1)
                    if w.finish and s == 13:
                        dve.wait_ge(s_rms, NT * (w.qf + 1))
                        o = Od.rearrange("p i h e -> p (i h) e")
                        link(dve.tensor_tensor(o, o, rms[:, :, None].broadcast_to([P, NT * HH, HDB]), ALU.mult))
                        o = Od.rearrange("p i h e -> p (i h e)")
                        dve.tensor_tensor(o, o, gate[:, :, :].rearrange("p i c -> p (i c)"), ALU.mult).then_inc(s_og, 1)
                    if w.score and p < NPR:
                        maximum(p, b2 + 2)
                        if s % 2:
                            split_maximum(p)
                    if w.score and s == 16:
                        if w.qm:
                            dve.wait_ge(s_one, NT * w.qm)
                        if w.finish:
                            dve.wait_ge(s_og, w.qf + 1)
                        for k in range(NT):
                            dve.reciprocal(gate[:, k, :], sigs[:, half, k, :]).then_inc(s_gate, 1)
                    if w.score and s >= 6:
                        if s % 4 == 0 and s // 4 - 2 <= NG - 2 and s >= 8:
                            normal(s // 4 - 2)
                    if w.norm and s == 1:
                        for k in range(NT):
                            st = dve.bn_stats(ln_stats[:, k, :], x_tile(w.b_norm, k))
                        link(st)
                        for k in range(NT):
                            st = dve.bn_aggr(ln_mv[:, k, :], ln_stats[:, k, :])
                        link(st)
                        dve.tensor_scalar(ln_var[:, :], ln_mv[:, :, 1], LN_EPS, None, ALU.add).then_inc(s_var, 1)
                    if w.norm and s == 4:
                        dve.wait_ge(s_rstd, 1)
                        for k in range(NT):
                            dve.tensor_scalar(h[:, k, :], x_tile(w.b_norm, k), ln_mv[:, k, 0:1], ln_rstd[:, k:k + 1],
                                              ALU.subtract, ALU.mult).then_inc(s_h, 1)
                    if w.finish and s == 17:
                        dve.wait_ge(s_fo, NT * (w.qf + 1))
                        for k in range(NT):
                            dve.tensor_tensor(x_tile(w.b_done, k), bank[:, rbank[k // 2], (k % 2) * D:(k % 2 + 1) * D],
                                              x_tile(w.b_done, k), ALU.add).then_inc(s_xo, 1)

            def gpsimd_part(pool, w):
                half, other = w.half, 1 - w.half
                sign = sigs[:, other]
                Od = Os[:, other]

                for s in range(STEPS):
                    i, part = made(s) if w.make else (None, None)
                    if part == 1:
                        t = w.qm * NT + i
                        pool.wait_ge(s_rp, t + 1)
                        if t:
                            pool.wait_ge(s_lo, t)
                            pool.wait_ge(s_qt, t)
                        pool.tensor_tensor(rot[:, :, :], rotA[:, :, :], rotB[:, :, :], ALU.add).then_inc(s_rot, 1)
                        if t:
                            pool.wait_ge(s_tq, 4 * t - 2)
                        pool.tensor_copy(rows[:, 0:HH, SROW:SROW + NCH],
                                         onehot[:, i, None, :].broadcast_to([P, HH, NCH]))
                    if part == 2:
                        t = w.qm * NT + i
                        pool.wait_ge(s_lo, t + 1)
                        lo, hi = slice(3 * HDB, 4 * HDB), slice(0, HDB)
                        pool.tensor_copy(rows[:, 0:HH, HDB:2 * HDB], rows[:, 0:HH, lo])
                        pool.tensor_copy(rows[:, 0:HH, 2 * HDB:3 * HDB], rows[:, 0:HH, hi])
                        pool.tensor_copy(rows[:, HH:2 * HH, HDB:2 * HDB], rows[:, HH:2 * HH, hi])
                        pool.tensor_copy(rows[:, HH:2 * HH, 2 * HDB:3 * HDB], rows[:, HH:2 * HH, lo]).then_inc(s_cp, 1)
                    if part == 3:
                        pool.wait_ge(s_ga, w.qm * NT + i + 1)
                        pool.tensor_scalar(sign[:, i, :], sign[:, i, :], 1.0, None, ALU.add).then_inc(s_one, 1)
                    if w.finish and s == 3:
                        pool.wait_ge(s_on, w.group(-1) + 1)
                        o = Od.rearrange("p i h e -> p (i h) e")
                        pool.tensor_tensor(sq[:, :, :], o, o, ALU.mult).then_inc(s_sq, 1)
                    if w.finish and s in (7, 8, 11, 12):
                        k = (7, 8, 11, 12).index(s)
                        if k == 0:
                            pool.wait_ge(s_mse, w.qf + 1)
                        pool.tensor_tensor(rms[:, k * HH:(k + 1) * HH], ms[:, k * HH:(k + 1) * HH],
                                           minus_half[:, 0:1].broadcast_to([P, HH]), ALU.pow).then_inc(s_rms, 1)
                    if w.norm and s == 2:
                        ln_gpsimd(pool, s_var, s_rstd)

            def stretch(*phases):
                parts = chain(*phases)
                with nc.Block() as block:
                    @block.tensor
                    def _(pe):
                        for w in parts:
                            tensor_part(pe, w)

                    @block.scalar
                    def _(act):
                        for w in parts:
                            scalar_part(act, w)

                    @block.vector
                    def _(dve):
                        link = Links(dve, s_dve)
                        for w in parts:
                            vector_part(dve, link, w)

                    @block.gpsimd
                    def _(pool):
                        for w in parts:
                            gpsimd_part(pool, w)
                clear(sems)

            with nc.Block() as block:
                @block.tensor
                def _(pe):
                    ln_turn(pe, [T0, T2], s_h, s_hT)

                @block.scalar
                def _(act):
                    ln_keep(act, [T0, T2], s_hT, s_hTs)

                @block.vector
                def _(dve):
                    ln_vector(dve, Links(dve, s_dve), 0, s_var, s_rstd, s_h)

                @block.gpsimd
                def _(pool):
                    ln_gpsimd(pool, s_var, s_rstd)
            clear(sems)
            stretch((1, False, True, None, None),
                    (0, True, True, None, 1),
                    (1, True, True, 0, None))
            with nc.Fori(1, B - 1) as b:
                stretch((0, True, True, b - 1, b + 1),
                        (1, True, True, b, None))
            stretch((0, True, True, B - 2, None),
                    (1, True, False, B - 1, None),
                    (0, False, False, B - 1, None))

        latent_attention()
        experts(0)
        block_attention()
        experts(1)

        s_out = sem(whole, "s_out")
        with nc.Block() as block:
            @block.sync
            def _(sp):
                for b in range(B):
                    sp.dma_start(out[b].rearrange("(i p) d -> p i d", p=P),
                                 x[:, b * NT * D:(b + 1) * NT * D].rearrange("p (i d) -> p i d", i=NT)).then_inc(s_out, 16)
                sp.wait_ge(s_out, 16 * B)


_INS = ["L0_attn_a_hidden_states", "L0_attn_a_Wq", "L0_attn_a_bq", "L0_attn_a_Wk", "L0_attn_a_bk", "L0_attn_a_Wv",
        "L0_attn_a_bv", "L0_attn_a_Wo", "L0_attn_a_bo", "L0_attn_a_latent_keys", "L0_attn_b_Wq", "L0_attn_b_Wk",
        "L0_attn_b_Wv", "L0_attn_b_Wo", "L0_attn_b_Wg1", "L0_attn_b_Wg2", "L0_attn_b_o_norm_weight",
        "L0_ffn_Wsh_up", "L0_ffn_Wsh_down", "L0_ffn_Wrt_up", "L0_ffn_Wrt_down", "L0_ffn_W_router"]


def rope_table():
    pos = np.arange(T, dtype=np.float32)
    inv_freq = (1.0 / np.float32(THETA) ** (np.arange(0, HDB, 2, dtype=np.float32) / np.float32(HDB))).astype(np.float32)
    ang = (pos[:, None] * inv_freq[None, :]).astype(np.float32)
    c, s = np.cos(ang), np.sin(ang)
    return np.concatenate([c, c, -s, s], axis=1).astype(np.float32)


def kernel(**inputs):
    import numpy as _np
    import concourse.bacc as _bacc
    from concourse import mybir as _mybir
    from concourse.bass_utils import run_bass_kernel_spmd as _run

    nc = _bacc.Bacc("TRN2", target_bir_lowering=False, num_devices=1)
    arrays, args = {}, []
    for name in _INS:
        a = _np.ascontiguousarray(inputs[name])
        arrays[f"in_{name}_dram"] = a
        args.append(nc.dram_tensor(f"in_{name}_dram", a.shape, _mybir.dt.from_np(a.dtype), kind="ExternalInput").ap())
    table = rope_table()
    arrays["rope_dram"] = table
    args.append(nc.dram_tensor("rope_dram", table.shape, _mybir.dt.float32, kind="ExternalInput").ap())
    args.append(nc.dram_tensor("out_0_dram", (B, T, D), _mybir.dt.float32, kind="ExternalOutput").ap())
    program(nc, *args)
    r = _run(nc, [arrays], core_ids=[0])
    return r.results[0]["out_0_dram"]
```

```python
from contextlib import ExitStack

import numpy as np

import concourse.bass as bass
from concourse import mybir

ALU = mybir.AluOpType
ACT = mybir.ActivationFunctionType
AX_X = mybir.AxisListType.X
F32 = mybir.dt.float32
F32R = mybir.dt.float32r
BF16 = mybir.dt.bfloat16

P = 128
B, T, D = 4, 512, 256
NT = T // P
DC = D // P
LN_EPS = 1e-5

HA, HDA = 16, 16
L = 64
TOP_A = 4
HPC = P // HDA
NPAIR_A = HA // 2
SCALE_A = 1.0 / float(np.sqrt(HDA))

HB, HDB = 32, 8
CH = 32
NCH = T // CH
CPT = P // CH
PAST = 3
THETA = 10000.0
RMS_EPS = 1e-6
SCALE_B = 1.0 / float(np.sqrt(HDB))
NEG = -1e30

E_SH, E_RT = 2, 16
E_ALL = E_SH + E_RT
DF = 128

MARK = 3.0e38
NONE = 3.3e38


class Links:

    def __init__(self, eng, sem):
        self.eng, self.sem, self.n, self.turned = eng, sem, 0, 0

    def turn(self, turned):
        self.turned = turned

    def __call__(self, ins):
        self.n += 1
        ins.then_inc(self.sem, 1)
        self.eng.wait_ge(self.sem, self.turned + self.n)


def program(nc, x_in, Wq_a, bq_a, Wk_a, bk_a, Wv_a, bv_a, Wo_a, bo_a, latent,
            Wq_b, Wk_b, Wv_b, Wo_b, Wg1, Wg2, o_norm, Wsh_up, Wsh_down, Wrt_up, Wrt_down, W_router,
            rope, out):
    with ExitStack() as whole:
        def sb(ctx, name, shape, dt=F32):
            return ctx.enter_context(nc.sbuf_tensor(name, shape, dt))

        def psum(ctx, name, shape, dt=F32):
            return ctx.enter_context(nc.psum_tensor(name, shape, dt))

        def sem(ctx, name):
            return ctx.enter_context(nc.semaphore(name))

        def clear(sems):
            nums = sorted(s.num for s in sems)
            assert nums == list(range(nums[0], nums[0] + len(nums)))
            nc.gpsimd.sem_clear(range(nums[0], nums[-1] + 1))
            nc.all_engine_barrier()

        x = sb(whole, "x", [P, B * NT * D])
        ident = sb(whole, "ident", [P, P])
        ones_row = sb(whole, "ones_row", [1, P])
        minus_half = sb(whole, "minus_half", [P, 1])
        ln_stats = sb(whole, "ln_stats", [P, NT, 6])
        ln_mv = sb(whole, "ln_mv", [P, NT, 2])
        ln_var = sb(whole, "ln_var", [P, NT])
        ln_rstd = sb(whole, "ln_rstd", [P, NT])
        h = sb(whole, "h", [P, NT, D])
        hT = sb(whole, "hT", [P, DC, T])

        s_setup = sem(whole, "s_setup")
        s_setup_dma = sem(whole, "s_setup_dma")

        with nc.Block() as block:
            @block.sync
            def _(sp):
                for b in range(B):
                    sp.dma_start(x[:, b * NT * D:(b + 1) * NT * D].rearrange("p (i d) -> p i d", i=NT),
                                 x_in[b].rearrange("(i p) d -> p i d", p=P)).then_inc(s_setup_dma, 16)
                sp.wait_ge(s_setup_dma, 16 * B)

            @block.gpsimd
            def _(pool):
                pool.memset(ident[:, :], 0.0).then_inc(s_setup, 1)
                pool.memset(ones_row[:, :], 1.0)
                pool.memset(minus_half[:, :], -0.5)
                pool.wait_ge(s_setup, 1)
                pool.affine_select(out=ident[:, :], in_=ident[:, :], compare_op=ALU.not_equal, fill=1.0,
                                   base=0, pattern=[[-1, P]], channel_multiplier=1)

        def x_tile(b, i):
            return x[:, bass.ds(b * (NT * D) + i * D, D)]

        def ln_spread(dve, link, b, s_var):
            for i in range(NT):
                st = dve.bn_stats(ln_stats[:, i, :], x_tile(b, i))
            link(st)
            for i in range(NT):
                st = dve.bn_aggr(ln_mv[:, i, :], ln_stats[:, i, :])
            link(st)
            dve.tensor_scalar(ln_var[:, :], ln_mv[:, :, 1], LN_EPS, None, ALU.add).then_inc(s_var, 1)

        def ln_apply(dve, b, s_h):
            for i in range(NT):
                dve.tensor_scalar(h[:, i, :], x_tile(b, i), ln_mv[:, i, 0:1], ln_rstd[:, i:i + 1],
                                  ALU.subtract, ALU.mult).then_inc(s_h, 1)

        def ln_vector(dve, link, b, s_var, s_rstd, s_h):
            ln_spread(dve, link, b, s_var)
            dve.wait_ge(s_rstd, 1)
            ln_apply(dve, b, s_h)

        def ln_gpsimd(pool, s_var, s_rstd):
            pool.wait_ge(s_var, 1)
            pool.tensor_tensor(ln_rstd[:, :], ln_var[:, :], minus_half[:, 0:1].broadcast_to([P, NT]), ALU.pow).then_inc(s_rstd, 1)

        def ln_turn(pe, banks, s_h, s_hT):
            for i in range(NT):
                pe.wait_ge(s_h, i + 1)
                for m in range(DC):
                    t = pe.transpose(banks[m][:, i * P:(i + 1) * P], h[:, i, m * P:(m + 1) * P], ident[:, :])
            t.then_inc(s_hT, 1)

        def ln_keep(act, banks, s_hT, s_hTs):
            act.wait_ge(s_hT, 1)
            for m in range(DC):
                act.activation(hT[:, m, :], banks[m][:, :], ACT.Copy).then_inc(s_hTs, 1)

        def latent_attention():
          with ExitStack() as ctx:
            WqT = sb(ctx, "a_WqT", [P, DC, D])
            WvT = sb(ctx, "a_WvT", [P, DC, D])
            WoT = sb(ctx, "a_WoT", [P, DC, D])
            bq = sb(ctx, "a_bq", [P, DC])
            bv = sb(ctx, "a_bv", [P, DC])
            bo = sb(ctx, "a_bo", [1, D])
            latT = sb(ctx, "a_latT", [P, DC, HPC, L])
            latP = sb(ctx, "a_latP", [P, NPAIR_A, 2 * HDA])
            lat2 = sb(ctx, "a_lat2", [P, D])
            QT = sb(ctx, "a_QT", [P, DC, T])
            logits = sb(ctx, "a_logits", [P, NT, HA, L])
            marked = sb(ctx, "a_marked", [P, 2, HA, L])
            shifted = sb(ctx, "a_shifted", [P, 2, HA, L])
            probs = sb(ctx, "a_probs", [P, 2, HA, L])
            probsT = sb(ctx, "a_probsT", [P, NPAIR_A, T])
            top8 = sb(ctx, "a_top8", [P, NT, HA, 8])
            find = sb(ctx, "a_find", [P, 2, HA, 8])
            topd = sb(ctx, "a_topd", [P, NT, HA, TOP_A])
            tope = sb(ctx, "a_tope", [P, NT, HA, TOP_A])
            total = sb(ctx, "a_total", [P, NT, HA])
            inv = sb(ctx, "a_inv", [P, NT, HA])
            AOT = sb(ctx, "a_AOT", [P, DC, T])
            raw = sb(ctx, "a_raw", [P, 3, DC, D])
            bk = [psum(ctx, f"a_bank{i}", [P, 512]) for i in range(8)]
            pT, pQ, pL, pP = bk[0:2], bk[2:4], bk[4:6], bk[6:8]
            d_w = sem(ctx, "a_d_w")
            s_zero, s_wT, s_ws, s_lT, s_ls, s_sel = (sem(ctx, "a_" + n) for n in
                                                     ("zero", "wT", "ws", "lT", "ls", "sel"))

            with nc.Block() as block:
                @block.sync
                def _(sp):
                    for n, w in enumerate((Wq_a, Wv_a, Wo_a)):
                        sp.dma_start(raw[:, n, :, :], w.rearrange("(m p) d -> p m d", p=P)).then_inc(d_w, 16)
                    sp.dma_start(lat2[0:L, :], latent).then_inc(d_w, 16)
                    sp.dma_start(lat2[L:2 * L, :], latent).then_inc(d_w, 16)
                    sp.dma_start(bq[:, :], bq_a.rearrange("(m p) -> p m", p=P), allow_slow_non_contiguous=True).then_inc(d_w, 16)
                    sp.dma_start(bv[:, :], bv_a.rearrange("(m p) -> p m", p=P), allow_slow_non_contiguous=True).then_inc(d_w, 16)
                    sp.dma_start(bo[:, :], bo_a.rearrange("(o d) -> o d", o=1)).then_inc(d_w, 16)
                    sp.wait_ge(d_w, 16 * 8)

                @block.tensor
                def _(pe):
                    pe.wait_ge(d_w, 16 * 8)
                    for n in range(3):
                        for m in range(DC):
                            for c in range(DC):
                                t = pe.transpose(bk[n][:, c * D + m * P:c * D + m * P + P],
                                                 raw[:, n, m, c * P:(c + 1) * P], ident[:, :])
                        t.then_inc(s_wT, 1)
                    for m in range(DC):
                        t = pe.transpose(bk[3][:, m * L:(m + 1) * L], lat2[0:L, m * P:(m + 1) * P],
                                         ident[0:L, 0:L])
                    t.then_inc(s_lT, 1)

                @block.scalar
                def _(act):
                    for n, w in enumerate((WqT, WvT, WoT)):
                        act.wait_ge(s_wT, n + 1)
                        act.activation(w[:, :, :], bk[n][:, :].rearrange("p (c o) -> p c o", c=DC), ACT.Copy)

                @block.vector
                def _(dve):
                    dve.memset(find[:, :, :, :], NONE)
                    dve.memset(latP[:, :, :], 0.0).then_inc(s_zero, 1)
                    dve.wait_ge(s_zero, 1)
                    dve.wait_ge(d_w, 16 * 8)
                    pairs = lat2[:, :].rearrange("p (c a e) -> p c a e", a=2, e=HDA)
                    for a in range(2):
                        dve.tensor_copy(latP[a * L:(a + 1) * L, :, a * HDA:(a + 1) * HDA],
                                        pairs[a * L:(a + 1) * L, :, a, :])
                    dve.wait_ge(s_lT, 1)
                    for m in range(DC):
                        for e in range(HPC):
                            t = dve.tensor_copy(latT[:, m, e, :], bk[3][:, m * L:(m + 1) * L])
                    t.then_inc(s_ls, 1)

                @block.gpsimd
                def _(pool):
                    pool.wait_ge(s_ls, 1)
                    v = latT[:, :, :, :]
                    pool.affine_select(out=v, in_=v, compare_op=ALU.is_ge, fill=0.0, base=0,
                                       pattern=[[0, DC], [-HDA, HPC], [0, L]], channel_multiplier=1).then_inc(s_sel, 1)
                    pool.wait_ge(s_sel, 1)
                    pool.affine_select(out=v, in_=v, compare_op=ALU.is_ge, fill=0.0, base=HDA - 1,
                                       pattern=[[0, DC], [HDA, HPC], [0, L]], channel_multiplier=-1).then_inc(s_sel, 1)

            sems = [sem(ctx, "a_" + n) for n in
                    ("var", "rstd", "h", "hT", "hTs", "q", "qs", "l", "lsb", "mx", "d4", "sh", "ex", "ex4",
                     "w", "inv", "pr", "pT", "pTs", "ao", "aos", "o", "xo", "dve")]
            (s_var, s_rstd, s_h, s_hT, s_hTs, s_q, s_qs, s_l, s_lsb, s_mx, s_d4, s_sh, s_ex, s_ex4,
             s_w, s_inv, s_pr, s_pT, s_pTs, s_ao, s_aos, s_o, s_xo, s_dve) = sems

            def open_tensor(pe):
                ln_turn(pe, pT, s_h, s_hT)
                pe.wait_ge(s_hTs, DC)
                for m in range(DC):
                    for c in range(DC):
                        mm = pe.matmul(pL[m][:, :], WqT[:, c, m * P:(m + 1) * P], hT[:, c, :],
                                       start=(c == 0), stop=(c == DC - 1))
                    mm.then_inc(s_q, 1)

            def open_scalar(act):
                ln_keep(act, pT, s_hT, s_hTs)
                for m in range(DC):
                    act.wait_ge(s_q, m + 1)
                    act.activation(QT[:, m, :], pL[m][:, :], ACT.Identity, bias=bq[:, m:m + 1]).then_inc(s_qs, 1)

            def attend(b, ahead):
                with nc.Block() as block:
                    @block.tensor
                    def _(pe):
                        for i in range(NT):
                            if i:
                                pe.wait_ge(s_lsb, i)
                            for m in range(DC):
                                mm = pe.matmul(pL[m][:, :], QT[:, m, i * P:(i + 1) * P],
                                               latT[:, m, :, :].rearrange("p e l -> p (e l)"), start=True, stop=True)
                            mm.then_inc(s_l, 1)
                        for m in range(DC):
                            for c in range(DC):
                                pe.matmul(pQ[m][:, :], WvT[:, c, m * P:(m + 1) * P], hT[:, c, :],
                                          start=(c == 0), stop=False, skip_group_check=True)
                        if ahead:
                            pe.wait_ge(s_lsb, NT)
                            open_tensor(pe)
                        def project(i):
                            pe.wait_ge(s_aos, i + 1)
                            if i >= 2:
                                pe.wait_ge(s_xo, i - 1)
                            o = pT[i % 2][:, 0:D]
                            pe.matmul(o, ones_row[:, :], bo[:, :], start=True, stop=False)
                            for c in range(DC):
                                mm = pe.matmul(o, AOT[:, c, i * P:(i + 1) * P], WoT[:, c, :],
                                               start=False, stop=(c == DC - 1))
                            mm.then_inc(s_o, 1)

                        for i in range(NT):
                            pe.wait_ge(s_pr, i + 1)
                            if i:
                                pe.wait_ge(s_pTs, i)
                            for c in range(NPAIR_A):
                                t = pe.transpose(pP[c // 4][:, (c % 4) * P:(c % 4 + 1) * P],
                                                 probs[:, i % 2, 2 * c:2 * c + 2, :].rearrange("p e l -> p (e l)"),
                                                 ident[:, :])
                            t.then_inc(s_pT, 1)
                            if i:
                                project(i - 1)
                            pe.wait_ge(s_pTs, i + 1)
                            for m in range(DC):
                                for q in range(4):
                                    mm = pe.matmul(pQ[m][32 * q:32 * q + 32, i * P:(i + 1) * P], latP[:, 4 * m + q, :],
                                                   probsT[:, 4 * m + q, i * P:(i + 1) * P], start=False, stop=True,
                                                   skip_group_check=True)
                            mm.then_inc(s_ao, 1)
                        project(NT - 1)

                    @block.scalar
                    def _(act):
                        for i in range(NT):
                            act.wait_ge(s_l, i + 1)
                            for m in range(DC):
                                cp = act.activation(logits[:, i, HPC * m:HPC * (m + 1), :].rearrange("p e l -> p (e l)"),
                                                    pL[m][:, :], ACT.Copy, scale=SCALE_A)
                            cp.then_inc(s_lsb, 1)

                        def summed(i):
                            act.wait_ge(s_ao, i + 1)
                            for m in range(DC):
                                cp = act.activation(AOT[:, m, i * P:(i + 1) * P], pQ[m][:, i * P:(i + 1) * P],
                                                    ACT.Identity, bias=bv[:, m:m + 1])
                            cp.then_inc(s_aos, 1)

                        def turned(i):
                            act.wait_ge(s_pT, i + 1)
                            for c in range(2):
                                cp = act.activation(probsT[:, 4 * c:4 * c + 4, i * P:(i + 1) * P],
                                                    pP[c][:, :].rearrange("p (c t) -> p c t", c=4), ACT.Copy)
                            cp.then_inc(s_pTs, 1)

                        for i in range(NT):
                            act.wait_ge(s_sh, i + 1)
                            act.activation(shifted[:, i % 2], shifted[:, i % 2], ACT.Exp).then_inc(s_ex, 1)
                            act.wait_ge(s_d4, i + 1)
                            act.activation(tope[:, i], topd[:, i], ACT.Exp).then_inc(s_ex4, 1)
                            if i == 0 and ahead:
                                open_scalar(act)
                            if i >= 2:
                                summed(i - 2)
                            if i:
                                turned(i - 1)
                        summed(NT - 2)
                        turned(NT - 1)
                        summed(NT - 1)

                    @block.vector
                    def _(dve):
                        link = Links(dve, s_dve)

                        def weights(i):
                            dve.wait_ge(s_ex, i + 1)
                            if i >= 2:
                                dve.wait_ge(s_pT, i - 1)
                            dve.scalar_tensor_tensor(out=probs[:, i % 2], in0=marked[:, i % 2], scalar=MARK,
                                                     in1=shifted[:, i % 2], op0=ALU.is_equal, op1=ALU.mult).then_inc(s_w, 1)
                            dve.wait_ge(s_ex4, i + 1)
                            link(dve.tensor_reduce(total[:, i], tope[:, i], AX_X, ALU.add))
                            dve.reciprocal(inv[:, i], total[:, i]).then_inc(s_inv, 1)

                        if ahead:
                            ln_spread(dve, link, b + 1, s_var)
                        for i in range(NT):
                            dve.wait_ge(s_lsb, i + 1)
                            for e in range(HA):
                                mx = dve.max(top8[:, i, e, :], logits[:, i, e, :])
                            link(mx)
                            dve.tensor_tensor(topd[:, i], top8[:, i, :, 0:TOP_A],
                                              top8[:, i, :, 0:1].broadcast_to([P, HA, TOP_A]), ALU.subtract).then_inc(s_d4, 1)
                            link(dve.tensor_copy(find[:, i % 2, :, 0:TOP_A], top8[:, i, :, 0:TOP_A]))
                            for e in range(HA):
                                mr = dve.match_replace(marked[:, i % 2, e, :], find[:, i % 2, e, :],
                                                       logits[:, i, e, :], MARK)
                            link(mr)
                            if i == 0 and ahead:
                                dve.wait_ge(s_rstd, 1)
                                ln_apply(dve, b + 1, s_h)
                            if i:
                                weights(i - 1)
                        weights(NT - 1)
                        for i in range(NT):
                            dve.wait_ge(s_o, i + 1)
                            dve.tensor_tensor(x_tile(b, i), pT[i % 2][:, 0:D], x_tile(b, i), ALU.add).then_inc(s_xo, 1)

                    @block.gpsimd
                    def _(pool):
                        if ahead:
                            ln_gpsimd(pool, s_var, s_rstd)

                        def scaled(i):
                            pool.wait_ge(s_w, i + 1)
                            pool.wait_ge(s_inv, i + 1)
                            pool.tensor_tensor(probs[:, i % 2], probs[:, i % 2],
                                               inv[:, i, :, None].broadcast_to([P, HA, L]), ALU.mult).then_inc(s_pr, 1)

                        for i in range(NT):
                            if i >= 2:
                                pool.wait_ge(s_w, i - 1)
                            pool.wait_ge(s_d4, i + 1)
                            pool.tensor_tensor(shifted[:, i % 2], logits[:, i],
                                               top8[:, i, :, 0:1].broadcast_to([P, HA, L]), ALU.subtract).then_inc(s_sh, 1)
                            if i:
                                scaled(i - 1)
                        scaled(NT - 1)
                clear(sems)

            with nc.Block() as block:
                @block.tensor
                def _(pe):
                    open_tensor(pe)

                @block.scalar
                def _(act):
                    open_scalar(act)

                @block.vector
                def _(dve):
                    ln_vector(dve, Links(dve, s_dve), 0, s_var, s_rstd, s_h)

                @block.gpsimd
                def _(pool):
                    ln_gpsimd(pool, s_var, s_rstd)
            clear(sems)
            with nc.Fori(0, B - 1) as b:
                attend(b, ahead=True)
            attend(B - 1, ahead=False)

        def experts(n):
          with ExitStack() as ctx:
            W_COLS = DC * DF + D
            w_hi = sb(ctx, f"f{n}_w_hi", [P, E_ALL, W_COLS], F32R)
            w_lo = sb(ctx, f"f{n}_w_lo", [P, E_ALL, W_COLS], F32R)
            RAW = 10
            raw = sb(ctx, f"f{n}_raw", [P, RAW, W_COLS])
            r_raw = sb(ctx, f"f{n}_r_raw", [P, DC, E_RT])
            r_w = sb(ctx, f"f{n}_r_w", [P, DC, 2, E_RT], F32R)
            rT = sb(ctx, f"f{n}_rT", [2 * E_RT, B, T])
            both = sb(ctx, f"f{n}_both", [2 * E_RT, E_RT])
            hs = sb(ctx, f"f{n}_h", [P, B * NT, D])
            hT_hi = sb(ctx, f"f{n}_hT_hi", [P, B, DC, T], F32R)
            hT_lo = sb(ctx, f"f{n}_hT_lo", [P, B, DC, T], F32R)
            mid = sb(ctx, f"f{n}_mid", [P, 3, T])
            mid_hi = sb(ctx, f"f{n}_mid_hi", [P, 3, T], F32R)
            mid_lo = sb(ctx, f"f{n}_mid_lo", [P, 3, T], F32R)
            stats = sb(ctx, f"f{n}_stats", [P, B * NT, 6])
            mv = sb(ctx, f"f{n}_mv", [P, B * NT, 2])
            var = sb(ctx, f"f{n}_var", [P, B * NT])
            rstd = sb(ctx, f"f{n}_rstd", [P, B * NT])
            lg = sb(ctx, f"f{n}_lg", [P, B * NT, E_RT])
            ex = sb(ctx, f"f{n}_ex", [P, B * NT, E_RT])
            pr = sb(ctx, f"f{n}_pr", [P, B * NT, E_RT])
            mk = sb(ctx, f"f{n}_mk", [P, B * NT, E_RT])
            gate = sb(ctx, f"f{n}_gate", [P, B * NT, E_RT])
            great = sb(ctx, f"f{n}_great", [P, B * NT])
            total = sb(ctx, f"f{n}_total", [P, B * NT])
            inv = sb(ctx, f"f{n}_inv", [P, B * NT])
            top8 = sb(ctx, f"f{n}_top8", [P, B * NT, 8])
            find = sb(ctx, f"f{n}_find", [P, B * NT, 8])
            bank = psum(ctx, f"f{n}_bank", [P, 8 * 512])
            pR = bank[:, 3 * 512:3 * 512 + B * NT * E_RT]
            pU = [bank[:, k * 512:(k + 1) * 512] for k in range(2)]
            d_r = sem(ctx, f"f{n}_d_r")
            d_w = [sem(ctx, f"f{n}_d_w{k}") for k in range(E_ALL // 2)]
            (s_var, s_rstd, s_h, s_hT, s_hi, s_lo, s_w, s_rsplit, s_rp, s_rT, s_r, s_sub, s_ex, s_gate, s_up, s_mid, s_mlo,
             s_dn, s_xo, s_dve, s_pool, s_whi) = (sem(ctx, f"f{n}_" + s) for s in
                                   ("var", "rstd", "h", "hT", "hi", "lo", "w", "rsplit", "rp", "rT", "r", "sub", "ex", "gate", "up",
                                    "mid", "mlo", "dn", "xo", "dve", "pool", "whi"))

            def up_w(w, e, c):
                return w[:, e, c * DF:(c + 1) * DF]

            def down_w(w, e):
                return w[:, e, DC * DF:W_COLS]

            def down_bank(e, i):
                at = (2 + 2 * (e % 2)) * 512 + i * D
                return bank[:, at:at + D]

            def x_tiles(b, i):
                return x[:, bass.ds(b * (NT * D) + i * D, D)]

            with nc.Block() as block:
                @block.sync
                def _(sp):
                    sp.dma_start(r_raw[:, :, :], W_router.rearrange("(m p) e -> p m e", p=P)).then_inc(d_r, 16)
                    for lo, count, up, down in ((0, E_SH, Wsh_up, Wsh_down), (E_SH, E_RT, Wrt_up, Wrt_down)):
                        for e in range(count):
                            g = lo + e
                            if g >= RAW and g % 2 == 0:
                                sp.wait_ge(s_w, g - RAW + 2)
                            sp.dma_start(raw[:, g % RAW, 0:DC * DF].rearrange("p (m f) -> p m f", m=DC),
                                         up[e].rearrange("(m p) f -> p m f", p=P)).then_inc(d_w[g // 2], 16)
                            sp.dma_start(raw[:, g % RAW, DC * DF:W_COLS], down[e]).then_inc(d_w[g // 2], 16)

                @block.tensor
                def _(pe):
                    for b in range(B):
                        pe.wait_ge(s_h, (b + 1) * NT)
                        for m in range(DC):
                            for i in range(NT):
                                at = (DC * b + m) * T + i * P
                                t = pe.transpose(bank[:, at:at + P], hs[:, b * NT + i, m * P:(m + 1) * P], ident[:, :])
                        t.then_inc(s_hT, 1)
                    pe.wait_ge(s_rsplit, 3)
                    for b in range(B):
                        pe.wait_ge(s_lo, b + 1)
                        o = bank[0:2 * E_RT, DC * b * T:(DC * b + 1) * T]
                        for c in range(DC):
                            for k, a in enumerate((hT_hi, hT_lo)):
                                mm = pe.matmul(o, r_w[:, c, :, :].rearrange("p a e -> p (a e)"), a[:, b, c, :],
                                               start=(c + k == 0), stop=(c + k == DC))
                        mm.then_inc(s_rp, 1)
                    for b in range(B):
                        pe.wait_ge(s_rT, b + 1)
                        for i in range(NT):
                            o = pR[:, (b * NT + i) * E_RT:(b * NT + i + 1) * E_RT]
                            mm = pe.matmul(o, rT[:, b, i * P:(i + 1) * P], both[:, :], start=True, stop=True)
                        mm.then_inc(s_r, 1)
                    pe.wait_ge(s_sub, 1)

                    with pe.Fori(0, B) as b:
                        def up(e):
                            pe.wait_ge(s_w, e + 1)
                            if e >= 2:
                                pe.wait_ge(s_mid, b * E_ALL + (e - 1))
                            k = 0
                            for c in range(DC):
                                for w, a in ((w_hi, hT_hi), (w_hi, hT_lo), (w_lo, hT_hi)):
                                    mm = pe.matmul(pU[e % 2], up_w(w, e, c),
                                                   a[:, bass.ds(b, 1), c, :].rearrange("p b t -> p (b t)"),
                                                   start=(k == 0), stop=(k == 3 * DC - 1))
                                    k += 1
                            mm.then_inc(s_up, 1)

                        up(0)
                        up(1)
                        for e in range(E_ALL):
                            if e + 2 < E_ALL:
                                up(e + 2)
                            pe.wait_ge(s_mlo, b * E_ALL + (e + 1))
                            pe.wait_ge(s_xo, b * (NT * E_ALL) + NT * (e + 1))
                            for i in range(NT):
                                for k, (a, w) in enumerate(((mid_hi, w_hi), (mid_hi, w_lo), (mid_lo, w_hi))):
                                    mm = pe.matmul(down_bank(e, i), a[:, e % 3, i * P:(i + 1) * P], down_w(w, e),
                                                   start=(k == 0), stop=(k == 2))
                            mm.then_inc(s_dn, 1)

                @block.scalar
                def _(act):
                    for b in range(B):
                        act.wait_ge(s_hT, b + 1)
                        act.activation(hT_hi[:, b].rearrange("p c t -> p (c t)"), bank[:, DC * b * T:DC * (b + 1) * T],
                                       ACT.Copy).then_inc(s_hi, 1)
                        act.wait_ge(d_w[b], 64)
                        for e in (2 * b, 2 * b + 1):
                            act.activation(w_hi[:, e, :], raw[:, e % RAW, :], ACT.Copy).then_inc(s_whi, 1)
                    for b in range(B):
                        act.wait_ge(s_rp, b + 1)
                        act.activation(rT[:, b, :], bank[0:2 * E_RT, DC * b * T:(DC * b + 1) * T],
                                       ACT.Copy).then_inc(s_rT, 1)
                    act.wait_ge(s_sub, 1)
                    act.activation(ex[:, :, :], lg[:, :, :], ACT.Exp).then_inc(s_ex, 1)
                    with act.Fori(0, B) as b:
                        for e in range(E_ALL):
                            act.wait_ge(s_up, b * E_ALL + (e + 1))
                            if e >= 3:
                                act.wait_ge(s_dn, b * E_ALL + (e - 2))
                            act.activation(mid_hi[:, e % 3, :], pU[e % 2], ACT.Gelu)
                            act.activation(mid[:, e % 3, :], pU[e % 2], ACT.Gelu).then_inc(s_mid, 1)

                @block.vector
                def _(dve):
                    link = Links(dve, s_dve)
                    dve.memset(find[:, :, :], NONE).then_inc(s_xo, 2 * NT)

                    def spread(b):
                        for i in range(b * NT, (b + 1) * NT):
                            st = dve.bn_stats(stats[:, i, :], x[:, i * D:(i + 1) * D])
                        link(st)
                        for i in range(b * NT, (b + 1) * NT):
                            st = dve.bn_aggr(mv[:, i, :], stats[:, i, :])
                        link(st)
                        dve.tensor_scalar(var[:, b * NT:(b + 1) * NT], mv[:, b * NT:(b + 1) * NT, 1], LN_EPS, None,
                                          ALU.add).then_inc(s_var, 1)

                    def normal(b):
                        dve.wait_ge(s_rstd, b + 1)
                        for i in range(b * NT, (b + 1) * NT):
                            dve.tensor_scalar(hs[:, i, :], x[:, i * D:(i + 1) * D], mv[:, i, 0:1], rstd[:, i:i + 1],
                                              ALU.subtract, ALU.mult).then_inc(s_h, 1)

                    def rest(b):
                        dve.wait_ge(s_hi, b + 1)
                        dve.tensor_tensor(hT_lo[:, b].rearrange("p c t -> p (c t)"), bank[:, b * DC * T:(b + 1) * DC * T],
                                          hT_hi[:, b].rearrange("p c t -> p (c t)"), ALU.subtract).then_inc(s_lo, 1)

                    for b in range(B + 2):
                        if b < B:
                            spread(b)
                        if 1 <= b <= B:
                            normal(b - 1)
                        if b >= 2:
                            rest(b - 2)
                    dve.wait_ge(s_r, B)
                    r = pR.rearrange("p (i e) -> p i e", e=E_RT)
                    link(dve.tensor_reduce(great[:, :], r, AX_X, ALU.max))
                    dve.tensor_tensor(lg[:, :, :], r, great[:, :, None].broadcast_to([P, B * NT, E_RT]),
                                      ALU.subtract).then_inc(s_sub, 1)
                    dve.wait_ge(s_ex, 1)
                    link(dve.tensor_reduce(total[:, :], ex[:, :, :], AX_X, ALU.add))
                    link(dve.reciprocal(inv[:, :], total[:, :]))
                    link(dve.tensor_tensor(pr[:, :, :], ex[:, :, :],
                                           inv[:, :, None].broadcast_to([P, B * NT, E_RT]), ALU.mult))
                    for i in range(B * NT):
                        mx = dve.max(top8[:, i, :], pr[:, i, :])
                    link(mx)
                    link(dve.tensor_copy(find[:, :, 0:2], top8[:, :, 0:2]))
                    for i in range(B * NT):
                        mr = dve.match_replace(mk[:, i, :], find[:, i, :], pr[:, i, :], MARK)
                    link(mr)
                    dve.scalar_tensor_tensor(out=gate[:, :, :], in0=mk[:, :, :], scalar=MARK,
                                             in1=pr[:, :, :], op0=ALU.is_equal, op1=ALU.mult).then_inc(s_gate, 1)
                    dve.wait_ge(s_gate, 1)
                    with dve.Fori(0, B) as b:
                        def low(e):
                            dve.wait_ge(s_mid, b * E_ALL + (e + 1))
                            dve.tensor_tensor(mid_lo[:, e % 3, :], mid[:, e % 3, :], mid_hi[:, e % 3, :],
                                              ALU.subtract).then_inc(s_mlo, 1)

                        low(0)
                        low(1)
                        for e in range(E_ALL):
                            if e + 2 < E_ALL:
                                low(e + 2)
                            dve.wait_ge(s_dn, b * E_ALL + (e + 1))
                            for i in range(NT):
                                dve.wait_ge(s_xo, b * (NT * E_ALL) + (NT * (e + 1) + i + 1))
                                if e < E_SH:
                                    st = dve.tensor_tensor(x_tiles(b, i), down_bank(e, i), x_tiles(b, i), ALU.add)
                                else:
                                    g = gate[:, bass.ds(b * NT + i, 1), e - E_SH]
                                    st = dve.scalar_tensor_tensor(out=x_tiles(b, i), in0=down_bank(e, i),
                                                                  scalar=g, in1=x_tiles(b, i),
                                                                  op0=ALU.mult, op1=ALU.add)
                                st.then_inc(s_xo, 1)

                @block.gpsimd
                def _(pool):
                    for b in range(B):
                        r = slice(b * NT, (b + 1) * NT)
                        pool.wait_ge(s_var, b + 1)
                        pool.tensor_tensor(rstd[:, r], var[:, r], minus_half[:, 0:1].broadcast_to([P, NT]),
                                           ALU.pow).then_inc(s_rstd, 1)
                        if b == 0:
                            pool.wait_ge(d_r, 16)
                            pool.tensor_copy(r_w[:, :, 0, :], r_raw[:, :, :]).then_inc(s_rsplit, 1)
                            pool.wait_ge(s_rsplit, 1)
                            pool.tensor_tensor(r_w[:, :, 1, :], r_raw[:, :, :], r_w[:, :, 0, :],
                                               ALU.subtract).then_inc(s_rsplit, 1)
                            pool.wait_ge(s_rsplit, 2)
                            pool.tensor_tensor(both[:, :], ident[0:2 * E_RT, 0:E_RT], ident[0:2 * E_RT, E_RT:2 * E_RT],
                                               ALU.add).then_inc(s_rsplit, 1)
                            pool.wait_ge(s_rsplit, 3)
                    for e in range(E_ALL):
                        if e >= 2 * B:
                            if e % 2 == 0:
                                pool.wait_ge(d_w[e // 2], 64)
                            pool.tensor_copy(w_hi[:, e, :], raw[:, e % RAW, :]).then_inc(s_whi, 1)
                        pool.wait_ge(s_whi, e + 1)
                        pool.tensor_tensor(w_lo[:, e, :], raw[:, e % RAW, :], w_hi[:, e, :],
                                           ALU.subtract).then_inc(s_w, 1)

        def block_attention():
          HH = HB // 2
          NPR = HH // 2
          HR = P // 2
          MROW = 4 * HDB
          SROW = MROW + 2
          NV = HDB + 1
          PTW = T + (T - P) + (T - 2 * P) + (T - 3 * P)
          RING = 6
          NG = HH // 4
          AT = [0, T, 2 * T, T + (T - P)]
          with ExitStack() as ctx:
            WT = sb(ctx, "b_WT", [P, DC, 2, 4, P])
            WoT = sb(ctx, "b_WoT", [P, DC, D])
            table = sb(ctx, "b_table", [P, NT, 2 * HDB])
            tri = sb(ctx, "b_tri", [P, P], BF16)
            identb = sb(ctx, "b_identb", [P, P], BF16)
            avg = sb(ctx, "b_avg", [P, CPT])
            own = sb(ctx, "b_own", [P, P // HDB])
            onehot = sb(ctx, "b_onehot", [P, NT, NCH])
            past = sb(ctx, "b_past", [P, NT, NCH])
            notself = sb(ctx, "b_notself", [P, NT, NCH])
            bank = psum(ctx, "b_bank", [P, 8, 512])
            d_w = sem(ctx, "b_d_w")
            s_g0, s_g1, s_g2, s_g3, s_wT, s_z, s_c0 = (sem(ctx, "b_" + n) for n in ("g0", "g1", "g2", "g3", "wT", "z", "c0"))
            QTs = sb(ctx, "b_QT", [P, 2, NPR, T], F32R)
            KTs = sb(ctx, "b_KT", [P, 2, HH, T], F32R)
            VAs = sb(ctx, "b_VA", [P, 2, NT, HH * NV + 32])
            rows = sb(ctx, "b_rows", [P, 2 * HH, HR], F32R)
            rot = sb(ctx, "b_rot", [P, 2 * HH, HDB])
            rotA = sb(ctx, "b_rotA", [P, 2 * HH, HDB])
            rotB = sb(ctx, "b_rotB", [P, 2 * HH, HDB])
            qT = sb(ctx, "b_qT", [P, P])
            kmean = sb(ctx, "b_kmean", [P, HH, NCH])
            gm = sb(ctx, "b_gm", [P, HH, NCH])
            vhold = sb(ctx, "b_vhold", [P, P])
            mk = sb(ctx, "b_mk", [P, HH, NCH])
            top8 = sb(ctx, "b_top8", [P, HH, 8])
            find = sb(ctx, "b_find", [P, HH, 8])
            identr = sb(ctx, "b_identr", [P, P], F32R)
            tick = sb(ctx, "b_tick", [P, 1])
            tock = sb(ctx, "b_tock", [P, 1])
            unit = sb(ctx, "b_unit", [P, 1])
            negmax = sb(ctx, "b_negmax", [P, 2, NT, 2])
            mrow = sb(ctx, "b_mrow", [P, NT, 2, HR], F32R)
            PT = sb(ctx, "b_PT", [P, RING, PTW])
            OT = sb(ctx, "b_OT", [P, T])
            OgT = sb(ctx, "b_OgT", [P, T])
            rden = sb(ctx, "b_rden", [P, NT, 4])
            Os = sb(ctx, "b_O", [P, 2, NT, HH, HDB])
            sigs = sb(ctx, "b_sig", [P, 2, NT, P])
            gate = sb(ctx, "b_gate", [P, NT, P])
            sq = sb(ctx, "b_sq", [P, NT * HH, HDB])
            ms = sb(ctx, "b_ms", [P, NT * HH])
            rms = sb(ctx, "b_rms", [P, NT * HH])

            sems = [sem(ctx, "b_" + n) for n in
                    ("var", "rstd", "h", "hT", "hTs",
                     "qkv", "rp", "vh", "ga", "one", "rot", "lo", "cp", "qt", "km", "gt", "gm", "top", "sel", "tq", "tqs", "tk",
                     "s1", "mx", "mr", "mt", "mts", "s2", "e2", "pv", "ot", "ott", "on",
                     "sq", "mse", "rms", "og", "gT", "gTs", "fo", "xo", "gate", "dve")]
            (s_var, s_rstd, s_h, s_hT, s_hTs,
             s_qkv, s_rp, s_vh, s_ga, s_one, s_rot, s_lo, s_cp, s_qt, s_km, s_gt, s_gm, s_top, s_sel, s_tq, s_tqs, s_tk,
             s_s1, s_mx, s_mr, s_mt, s_mts, s_s2, s_e2, s_pv, s_ot, s_ott, s_on,
             s_sq, s_mse, s_rms, s_og, s_gT, s_gTs, s_fo, s_xo, s_gate, s_dve) = sems

            raw = PT[:, 0:2, :].rearrange("p k w -> p (k w)")[:, 0:4 * DC * D].rearrange("p (n m d) -> p n m d", n=4, m=DC)
            rawg1, Wg2T = PT[0:HDB, 2, 0:D], PT[0:HDB, 3, 0:D]
            rawg2 = PT[:, 4, 0:DC * HDB].rearrange("p (m e) -> p m e", m=DC)
            wcol = PT[:, 5, 0:1]
            with nc.Block() as block:
                @block.sync
                def _(sp):
                    for n, w in enumerate((Wq_b, Wk_b, Wv_b, Wo_b)):
                        sp.dma_start(raw[:, n, :, :], w.rearrange("(m p) d -> p m d", p=P)).then_inc(d_w, 16)
                    sp.dma_start(rawg1[:, :], Wg1).then_inc(d_w, 16)
                    sp.dma_start(rawg2[:, :, :], Wg2.rearrange("(m p) d -> p m d", p=P)).then_inc(d_w, 16)
                    sp.dma_start(table[:, :, :], rope.rearrange("(i p) e -> p i e", p=P)).then_inc(d_w, 16)
                    for r in range(P // HDB):
                        sp.dma_start(wcol[r * HDB:(r + 1) * HDB, :],
                                     o_norm.rearrange("(d o) -> d o", o=1)).then_inc(d_w, 16)
                    sp.wait_ge(d_w, 16 * (7 + P // HDB))

                @block.tensor
                def _(pe):
                    ln_turn(pe, [bank[:, 7, :], bank[:, 4, :]], s_h, s_hT)
                    pe.wait_ge(d_w, 16 * (7 + P // HDB))
                    for n in range(4):
                        for m in range(DC):
                            for c in range(DC):
                                pe.transpose(bank[:, n, c * D + m * P:c * D + m * P + P],
                                             raw[:, n, m, c * P:(c + 1) * P], ident[:, :])
                    for m in range(DC):
                        t = pe.transpose(bank[0:HDB, 5, m * P:(m + 1) * P], rawg2[:, m, :], ident[:, :])
                    t.then_inc(s_wT, 1)
                    pe.wait_ge(s_c0, 1)
                    for c in range(DC):
                        mm = pe.matmul(bank[:, 6, c * D:(c + 1) * D], rawg1[:, c * P:(c + 1) * P], Wg2T[:, :],
                                       start=True, stop=True)
                    mm.then_inc(s_wT, 1)

                @block.scalar
                def _(act):
                    ln_keep(act, [bank[:, 7, :], bank[:, 4, :]], s_hT, s_hTs)
                    act.wait_ge(s_wT, 1)
                    act.activation(Wg2T[:, :], bank[0:HDB, 5, 0:D], ACT.Copy).then_inc(s_c0, 1)
                    for n in range(3):
                        act.activation(WT[:, :, :, n, :],
                                       bank[:, n, :].rearrange("p (c f o) -> p c f o", c=DC, f=2), ACT.Copy)
                    act.activation(WoT[:, :, :], bank[:, 3, :].rearrange("p (c o) -> p c o", c=DC),
                                   ACT.Copy, scale=wcol[:, 0:1])
                    act.wait_ge(s_wT, 2)
                    act.activation(WT[:, :, :, 3, :], bank[:, 6, :].rearrange("p (c f o) -> p c f o", c=DC, f=2),
                                   ACT.Copy)

                @block.gpsimd
                def _(pool):
                    pool.memset(tri[:, :], 0.0)
                    pool.memset(avg[:, :], 1.0 / CH)
                    pool.memset(own[:, :], 1.0)
                    pool.memset(onehot[:, :, :], 1.0)
                    pool.memset(past[:, :, :], 0.0)
                    pool.tensor_copy(identb[:, :], ident[:, :]).then_inc(s_g0, 1)
                    pool.wait_ge(s_g0, 1)

                    def keep(t, base, pattern, mult, fill):
                        return pool.affine_select(out=t, in_=t, compare_op=ALU.is_ge, fill=fill, base=base,
                                                  pattern=pattern, channel_multiplier=mult)

                    keep(tri[:, :], 0, [[1, P]], -1, NEG)
                    keep(avg[:, :], 0, [[-CH, CPT]], 1, 0.0)
                    keep(own[:, :], 0, [[-HDB, P // HDB]], 1, 0.0)
                    keep(onehot[:, :, :], 0, [[P, NT], [-CH, NCH]], 1, 0.0)
                    keep(past[:, :, :], -CH, [[P, NT], [-CH, NCH]], 1, NEG).then_inc(s_g1, 1)
                    pool.wait_ge(s_g1, 1)
                    keep(avg[:, :], CH - 1, [[CH, CPT]], -1, 0.0)
                    keep(own[:, :], HDB - 1, [[HDB, P // HDB]], -1, 0.0)
                    keep(onehot[:, :, :], CH - 1, [[-P, NT], [CH, NCH]], -1, 0.0).then_inc(s_g2, 1)
                    ln_gpsimd(pool, s_var, s_rstd)
                    pool.wait_ge(s_rstd, 1)
                    pool.memset(KTs[HR:P, :, 0:HH:2, :].bitcast(F32), 0.0).then_inc(s_g3, 1)
                    pool.wait_ge(s_g3, 1)
                    pool.memset(rows[:, :, MROW:HR].bitcast(F32), 0.0).then_inc(s_g3, 1)
                    pool.memset(mrow[:, :, :, :].bitcast(F32), 0.0)
                    pool.memset(unit[:, :], 1.0)
                    pool.wait_ge(s_g3, 2)
                    pool.memset(rows[:, 0:HH, MROW:MROW + 2].bitcast(F32), 1.0)

                @block.vector
                def _(dve):
                    ln_vector(dve, Links(dve, s_dve), 0, s_var, s_rstd, s_h)
                    dve.memset(KTs[0:HR, :, 1:HH:2, :].bitcast(F32), 0.0)
                    dve.memset(find[:, :, :], NONE)
                    dve.memset(kmean[:, :, :], 0.0)
                    dve.tensor_copy(identr[:, :], ident[:, :])
                    dve.memset(VAs[:, :, :, :], 0.0).then_inc(s_z, 1)
                    dve.wait_ge(s_z, 1)
                    for f in range(2):
                        dve.memset(VAs[:, f, :, 0:HH * NV].rearrange("p i (h e) -> p i h e", e=NV)[:, :, :, HDB:NV], 1.0)
                    dve.wait_ge(s_g2, 1)
                    dve.tensor_scalar(notself[:, :, :], onehot[:, :, :], -NEG, NEG, ALU.mult, ALU.add)

            T0, T1, T2, V0 = (bank[:, k, :] for k in (0, 1, 2, 7))
            rbank, sbank = (3, 4), (5, 6)
            FILL1 = [(0, (0, 1)), (1, (0, 1)), (2, (0,)), (2, (1,)), (3, (0,)), (3, (1,))]
            FILL2 = [(0, (0,), ((0, 0),)), (T, (0,), ((1, 0), (3, T - P))),
                     (0, (1,), ((0, 0),)), (T, (1,), ((1, 0), (3, T - P))),
                     (2 * T, (0, 1), ((2, 0),))]
            N1, N2 = len(FILL1), len(FILL2)
            USES1 = N1 + 1
            STEPS = 2 * NPR
            ROOTS = (7, 9, 10, 12)
            START = [0, 3, 6, 10]
            """
            Steps of a phase. Score: step s makes three fills of the first pass of pair s // 2, and two or three
            of the second pass, from step 2 p + 3 on for pair p (see `behind`). Make: tile i
            is projected at START[i], rotated at + 1, split at + 2, its chunks chosen at + 3 and + 4, and its rows
            are turned at + 3 to + 5. Values of heads 4 g to 4 g + 3: from step 4 g + 7; the last four's at step 3
            of the phase after. Finish, of the unit before: squares, mean and root at steps 6 to 12, gate 13,
            transposes 14; projection and sum at steps 1 and 2 of the phase after that.
            """

            def carry_wait():
                nc.vector.memset(tick[:, :], 0.0)

            def due(w, s, part):
                return START.index(s - part) if w.make and s - part in START else None

            def above(count, n=0):
                return not isinstance(count, int) or count > n

            def behind(s):
                return (s - 3) // 2 if s % 2 else (s - 4) // 2, 0 if s % 2 else 2

            class Part:

                def __init__(self, half, score, make, b_done, b_norm, b_add, counts):
                    self.half, self.score, self.make = half, score, make
                    self.b_done, self.b_norm, self.b_add = b_done, b_norm, b_add
                    self.finish, self.norm, self.add = b_done is not None, b_norm is not None, b_add is not None
                    self.qs, self.qm, self.qf, self.qn, self.qa = counts

                def after(self):
                    return (self.qs + self.score, self.qm + self.make, self.qf + self.finish, self.qn + self.norm,
                            self.qa + self.add)

                def group(self, g):
                    return self.qf + (NG - 1) * self.qs + (g + 1 if self.finish else g)

            def chain(counts, *phases):
                parts = []
                for phase in phases:
                    parts.append(Part(*phase, counts))
                    counts = parts[-1].after()
                return parts

            opening = chain((0, 0, 0, 0, 0),
                            (1, False, True, None, None, None),
                            (0, True, True, None, 1, None),
                            (1, True, True, 0, None, None))
            LOOPS = B - 2
            base = opening[-1].after()
            STRIDE = (2, 2, 2, 1, 2)

            def round_of(b):
                return chain(tuple((b - 1) * d + q for q, d in zip(base, STRIDE)),
                             (0, True, True, b - 1, b + 1, b - 1),
                             (1, True, True, b, None, b - 1))

            closing = chain(tuple(q + LOOPS * d for q, d in zip(base, STRIDE)),
                            (0, True, True, B - 2, None, B - 2),
                            (1, True, False, B - 1, None, B - 2),
                            (0, False, False, B - 1, None, B - 1),
                            (1, False, False, None, None, B - 1))

            def tensor_part(pe, w):
                half, other = w.half, 1 - w.half
                QT, KT = QTs[:, half], KTs[:, half]
                first_pair = w.qs * NPR
                Od = Os[:, other]

                def project(i):
                    t = w.qm * NT + i
                    if i > 1:
                        pe.wait_ge(s_gm, w.qm * (NT - 1) + (i - 1))
                    elif i:
                        pe.wait_ge(s_km, t)
                    elif above(w.qm):
                        pe.wait_ge(s_gm, w.qm * (NT - 1))
                    if i == 0 and above(w.qf):
                        pe.wait_ge(s_gTs, w.qf)
                    if i == 0 and above(w.qn):
                        pe.wait_ge(s_hTs, w.qn * DC)
                    for c in range(DC):
                        mm = pe.matmul(T0, hT[:, c, i * P:(i + 1) * P],
                                       WT[:, c, other, :, :].rearrange("p n o -> p (n o)"),
                                       start=(c == 0), stop=(c == DC - 1))
                    mm.then_inc(s_qkv, 1)

                def means(i):
                    t = w.qm * NT + i
                    pe.wait_ge(s_rot, t + 1)
                    pe.wait_ge(s_ga, t + 1)
                    flat = rot[:, :, :].rearrange("p h e -> p (h e)")
                    pe.transpose(T0[:, 0:P], flat[:, 0:P], ident[:, :])
                    pe.matmul(T0[:, P:P + CPT], flat[:, P:2 * P], avg[:, :], start=True, stop=True).then_inc(s_qt, 1)

                def gates(i):
                    pe.wait_ge(s_km, w.qm * NT + i + 1)
                    pe.matmul(T0[:, 0:HH * NCH], qT[:, :], kmean[:, :, :].rearrange("p h n -> p (h n)"),
                              start=True, stop=True).then_inc(s_gt, 1)

                def turn_rows(i, f):
                    t = w.qm * NT + i
                    if f < 2 and i == 0 and above(w.qa + w.add):
                        pe.wait_ge(s_xo, (w.qa + w.add) * NT)
                    if f == 0:
                        pe.wait_ge(s_cp, t + 1)
                        if above(t):
                            pe.wait_ge(s_tqs, t * 2 - 1)
                    elif f == 1:
                        if above(t):
                            pe.wait_ge(s_tqs, t * 2)
                    else:
                        pe.wait_ge(s_sel, t + 1)
                        pe.wait_ge(s_tk, t * 2 + (f - 1))
                    for k in range(4):
                        hd = 8 * f + 2 * k
                        mm = pe.matmul((T1 if f % 2 else T2)[:, k * P:(k + 1) * P],
                                       rows[:, hd:hd + 2, :].rearrange("p h r -> p (h r)"), identr[:, :],
                                       start=True, stop=True)
                    mm.then_inc(s_tq, 1)

                def first_pass(p, n):
                    pair = first_pair + p
                    i, heads = FILL1[n]
                    if n == 2:
                        if above(pair):
                            pe.wait_ge(s_mts, pair)
                    elif n or above(pair):
                        back = {0: -1, 1: 1, 3: 2, 4: 3, 5: 4}[n]
                        pe.wait_ge(s_mx, pair * N1 + back)
                    if n == 0 and p == 0:
                        pe.wait_ge(s_tqs, w.qm * (2 * NT))
                        pe.wait_ge(s_tk, w.qm * (2 * NT))
                    use = USES1 * p + (n + 1 if n else 0)
                    wd = P * (i + 1)
                    o = bank[:, rbank[use % 2], 0:wd * len(heads)].rearrange("p (h w) -> p h w", w=wd)
                    for k, a in enumerate(heads):
                        pe.matmul(o[:, k, :], QT[:, p, i * P:wd], KT[:, 2 * p + a, 0:wd], start=(k == 0), stop=True,
                                  skip_group_check=True)
                    pe.matmul(o[:, :, P * i:wd], tri[:, :], identb[:, None, :].broadcast_to([P, len(heads), P]),
                              start=False, stop=True, skip_group_check=True).then_inc(s_s1, 1)

                def turn_maximum(p):
                    pair = first_pair + p
                    pe.wait_ge(s_mr, pair + 1)
                    o = bank[:, rbank[(USES1 * (p + 1) + 1) % 2], :]
                    for i in range(NT):
                        mm = pe.matmul(o[:, i * P:(i + 1) * P], mrow[:, i, :, :].rearrange("p a r -> p (a r)"),
                                       identr[:, :], start=True, stop=True)
                    mm.then_inc(s_mt, 1)

                def second_pass(p, n):
                    pair = first_pair + p
                    u = pair * N2 + n
                    Q, K = (QT, KT) if p >= 0 else (QTs[:, other], KTs[:, other])
                    q = p % NPR
                    _, heads, blocks = FILL2[n]
                    if n == 0:
                        pe.wait_ge(s_mts, pair + 1)
                    if above(u, 1):
                        pe.wait_ge(s_e2, u - 1)
                    at = []
                    for k, a in enumerate(heads):
                        for j, c0 in blocks:
                            at.append(c0 + k * (T - 2 * P))
                            o = bank[:, sbank[(N2 * p + n) % 2], at[-1]:at[-1] + T - P * j]
                            pe.matmul(o, K[:, 2 * q + a, j * P:(j + 1) * P], Q[:, q, j * P:T],
                                      start=(len(at) == 1), stop=True, skip_group_check=True)
                    o = bank[:, sbank[(N2 * p + n) % 2], :].rearrange("p (m t) -> p m t", t=P)[:, 0:at[-1] // P + 1:max(at[-1] // P, 1)]
                    pe.matmul(o, identb[:, :], tri[:, None, :].broadcast_to([P, len(at), P]), start=False, stop=True,
                              skip_group_check=True).then_inc(s_s2, 1)

                def values(g, tiles):
                    n = w.group(g)
                    if 0 in tiles:
                        pe.wait_ge(s_e2, (first_pair + 2 * (g + 1)) * N2)
                        if g == 0:
                            pe.wait_ge(s_ga, w.qm * NT)
                        if above(n):
                            pe.wait_ge(s_on, n)
                    hd0 = 4 * (g % NG)
                    VA = VAs[:, other if g < 0 else half]
                    for j in tiles:
                        for s in range(4):
                            hd = hd0 + s
                            mm = pe.matmul(V0[32 * s:32 * s + 32, j * P:T], VA[:, j, hd * NV:hd * NV + 32],
                                           PT[:, hd % RING, AT[j]:AT[j] + T - P * j],
                                           start=(j == 0), stop=True, skip_group_check=True)
                    if NT - 1 in tiles:
                        mm.then_inc(s_pv, 1)

                def turn(g):
                    pe.wait_ge(s_ot, w.group(g) + 1)
                    for i in range(NT):
                        t = pe.transpose(V0[:, i * P:(i + 1) * P], OT[:, i * P:(i + 1) * P], ident[:, :])
                    t.then_inc(s_ott, 1)

                def finish_turn():
                    if w.make:
                        pe.wait_ge(s_gm, (w.qm + 1) * (NT - 1))
                    if w.norm:
                        pe.wait_ge(s_hTs, w.qn * DC + 1)
                    pe.wait_ge(s_og, w.qf + 1)
                    for i in range(NT):
                        t = pe.transpose(T0[:, i * P:(i + 1) * P], Od[:, i].rearrange("p h e -> p (h e)"), ident[:, :])
                    t.then_inc(s_gT, 1)

                def add_project():
                    pe.wait_ge(s_gTs, w.qa + 1)
                    if above(w.qm):
                        pe.wait_ge(s_tqs, w.qm * (2 * NT))
                    for i in range(NT):
                        o = (T1, T2)[i // 2][:, (i % 2) * D:(i % 2 + 1) * D]
                        pe.matmul(o, OgT[:, i * P:(i + 1) * P], WoT[:, half, :], start=True, stop=True).then_inc(s_fo, 1)

                def turn_h(m):
                    if m == 0:
                        pe.wait_ge(s_h, (w.qn + 1) * NT)
                        pe.wait_ge(s_gm, (w.qm + 1) * (NT - 1))
                    else:
                        pe.wait_ge(s_hTs, w.qn * DC + m)
                        if w.finish:
                            pe.wait_ge(s_gTs, w.qf + 1)
                    for i in range(NT):
                        t = pe.transpose(T0[:, i * P:(i + 1) * P], h[:, i, m * P:(m + 1) * P], ident[:, :])
                    t.then_inc(s_hT, 1)

                for s in range(STEPS):
                    p, b2 = s // 2, 3 * (s % 2)
                    q, n = behind(s)
                    if w.score:
                        first_pass(p, b2)
                    if (w.finish if q < 0 else w.score) and n:
                        second_pass(q, 2)
                    if (i := due(w, s, 5)) is not None:
                        turn_rows(i, 3)
                    if (i := due(w, s, 4)) is not None:
                        turn_rows(i, 1)
                    if w.finish and s == 3:
                        values(-1, (0, 1, 2, 3))
                    if w.finish and s == 4:
                        turn(-1)
                    if w.score and s in (9, 13) or w.finish and s == 1:
                        turn(s // 4 - 2)
                    if (i := due(w, s, 2)) is not None:
                        means(i)
                    if due(w, s, 3):
                        gates(due(w, s, 3))
                    if (w.score if p else w.finish) and s % 2 == 0:
                        turn_maximum(p - 1)
                    if w.score:
                        first_pass(p, b2 + 1)
                    if w.score and s in (8, 12) or w.finish and s == 0:
                        values(s // 4 - 2, (2, 3))
                    if w.finish if q < 0 else w.score:
                        second_pass(q, 3 if n else 0)
                    if (i := due(w, s, 0)) is not None:
                        project(i)
                    if w.score:
                        first_pass(p, b2 + 2)
                    if w.add and s == 1:
                        add_project()
                    if w.norm and s == 14:
                        turn_h(0)
                    if (i := due(w, s, 3)) is not None:
                        turn_rows(i, 0)
                    if w.score and s in (7, 11, 15):
                        values(s // 4 - 1, (0, 1))
                    if w.finish if q < 0 else w.score:
                        second_pass(q, 4 if n else 1)
                    if (i := due(w, s, 4)) is not None:
                        turn_rows(i, 2)
                    if w.finish and s == 14:
                        finish_turn()
                    if w.norm and s == 15:
                        turn_h(1)

            def scalar_part(act, w):
                half, other = w.half, 1 - w.half
                QT, QTn, KTn, sign = QTs[:, half], QTs[:, other], KTs[:, other], sigs[:, other]
                first_pair = w.qs * NPR

                def keep_values(i):
                    t = w.qm * NT + i
                    act.wait_ge(s_rp, t + 1)
                    if i == 0 and above(w.qs):
                        act.wait_ge(s_gate, w.qs * NT)
                    if i == 0:
                        hold = act.activation(vhold[:, :], T0[:, 2 * P:3 * P], ACT.Copy)
                        hold.then_inc(s_vh, 1)
                    else:
                        act.activation(VAs[:, other, i, 0:HH * NV].rearrange("p (h e) -> p h e", e=NV)[:, :, 0:HDB],
                                       T0[:, 2 * P:3 * P].rearrange("p (h e) -> p h e", e=HDB), ACT.Copy)
                    act.activation(sign[:, i, :], T0[:, 3 * P:4 * P], ACT.Exp, scale=-1.0).then_inc(s_ga, 1)

                def place_values():
                    act.wait_ge(s_vh, w.qm + 1)
                    if w.finish:
                        act.wait_ge(s_pv, w.group(-1) + 1)
                    act.activation(VAs[:, other, 0, 0:HH * NV].rearrange("p (h e) -> p h e", e=NV)[:, :, 0:HDB],
                                   vhold[:, :].rearrange("p (h e) -> p h e", e=HDB), ACT.Copy)

                def keep_keys(i, f):
                    act.wait_ge(s_tq, (w.qm * NT + i) * 4 + (f + 1))
                    for a in range(2):
                        r = slice(HR * a, HR * (a + 1))
                        cp = act.activation(KTn[r, 8 * f + a:8 * f + 7 + a:2, i * P:(i + 1) * P],
                                            (T1 if f else T2)[r, :].rearrange("p (k t) -> p k t", k=4), ACT.Copy)
                    cp.then_inc(s_tk, 1)

                def keep_queries(i, f):
                    act.wait_ge(s_tq, (w.qm * NT + i) * 4 + (f + 3))
                    act.activation(QTn[:, 4 * f:4 * f + 4, i * P:(i + 1) * P],
                                   (T1 if f else T2).rearrange("p (k t) -> p k t", k=4), ACT.Copy).then_inc(s_tqs, 1)

                def take(g):
                    n = w.group(g)
                    act.wait_ge(s_pv, n + 1)
                    if above(n):
                        act.wait_ge(s_ott, n)
                    act.activation(OT[:, :], V0, ACT.Copy).then_inc(s_ot, 1)

                def keep_maximum(p):
                    pair = first_pair + p
                    act.wait_ge(s_mt, pair + 1)
                    o = bank[:, rbank[(USES1 * (p + 1) + 1) % 2], :]
                    for a in range(2):
                        r = slice(HR * a + MROW, HR * a + MROW + 2)
                        cp = act.activation((QT if p >= 0 else QTn)[r, p % NPR, :], o[r, :], ACT.Copy)
                    cp.then_inc(s_mts, 1)

                def exponentials(p, n):
                    pair = first_pair + p
                    c0, heads, blocks = FILL2[n]
                    act.wait_ge(s_s2, pair * N2 + (n + 1))
                    if n == 0:
                        if p >= RING // 2:
                            act.wait_ge(s_pv, w.group((p - RING // 2) // 2) + 1)
                        elif p >= 0 and w.finish:
                            act.wait_ge(s_pv, w.group(-1) + 1)
                        elif p < 0:
                            act.wait_ge(s_pv, w.group(-1))
                    wd = sum(T - P * j for j, _ in blocks)
                    r0 = (2 * (p % NPR)) % RING + heads[0]
                    act.activation(PT[:, r0:r0 + len(heads), c0:c0 + wd],
                                   bank[:, sbank[(N2 * p + n) % 2], 0:wd * len(heads)].rearrange("p (h w) -> p h w", w=wd),
                                   ACT.Exp, scale=SCALE_B).then_inc(s_e2, 1)

                def keep_h(m):
                    act.wait_ge(s_hT, w.qn * DC + (m + 1))
                    act.activation(hT[:, m, :], T0, ACT.Copy).then_inc(s_hTs, 1)

                for s in range(STEPS):
                    p = s // 2 - 1
                    q, n = behind(s)
                    if (i := due(w, s, 5)) is not None:
                        keep_queries(i, 0)
                    if (i := due(w, s, 4)) is not None:
                        keep_keys(i, 0)
                    if (i := due(w, s, 1)) is not None:
                        keep_values(i)
                    if (w.finish if q < 0 else w.score) and n:
                        exponentials(q, 2)
                    if (w.score if p >= 0 else w.finish) and s % 2 == 0:
                        keep_maximum(p)
                    if (i := due(w, s, 5)) is not None:
                        keep_queries(i, 1)
                    if (i := due(w, s, 4)) is not None:
                        keep_keys(i, 1)
                    if w.finish and s == 3:
                        take(-1)
                    if w.score and s in (8, 12) or w.finish and s == 0:
                        take(s // 4 - 2)
                    if w.make and s == 3:
                        place_values()
                    if w.finish if q < 0 else w.score:
                        exponentials(q, 3 if n else 0)
                    if w.norm and s == 14:
                        keep_h(0)
                    if w.finish if q < 0 else w.score:
                        exponentials(q, 4 if n else 1)
                    if w.finish and s == 14:
                        act.wait_ge(s_gT, w.qf + 1)
                        if above(w.qf):
                            act.wait_ge(s_fo, w.qf * NT)
                        act.activation(OgT[:, :], T0, ACT.Copy).then_inc(s_gTs, 1)
                    if w.norm and s == 15:
                        keep_h(1)

            def vector_part(dve, link, w):
                half, other = w.half, 1 - w.half
                KTn = KTs[:, other]
                first_pair = w.qs * NPR
                Od = Os[:, other]

                def rotate(i):
                    t = w.qm * NT + i
                    dve.wait_ge(s_qkv, t + 1)
                    if above(t):
                        dve.wait_ge(s_rot, t)
                    qk = T0[:, 0:2 * P].rearrange("p (h e) -> p h e", e=HDB)
                    mid = HDB // 2

                    def tab(lo, hi):
                        return table[:, i, None, lo:hi].broadcast_to([P, 2 * HH, hi - lo])

                    dve.tensor_tensor(rotA[:, :, :], qk, tab(0, HDB), ALU.mult)
                    dve.tensor_tensor(rotB[:, :, 0:mid], qk[:, :, mid:HDB], tab(HDB, HDB + mid), ALU.mult)
                    dve.tensor_tensor(rotB[:, :, mid:HDB], qk[:, :, 0:mid], tab(HDB + mid, 2 * HDB),
                                      ALU.mult).then_inc(s_rp, 1)

                def split(i):
                    t = w.qm * NT + i
                    dve.wait_ge(s_rot, t + 1)
                    if above(t):
                        dve.wait_ge(s_tq, t * 4)
                    for lo, hi in ((0, HH), (HH, 2 * HH)):
                        sp = dve.tensor_copy(rows[:, HH - lo:2 * HH - lo, 0:HDB], rot[:, lo:hi, :])
                    link(sp)
                    for lo, hi in ((0, HH), (HH, 2 * HH)):
                        sp = dve.tensor_tensor(rows[:, HH - lo:2 * HH - lo, 3 * HDB:4 * HDB], rot[:, lo:hi, :],
                                               rows[:, HH - lo:2 * HH - lo, 0:HDB], ALU.subtract)
                    sp.then_inc(s_lo, 1)

                def keep_means(i):
                    t = w.qm * NT + i
                    dve.wait_ge(s_qt, t + 1)
                    if i > 1:
                        dve.wait_ge(s_gt, w.qm * (NT - 1) + (i - 1))
                    elif i == 0 and above(w.qm):
                        dve.wait_ge(s_gt, w.qm * (NT - 1))
                    dve.tensor_copy(qT[:, :], T0[:, 0:P])
                    dve.tensor_tensor(kmean[:, :, i * CPT:(i + 1) * CPT],
                                      T0[:, None, P:P + CPT].broadcast_to([P, HH, CPT]),
                                      own[:, :, None].broadcast_to([P, HH, CPT]), ALU.mult).then_inc(s_km, 1)

                def greatest(i):
                    n = w.qm * (NT - 1) + i
                    dve.wait_ge(s_gt, n)
                    dve.tensor_tensor(gm[:, :, :], T0[:, 0:HH * NCH].rearrange("p (h n) -> p h n", n=NCH),
                                      past[:, i, None, :].broadcast_to([P, HH, NCH]), ALU.add).then_inc(s_gm, 1)
                    dve.wait_ge(s_gm, n)
                    carry_wait()
                    for e in range(HH):
                        mx = dve.max(top8[:, e, :], gm[:, e, :])
                    mx.then_inc(s_top, 1)

                def choose(i):
                    if i == 0:
                        dve.memset(rows[:, HH:2 * HH, SROW:SROW + NCH].bitcast(F32), 0.0).then_inc(s_sel, 1)
                        return
                    dve.wait_ge(s_top, w.qm * (NT - 1) + i)
                    link(dve.tensor_copy(find[:, :, 0:PAST], top8[:, :, 0:PAST]))
                    carry_wait()
                    for e in range(HH):
                        mr = dve.match_replace(mk[:, e, :], find[:, e, :], gm[:, e, :], MARK)
                    link(mr)
                    dve.scalar_tensor_tensor(out=rows[:, HH:2 * HH, SROW:SROW + NCH], in0=mk[:, :, :],
                                             scalar=MARK,
                                             in1=notself[:, i, None, :].broadcast_to([P, HH, NCH]),
                                             op0=ALU.not_equal, op1=ALU.mult).then_inc(s_sel, 1)

                def maximum(p, n):
                    i, heads = FILL1[n]
                    wd = P * (i + 1)
                    use = USES1 * p + (n + 1 if n else 0)
                    dve.wait_ge(s_s1, (first_pair + p) * N1 + (n + 1))
                    if n == 0 and above(first_pair + p, 1):
                        dve.wait_ge(s_mr, first_pair + (p - 1))
                    dve.tensor_reduce(negmax[:, p % 2, i, heads[0]:heads[0] + len(heads)],
                                      bank[:, rbank[use % 2], 0:wd * len(heads)].rearrange("p (h w) -> p h w", w=wd),
                                      AX_X, ALU.max, negate=True).then_inc(s_mx, 1)

                def split_maximum(p):
                    pair = first_pair + p
                    dve.wait_ge(s_mx, (pair + 1) * N1)
                    if above(pair):
                        dve.wait_ge(s_mt, pair)
                    nm = negmax[:, p % 2]
                    link(dve.tensor_copy(mrow[:, :, :, MROW], nm))
                    dve.tensor_tensor(mrow[:, :, :, MROW + 1], nm, mrow[:, :, :, MROW],
                                      ALU.subtract).then_inc(s_mr, 1)

                def normal(g):
                    O = Od if g < 0 else Os[:, half]
                    h0 = 4 * (g % NG)
                    dve.wait_ge(s_ott, w.group(g) + 1)
                    if g == 0 and above(w.qf):
                        dve.wait_ge(s_gT, w.qf)
                    o = V0.rearrange("p (i s e) -> p i s e", i=NT, s=4)
                    link(dve.reciprocal(rden[:, :, :], o[:, :, :, HDB]))
                    dve.tensor_tensor(O[:, :, h0:h0 + 4, :], o[:, :, :, 0:HDB],
                                      rden[:, :, :, None].broadcast_to([P, NT, 4, HDB]), ALU.mult).then_inc(s_on, 1)

                for s in range(STEPS):
                    p, b2 = s // 2, 3 * (s % 2)
                    if w.score:
                        maximum(p, b2)
                    if (i := due(w, s, 1)) is not None:
                        rotate(i)
                    if (i := due(w, s, 2)) is not None:
                        split(i)
                    if due(w, s, 3):
                        greatest(due(w, s, 3))
                    if w.score:
                        maximum(p, b2 + 1)
                    if (i := due(w, s, 2)) is not None:
                        keep_means(i)
                    if (i := due(w, s, 4)) is not None:
                        choose(i)
                    if w.finish and s == 1:
                        normal(-2)
                    if w.add and s == 2:
                        dve.wait_ge(s_fo, w.qa * NT + NT)
                        for k in range(NT):
                            dve.tensor_tensor(x_tile(w.b_add, k), (T1, T2)[k // 2][:, (k % 2) * D:(k % 2 + 1) * D],
                                              x_tile(w.b_add, k), ALU.add).then_inc(s_xo, 1)
                    if w.finish and s == 5:
                        normal(-1)
                    if w.finish and s == 7:
                        dve.wait_ge(s_sq, w.qf + 1)
                        link(dve.tensor_reduce(ms[:, :], sq[:, :, :], AX_X, ALU.add))
                        dve.tensor_scalar(ms[:, :], ms[:, :], 1.0 / HDB, RMS_EPS, ALU.mult, ALU.add).then_inc(s_mse, 1)
                    if w.finish and s == 13:
                        dve.wait_ge(s_rms, (w.qf + 1) * NT)
                        o = Od.rearrange("p i h e -> p (i h) e")
                        link(dve.tensor_tensor(o, o, rms[:, :, None].broadcast_to([P, NT * HH, HDB]), ALU.mult))
                        o = Od.rearrange("p i h e -> p (i h e)")
                        dve.tensor_tensor(o, o, gate[:, :, :].rearrange("p i c -> p (i c)"), ALU.mult).then_inc(s_og, 1)
                    if w.score:
                        maximum(p, b2 + 2)
                        if s % 2:
                            split_maximum(p)
                    if w.score and s >= 14:
                        if s == 14:
                            dve.wait_ge(s_one, w.qm * NT)
                            if w.finish:
                                dve.wait_ge(s_og, w.qf + 1)
                        for k in (0, 1) if s == 14 else (2, 3):
                            dve.reciprocal(gate[:, k, :], sigs[:, half, k, :]).then_inc(s_gate, 1)
                    if w.score and s in (10, 14):
                        normal(s // 4 - 2)
                    if w.norm and s == 1:
                        if above(w.qn):
                            dve.wait_ge(s_h, w.qn * NT)
                            dve.wait_ge(s_hT, w.qn * DC)
                        for k in range(NT):
                            st = dve.bn_stats(ln_stats[:, k, :], x_tile(w.b_norm, k))
                        link(st)
                        carry_wait()
                        for k in range(NT):
                            st = dve.bn_aggr(ln_mv[:, k, :], ln_stats[:, k, :])
                        link(st)
                        dve.tensor_scalar(ln_var[:, :], ln_mv[:, :, 1], LN_EPS, None, ALU.add).then_inc(s_var, 1)
                    if w.norm and s == 5:
                        dve.wait_ge(s_rstd, w.qn + 1)
                        for k in range(NT):
                            dve.tensor_scalar(h[:, k, :], x_tile(w.b_norm, k), ln_mv[:, k, 0:1], ln_rstd[:, k:k + 1],
                                              ALU.subtract, ALU.mult).then_inc(s_h, 1)

            def gpsimd_part(pool, w):
                half, other = w.half, 1 - w.half
                sign = sigs[:, other]
                Od = Os[:, other]

                for s in range(STEPS):
                    if (i := due(w, s, 3)) is not None:
                        pool.wait_ge(s_ga, w.qm * NT + (i + 1))
                        pool.tensor_tensor(sign[:, i, :], sign[:, i, :], unit[:, 0:1].broadcast_to([P, P]),
                                           ALU.add).then_inc(s_one, 1)
                    if (i := due(w, s, 1)) is not None:
                        t = w.qm * NT + i
                        pool.wait_ge(s_rp, t + 1)
                        if above(t):
                            pool.wait_ge(s_lo, t)
                            pool.wait_ge(s_qt, t)
                        if above(t):
                            pool.wait_ge(s_tq, t * 4 - 2)
                        pool.tensor_tensor(rot[:, :, :], rotA[:, :, :], rotB[:, :, :], ALU.add).then_inc(s_rot, 1)
                        pool.tensor_copy(rows[:, 0:HH, SROW:SROW + NCH],
                                         onehot[:, i, None, :].broadcast_to([P, HH, NCH]))
                    if (i := due(w, s, 2)) is not None:
                        pool.wait_ge(s_lo, w.qm * NT + (i + 1))
                        pool.tensor_tensor(tock[:, :], unit[:, :], unit[:, :], ALU.mult)
                        lo, hi = slice(3 * HDB, 4 * HDB), slice(0, HDB)
                        pool.tensor_copy(rows[:, 0:HH, HDB:2 * HDB], rows[:, 0:HH, lo])
                        pool.tensor_copy(rows[:, 0:HH, 2 * HDB:3 * HDB], rows[:, 0:HH, hi])
                        pool.tensor_copy(rows[:, HH:2 * HH, HDB:2 * HDB], rows[:, HH:2 * HH, hi])
                        pool.tensor_copy(rows[:, HH:2 * HH, 2 * HDB:3 * HDB], rows[:, HH:2 * HH, lo]).then_inc(s_cp, 1)
                    if w.finish and s == 6:
                        pool.wait_ge(s_on, w.group(-1) + 1)
                        o = Od.rearrange("p i h e -> p (i h) e")
                        pool.tensor_tensor(sq[:, :, :], o, o, ALU.mult).then_inc(s_sq, 1)
                    if w.finish and s in ROOTS:
                        k = ROOTS.index(s)
                        if k == 0:
                            pool.wait_ge(s_mse, w.qf + 1)
                        pool.tensor_tensor(rms[:, k * HH:(k + 1) * HH], ms[:, k * HH:(k + 1) * HH],
                                           minus_half[:, 0:1].broadcast_to([P, HH]), ALU.pow).then_inc(s_rms, 1)
                    if w.norm and s == 2:
                        pool.wait_ge(s_var, w.qn + 1)
                        pool.tensor_tensor(ln_rstd[:, :], ln_var[:, :], minus_half[:, 0:1].broadcast_to([P, NT]),
                                           ALU.pow).then_inc(s_rstd, 1)

            clear(sems)
            LINKS = 50

            def run(engine, part):
                for w in opening:
                    part(engine, w)
                with engine.Fori(1, B - 1) as b:
                    for w in round_of(b):
                        part(engine, w)
                for w in closing:
                    part(engine, w)

            with nc.Block() as block:
                @block.tensor
                def _(pe):
                    run(pe, tensor_part)

                @block.scalar
                def _(act):
                    run(act, scalar_part)

                @block.vector
                def _(dve):
                    link = Links(dve, s_dve)
                    for w in opening:
                        vector_part(dve, link, w)
                    opened = link.n
                    with dve.Fori(1, B - 1) as b:
                        link.turn((b - 1) * LINKS)
                        for w in round_of(b):
                            vector_part(dve, link, w)
                    assert link.n - opened == LINKS, link.n - opened
                    link.turn(LINKS * (LOOPS - 1))
                    for w in closing:
                        vector_part(dve, link, w)

                @block.gpsimd
                def _(pool):
                    run(pool, gpsimd_part)

        latent_attention()
        experts(0)
        block_attention()
        experts(1)

        s_out = sem(whole, "s_out")
        with nc.Block() as block:
            @block.sync
            def _(sp):
                for b in range(B):
                    sp.dma_start(out[b].rearrange("(i p) d -> p i d", p=P),
                                 x[:, b * NT * D:(b + 1) * NT * D].rearrange("p (i d) -> p i d", i=NT)).then_inc(s_out, 16)
                sp.wait_ge(s_out, 16 * B)


_INS = ["L0_attn_a_hidden_states", "L0_attn_a_Wq", "L0_attn_a_bq", "L0_attn_a_Wk", "L0_attn_a_bk", "L0_attn_a_Wv",
        "L0_attn_a_bv", "L0_attn_a_Wo", "L0_attn_a_bo", "L0_attn_a_latent_keys", "L0_attn_b_Wq", "L0_attn_b_Wk",
        "L0_attn_b_Wv", "L0_attn_b_Wo", "L0_attn_b_Wg1", "L0_attn_b_Wg2", "L0_attn_b_o_norm_weight",
        "L0_ffn_Wsh_up", "L0_ffn_Wsh_down", "L0_ffn_Wrt_up", "L0_ffn_Wrt_down", "L0_ffn_W_router"]


def rope_table():
    pos = np.arange(T, dtype=np.float32)
    inv_freq = (1.0 / np.float32(THETA) ** (np.arange(0, HDB, 2, dtype=np.float32) / np.float32(HDB))).astype(np.float32)
    ang = (pos[:, None] * inv_freq[None, :]).astype(np.float32)
    c, s = np.cos(ang), np.sin(ang)
    return np.concatenate([c, c, -s, s], axis=1).astype(np.float32)


def kernel(**inputs):
    import numpy as _np
    import concourse.bacc as _bacc
    from concourse import mybir as _mybir
    from concourse.bass_utils import run_bass_kernel_spmd as _run

    nc = _bacc.Bacc("TRN2", target_bir_lowering=False, num_devices=1)
    arrays, args = {}, []
    for name in _INS:
        a = _np.ascontiguousarray(inputs[name])
        arrays[f"in_{name}_dram"] = a
        args.append(nc.dram_tensor(f"in_{name}_dram", a.shape, _mybir.dt.from_np(a.dtype), kind="ExternalInput").ap())
    table = rope_table()
    arrays["rope_dram"] = table
    args.append(nc.dram_tensor("rope_dram", table.shape, _mybir.dt.float32, kind="ExternalInput").ap())
    args.append(nc.dram_tensor("out_0_dram", (B, T, D), _mybir.dt.float32, kind="ExternalOutput").ap())
    program(nc, *args)
    r = _run(nc, [arrays], core_ids=[0])
    return r.results[0]["out_0_dram"]
```
